# Optimizing a Trainium2 kernel written in Bass

```python
import numpy as np
import jax
import jax.numpy as jnp

def _softmax(x, axis=-1):
    return jax.nn.softmax(x, axis=axis)

def _gelu(x):
    return jax.nn.gelu(x, approximate=True)

def _silu(x):
    return jax.nn.silu(x)

def _sigmoid(x):
    return jax.nn.sigmoid(x)

def _layernorm(x, axis=-1, eps=1e-05):
    m = jnp.mean(x, axis=axis, keepdims=True)
    v = jnp.var(x, axis=axis, keepdims=True)
    return (x - m) / jnp.sqrt(v + eps)

def _scatter_add(tgt, idx, src, axis=0):
    return tgt.at[idx].add(src)

def _segment_sum(src, seg, n):
    return jax.ops.segment_sum(src, seg, n)
kernel_name = 'mk_hybrid_d2_jaxref_r8_aa72f0'

def setup_inputs(seed: int=0):
    np.random.seed(seed)
    _w = jnp.asarray

    def _L0_attn_a_setup():
        import jax, jax.numpy as jnp
        import numpy as np

        def _ln(x, g, b):
            m = x.mean(-1, keepdims=True)
            v = x.var(-1, keepdims=True)
            return (x - m) * jax.lax.rsqrt(v + 1e-05) * g + b

        def _shift(x):
            return jnp.pad(x, ((0, 0), (1, 0), (0, 0)))[:, :-1]
        key = jax.random.key(seed)
        ks = jax.random.split(key, 20)
        B, S, D, E, F = (2, 256, 128, 8, 256)
        s = 0.02
        return dict(x=jax.random.normal(ks[0], (B, S, D), jnp.float32), ln1_g=jnp.ones((D,), jnp.float32), ln1_b=jnp.zeros((D,), jnp.float32), ln2_g=jnp.ones((D,), jnp.float32), ln2_b=jnp.zeros((D,), jnp.float32), tm_mu_k=jax.random.uniform(ks[1], (D,), jnp.float32), tm_mu_v=jax.random.uniform(ks[2], (D,), jnp.float32), tm_mu_r=jax.random.uniform(ks[3], (D,), jnp.float32), time_decay=jax.random.normal(ks[4], (D,), jnp.float32) * 0.1, time_first=jax.random.normal(ks[5], (D,), jnp.float32) * 0.1, Wk=jax.random.normal(ks[6], (D, D), jnp.float32) * s, Wv=jax.random.normal(ks[7], (D, D), jnp.float32) * s, Wr=jax.random.normal(ks[8], (D, D), jnp.float32) * s, Wo=jax.random.normal(ks[9], (D, D), jnp.float32) * s, router_w=jax.random.normal(ks[10], (D, E), jnp.float32) * s, cm_mu_k=jax.random.uniform(ks[11], (E, D), jnp.float32), cm_mu_r=jax.random.uniform(ks[12], (E, D), jnp.float32), eWk=jax.random.normal(ks[13], (E, D, F), jnp.float32) * s, eWv=jax.random.normal(ks[14], (E, F, D), jnp.float32) * s, eWr=jax.random.normal(ks[15], (E, D, D), jnp.float32) * s)
    _L0_attn_a_in = _L0_attn_a_setup()

    def _L0_attn_b_setup():
        import jax, jax.numpy as jnp
        import numpy as np
        import math
        EPS = 1e-06

        def favorplus_features(x, proj):
            xw = jnp.einsum('bhtd,hmd->bhtm', x, proj)
            xw = xw - jnp.max(xw, axis=-1, keepdims=True)
            x_norm_sq = jnp.sum(x * x, axis=-1, keepdims=True)
            return jnp.exp(xw) * jnp.exp(-0.5 * x_norm_sq) + EPS
        key = jax.random.key(seed)
        ks = jax.random.split(key, 6)
        B, T, d = (2, 512, 128)
        h, m = (16, 32)
        dk = d // h
        s = 1.0 / math.sqrt(d)
        return {'x': jax.random.normal(ks[0], (B, T, d), dtype=jnp.float32), 'Wq': jax.random.normal(ks[1], (d, d), dtype=jnp.float32) * s, 'Wk': jax.random.normal(ks[2], (d, d), dtype=jnp.float32) * s, 'Wv': jax.random.normal(ks[3], (d, d), dtype=jnp.float32) * s, 'Wo': jax.random.normal(ks[4], (d, d), dtype=jnp.float32) * s, 'bo': jnp.zeros((d,), dtype=jnp.float32), 'proj': jax.random.normal(ks[5], (h, m, dk), dtype=jnp.float32)}
    _L0_attn_b_in = _L0_attn_b_setup()

    def _L0_ffn_setup():
        import jax, jax.numpy as jnp
        import numpy as np
        B, S, D = (4, 256, 128)
        P = 9
        DM = D // 4
        EPS = 1e-05

        def _mix(x, mix_kernel):
            xp = jnp.pad(x, ((0, 0), (1, 1), (0, 0)))
            return mix_kernel[0] * xp[:, :-2] + mix_kernel[1] * xp[:, 1:-1] + mix_kernel[2] * xp[:, 2:]

        def _layernorm(h, gamma, beta):
            mu = jnp.mean(h, axis=-1, keepdims=True)
            var = jnp.var(h, axis=-1, keepdims=True)
            return (h - mu) * jax.lax.rsqrt(var + EPS) * gamma + beta
        key = jax.random.key(seed)
        ks = jax.random.split(key, 12)
        sc_in = 1.0 / np.sqrt(D)
        sc_mid = 1.0 / np.sqrt(DM)
        return {'x': jax.random.normal(ks[0], (B, S, D), dtype=jnp.float32), 'mix_kernel': jax.random.normal(ks[1], (3, D), dtype=jnp.float32) * 0.5, 'W1': jax.random.normal(ks[2], (P, D, DM), dtype=jnp.float32) * sc_in, 'b1': jnp.zeros((P, DM), dtype=jnp.float32), 'W2': jax.random.normal(ks[3], (P, DM, D), dtype=jnp.float32) * sc_mid, 'b2': jnp.zeros((P, D), dtype=jnp.float32), 'Wo1': jax.random.normal(ks[4], (D, DM), dtype=jnp.float32) * sc_in, 'bo1': jnp.zeros((DM,), dtype=jnp.float32), 'Wo2': jax.random.normal(ks[5], (DM, P), dtype=jnp.float32) * sc_mid, 'bo2': jnp.zeros((P,), dtype=jnp.float32), 'gamma': jnp.ones((D,), dtype=jnp.float32), 'beta': jnp.zeros((D,), dtype=jnp.float32)}
    _L0_ffn_in = _L0_ffn_setup()

    def _L1_attn_a_setup():
        import jax, jax.numpy as jnp
        import numpy as np
        import math
        DIM = 128
        H = 16
        DK = DIM // H
        SEG = 64
        NN = 2
        DIL = 4
        B, L = (2, 1024)

        def _attn(q, k, v):
            scores = jnp.einsum('bshqd,bshkd->bshqk', q, k) / math.sqrt(q.shape[-1])
            a = jax.nn.softmax(scores, axis=-1)
            return jnp.einsum('bshqk,bshkd->bshqd', a, v)
        key = jax.random.key(seed)
        ks = jax.random.split(key, 9)
        scale = 1.0 / math.sqrt(DIM)

        def lin(k):
            return jax.random.normal(k, (DIM, DIM), jnp.float32) * scale
        return {'x': jax.random.normal(ks[0], (B, L, DIM), jnp.float32), 'Wq': lin(ks[1]), 'bq': jnp.zeros((DIM,), jnp.float32), 'Wk': lin(ks[2]), 'bk': jnp.zeros((DIM,), jnp.float32), 'Wv': lin(ks[3]), 'bv': jnp.zeros((DIM,), jnp.float32), 'Wo': lin(ks[4]), 'bo': jnp.zeros((DIM,), jnp.float32)}
    _L1_attn_a_in = _L1_attn_a_setup()

    def _L1_attn_b_setup():
        import jax, jax.numpy as jnp
        import numpy as np
        B, L, H, U = (4, 512, 128, 128)
        key = jax.random.key(seed)
        k0, k1, k2, k3 = jax.random.split(key, 4)
        inputs = jax.random.normal(k0, (B, L, H), dtype=jnp.float32)
        W_rkv = jax.random.normal(k1, (H, 3 * U), dtype=jnp.float32) / np.sqrt(H)
        b_rkv = jnp.zeros((3 * U,), dtype=jnp.float32)
        W_o = jax.random.normal(k2, (U, H), dtype=jnp.float32) / np.sqrt(U)
        b_o = jnp.zeros((H,), dtype=jnp.float32)
        r_min, r_max = (0.9, 0.999)
        u = jax.random.uniform(k3, (U,), dtype=jnp.float32)
        nu_log = jnp.log(-0.5 * jnp.log(u * (r_max ** 2 - r_min ** 2) + r_min ** 2))
        gamma_log = jnp.zeros((U,), dtype=jnp.float32)
        return {'inputs': inputs, 'W_rkv': W_rkv, 'b_rkv': b_rkv, 'W_o': W_o, 'b_o': b_o, 'nu_log': nu_log, 'gamma_log': gamma_log}
    _L1_attn_b_in = _L1_attn_b_setup()

    def _L1_ffn_setup():
        import jax, jax.numpy as jnp
        import numpy as np
        D_MODEL = 128
        DEPTH = 8
        M = 2 ** DEPTH
        N_INTERNAL = M - 1
        B, T = (8, 512)

        def _leaf_probs(gate):
            BT = gate.shape[0]
            lp = jnp.ones((BT, M), dtype=gate.dtype)
            for level in range(DEPTH):
                n = 2 ** level
                half = M // (2 * n)
                g = gate[:, n - 1:2 * n - 1]
                f = jnp.stack([1.0 - g, g], axis=-1)
                f = jnp.broadcast_to(f[..., None], (BT, n, 2, half))
                lp = lp * f.reshape(BT, M)
            return lp
        key = jax.random.key(seed)
        ks = jax.random.split(key, 7)
        x = jax.random.normal(ks[0], (B, T, D_MODEL), dtype=jnp.float32)
        Wq = jax.random.normal(ks[1], (D_MODEL, D_MODEL), dtype=jnp.float32) * 0.02
        routers = jax.random.normal(ks[2], (N_INTERNAL, D_MODEL), dtype=jnp.float32) * 0.02
        leaf_keys = jax.random.normal(ks[3], (M, D_MODEL), dtype=jnp.float32) * 0.02
        leaf_values = jax.random.normal(ks[4], (M, D_MODEL), dtype=jnp.float32) * 0.02
        Wout_w = jax.random.normal(ks[5], (D_MODEL, D_MODEL), dtype=jnp.float32) * 0.02
        Wout_b = jax.random.normal(ks[6], (D_MODEL,), dtype=jnp.float32) * 0.02
        return {'x': x, 'Wq': Wq, 'routers': routers, 'leaf_keys': leaf_keys, 'leaf_values': leaf_values, 'Wout_w': Wout_w, 'Wout_b': Wout_b}
    _L1_ffn_in = _L1_ffn_setup()
    _d = {'L0_attn_a_x': _L0_attn_a_in['x'], 'L0_attn_a_ln1_g': _L0_attn_a_in['ln1_g'], 'L0_attn_a_ln1_b': _L0_attn_a_in['ln1_b'], 'L0_attn_a_ln2_g': _L0_attn_a_in['ln2_g'], 'L0_attn_a_ln2_b': _L0_attn_a_in['ln2_b'], 'L0_attn_a_tm_mu_k': _L0_attn_a_in['tm_mu_k'], 'L0_attn_a_tm_mu_v': _L0_attn_a_in['tm_mu_v'], 'L0_attn_a_tm_mu_r': _L0_attn_a_in['tm_mu_r'], 'L0_attn_a_time_decay': _L0_attn_a_in['time_decay'], 'L0_attn_a_time_first': _L0_attn_a_in['time_first'], 'L0_attn_a_Wk': _L0_attn_a_in['Wk'], 'L0_attn_a_Wv': _L0_attn_a_in['Wv'], 'L0_attn_a_Wr': _L0_attn_a_in['Wr'], 'L0_attn_a_Wo': _L0_attn_a_in['Wo'], 'L0_attn_a_router_w': _L0_attn_a_in['router_w'], 'L0_attn_a_cm_mu_k': _L0_attn_a_in['cm_mu_k'], 'L0_attn_a_cm_mu_r': _L0_attn_a_in['cm_mu_r'], 'L0_attn_a_eWk': _L0_attn_a_in['eWk'], 'L0_attn_a_eWv': _L0_attn_a_in['eWv'], 'L0_attn_a_eWr': _L0_attn_a_in['eWr'], 'L0_attn_b_Wq': _L0_attn_b_in['Wq'], 'L0_attn_b_Wk': _L0_attn_b_in['Wk'], 'L0_attn_b_Wv': _L0_attn_b_in['Wv'], 'L0_attn_b_Wo': _L0_attn_b_in['Wo'], 'L0_attn_b_bo': _L0_attn_b_in['bo'], 'L0_attn_b_proj': _L0_attn_b_in['proj'], 'L0_ffn_mix_kernel': _L0_ffn_in['mix_kernel'], 'L0_ffn_W1': _L0_ffn_in['W1'], 'L0_ffn_b1': _L0_ffn_in['b1'], 'L0_ffn_W2': _L0_ffn_in['W2'], 'L0_ffn_b2': _L0_ffn_in['b2'], 'L0_ffn_Wo1': _L0_ffn_in['Wo1'], 'L0_ffn_bo1': _L0_ffn_in['bo1'], 'L0_ffn_Wo2': _L0_ffn_in['Wo2'], 'L0_ffn_bo2': _L0_ffn_in['bo2'], 'L0_ffn_gamma': _L0_ffn_in['gamma'], 'L0_ffn_beta': _L0_ffn_in['beta'], 'L1_attn_a_Wq': _L1_attn_a_in['Wq'], 'L1_attn_a_bq': _L1_attn_a_in['bq'], 'L1_attn_a_Wk': _L1_attn_a_in['Wk'], 'L1_attn_a_bk': _L1_attn_a_in['bk'], 'L1_attn_a_Wv': _L1_attn_a_in['Wv'], 'L1_attn_a_bv': _L1_attn_a_in['bv'], 'L1_attn_a_Wo': _L1_attn_a_in['Wo'], 'L1_attn_a_bo': _L1_attn_a_in['bo'], 'L1_attn_b_W_rkv': _L1_attn_b_in['W_rkv'], 'L1_attn_b_b_rkv': _L1_attn_b_in['b_rkv'], 'L1_attn_b_W_o': _L1_attn_b_in['W_o'], 'L1_attn_b_b_o': _L1_attn_b_in['b_o'], 'L1_attn_b_nu_log': _L1_attn_b_in['nu_log'], 'L1_attn_b_gamma_log': _L1_attn_b_in['gamma_log'], 'L1_ffn_Wq': _L1_ffn_in['Wq'], 'L1_ffn_routers': _L1_ffn_in['routers'], 'L1_ffn_leaf_keys': _L1_ffn_in['leaf_keys'], 'L1_ffn_leaf_values': _L1_ffn_in['leaf_values'], 'L1_ffn_Wout_w': _L1_ffn_in['Wout_w'], 'L1_ffn_Wout_b': _L1_ffn_in['Wout_b']}
    _x0 = _d['L0_attn_a_x']
    _d['L0_attn_a_x'] = jax.random.normal(jax.random.fold_in(jax.random.key(seed), 1), (4, 1024, 128), dtype=_x0.dtype)
    del _x0
    return _d

def reference(L0_attn_a_x, L0_attn_a_ln1_g, L0_attn_a_ln1_b, L0_attn_a_ln2_g, L0_attn_a_ln2_b, L0_attn_a_tm_mu_k, L0_attn_a_tm_mu_v, L0_attn_a_tm_mu_r, L0_attn_a_time_decay, L0_attn_a_time_first, L0_attn_a_Wk, L0_attn_a_Wv, L0_attn_a_Wr, L0_attn_a_Wo, L0_attn_a_router_w, L0_attn_a_cm_mu_k, L0_attn_a_cm_mu_r, L0_attn_a_eWk, L0_attn_a_eWv, L0_attn_a_eWr, L0_attn_b_Wq, L0_attn_b_Wk, L0_attn_b_Wv, L0_attn_b_Wo, L0_attn_b_bo, L0_attn_b_proj, L0_ffn_mix_kernel, L0_ffn_W1, L0_ffn_b1, L0_ffn_W2, L0_ffn_b2, L0_ffn_Wo1, L0_ffn_bo1, L0_ffn_Wo2, L0_ffn_bo2, L0_ffn_gamma, L0_ffn_beta, L1_attn_a_Wq, L1_attn_a_bq, L1_attn_a_Wk, L1_attn_a_bk, L1_attn_a_Wv, L1_attn_a_bv, L1_attn_a_Wo, L1_attn_a_bo, L1_attn_b_W_rkv, L1_attn_b_b_rkv, L1_attn_b_W_o, L1_attn_b_b_o, L1_attn_b_nu_log, L1_attn_b_gamma_log, L1_ffn_Wq, L1_ffn_routers, L1_ffn_leaf_keys, L1_ffn_leaf_values, L1_ffn_Wout_w, L1_ffn_Wout_b):

    def _L0_attn_a_ref(x, ln1_g, ln1_b, ln2_g, ln2_b, tm_mu_k, tm_mu_v, tm_mu_r, time_decay, time_first, Wk, Wv, Wr, Wo, router_w, cm_mu_k, cm_mu_r, eWk, eWv, eWr):
        import jax, jax.numpy as jnp
        import numpy as np

        def _ln(x, g, b):
            m = x.mean(-1, keepdims=True)
            v = x.var(-1, keepdims=True)
            return (x - m) * jax.lax.rsqrt(v + 1e-05) * g + b

        def _shift(x):
            return jnp.pad(x, ((0, 0), (1, 0), (0, 0)))[:, :-1]
        TOP_K = 2
        E = router_w.shape[1]
        B, S, D = x.shape
        xn = _ln(x, ln1_g, ln1_b)
        xx = _shift(xn)
        xk = xn * tm_mu_k + xx * (1.0 - tm_mu_k)
        xv = xn * tm_mu_v + xx * (1.0 - tm_mu_v)
        xr = xn * tm_mu_r + xx * (1.0 - tm_mu_r)
        k = xk @ Wk
        v = xv @ Wv
        r = jax.nn.sigmoid(xr @ Wr)
        w = -jnp.exp(time_decay)
        u = time_first

        def step(carry, kv_t):
            aa, bb, pp = carry
            kt, vt = kv_t
            qq = jnp.maximum(pp, u + kt)
            e1 = jnp.exp(pp - qq)
            e2 = jnp.exp(u + kt - qq)
            wkv_t = (e1 * aa + e2 * vt) / (e1 * bb + e2)
            qq2 = jnp.maximum(pp + w, kt)
            e1b = jnp.exp(pp + w - qq2)
            e2b = jnp.exp(kt - qq2)
            return ((e1b * aa + e2b * vt, e1b * bb + e2b, qq2), wkv_t)
        init = (jnp.zeros((B, D), x.dtype), jnp.zeros((B, D), x.dtype), jnp.full((B, D), -1e+30, x.dtype))
        _, wkv = jax.lax.scan(step, init, (k.transpose(1, 0, 2), v.transpose(1, 0, 2)))
        wkv = wkv.transpose(1, 0, 2)
        x = x + r * wkv @ Wo
        ei = _ln(x, ln2_g, ln2_b)
        probs = jax.nn.softmax(ei @ router_w, axis=-1)
        vals, idx = jax.lax.top_k(probs, TOP_K)
        wts = vals / vals.sum(-1, keepdims=True)
        tw = jnp.sum(jax.nn.one_hot(idx, E, dtype=x.dtype) * wts[..., None], axis=-2)
        exx = _shift(ei)
        mk = cm_mu_k[:, None, None, :]
        mr = cm_mu_r[:, None, None, :]
        xk_e = ei[None] * mk + exx[None] * (1.0 - mk)
        xr_e = ei[None] * mr + exx[None] * (1.0 - mr)
        k_e = jnp.square(jax.nn.relu(jnp.einsum('ebsd,edf->ebsf', xk_e, eWk)))
        kv_e = jnp.einsum('ebsf,efd->ebsd', k_e, eWv)
        r_e = jax.nn.sigmoid(jnp.einsum('ebsd,edg->ebsg', xr_e, eWr))
        expert_out = r_e * kv_e
        moe = jnp.einsum('ebsd,bse->bsd', expert_out, tw)
        return x + moe

    def _L0_attn_b_ref(x, Wq, Wk, Wv, Wo, bo, proj):
        import jax, jax.numpy as jnp
        import numpy as np
        import math
        EPS = 1e-06

        def favorplus_features(x, proj):
            xw = jnp.einsum('bhtd,hmd->bhtm', x, proj)
            xw = xw - jnp.max(xw, axis=-1, keepdims=True)
            x_norm_sq = jnp.sum(x * x, axis=-1, keepdims=True)
            return jnp.exp(xw) * jnp.exp(-0.5 * x_norm_sq) + EPS
        B, T, d = x.shape
        h, m, dk = proj.shape

        def heads(W):
            y = jnp.einsum('btd,ed->bte', x, W)
            return y.reshape(B, T, h, dk).transpose(0, 2, 1, 3)
        Q = heads(Wq) / math.sqrt(dk)
        K = heads(Wk) / math.sqrt(dk)
        V = heads(Wv)
        inv_sqrt_m = 1.0 / math.sqrt(m)
        phiQ = favorplus_features(Q, proj) * inv_sqrt_m
        phiK = favorplus_features(K, proj) * inv_sqrt_m
        KV = jnp.einsum('bhtm,bhtd->bhmd', phiK, V)
        Ksum = jnp.sum(phiK, axis=2)
        num = jnp.einsum('bhtm,bhmd->bhtd', phiQ, KV)
        den = jnp.einsum('bhtm,bhm->bht', phiQ, Ksum)[..., None] + EPS
        out_heads = num / den
        merged = out_heads.transpose(0, 2, 1, 3).reshape(B, T, d)
        return jnp.einsum('btd,ed->bte', merged, Wo) + bo

    def _L0_ffn_ref(x, mix_kernel, W1, b1, W2, b2, Wo1, bo1, Wo2, bo2, gamma, beta):
        import jax, jax.numpy as jnp
        import numpy as np
        B, S, D = (4, 256, 128)
        P = 9
        DM = D // 4
        EPS = 1e-05

        def _mix(x, mix_kernel):
            xp = jnp.pad(x, ((0, 0), (1, 1), (0, 0)))
            return mix_kernel[0] * xp[:, :-2] + mix_kernel[1] * xp[:, 1:-1] + mix_kernel[2] * xp[:, 2:]

        def _layernorm(h, gamma, beta):
            mu = jnp.mean(h, axis=-1, keepdims=True)
            var = jnp.var(h, axis=-1, keepdims=True)
            return (h - mu) * jax.lax.rsqrt(var + EPS) * gamma + beta
        x_mixed = _mix(x, mix_kernel)
        h = jnp.einsum('bsd,pdm->bspm', x_mixed, W1) + b1
        stacked_paths = jnp.einsum('bspm,pmd->bspd', h, W2) + b2
        scores = jnp.tanh(x_mixed @ Wo1 + bo1) @ Wo2 + bo2
        idx = jnp.argmax(scores, axis=-1)
        weights = jax.nn.one_hot(idx, P, dtype=stacked_paths.dtype)
        collapsed = jnp.einsum('bspd,bsp->bsd', stacked_paths, weights)
        return _layernorm(x + collapsed, gamma, beta)

    def _L1_attn_a_ref(x, Wq, bq, Wk, bk, Wv, bv, Wo, bo):
        import jax, jax.numpy as jnp
        import numpy as np
        import math
        DIM = 128
        H = 16
        DK = DIM // H
        SEG = 64
        NN = 2
        DIL = 4
        B, L = (2, 1024)

        def _attn(q, k, v):
            scores = jnp.einsum('bshqd,bshkd->bshqk', q, k) / math.sqrt(q.shape[-1])
            a = jax.nn.softmax(scores, axis=-1)
            return jnp.einsum('bshqk,bshkd->bshqd', a, v)
        Bx, Lx, C = x.shape
        pad = -Lx % SEG

        def proj_chunk(W, b):
            t = x @ W + b
            t = jnp.pad(t, ((0, 0), (0, pad), (0, 0)))
            S = t.shape[1] // SEG
            t = t.reshape(Bx, S, SEG, H, DK)
            return t.transpose(0, 1, 3, 2, 4)
        q = proj_chunk(Wq, bq)
        k = proj_chunk(Wk, bk)
        v = proj_chunk(Wv, bv)
        S = q.shape[1]
        out = _attn(q, k, v)
        dil_idx = jnp.arange(0, SEG, DIL)
        kd = k[:, :, :, dil_idx, :]
        vd = v[:, :, :, dil_idx, :]
        seg_ids = jnp.arange(S)
        w = 1.0 / (2 * NN)
        for off in range(1, NN + 1):
            for sign in (-1, 1):
                n = seg_ids + sign * off
                valid = (n >= 0) & (n < S)
                nc = jnp.clip(n, 0, S - 1)
                cross = _attn(q, kd[:, nc], vd[:, nc])
                out = out + jnp.where(valid[None, :, None, None, None], cross * w, 0.0)
        out = out.transpose(0, 1, 3, 2, 4).reshape(Bx, S * SEG, C)
        out = out[:, :Lx, :]
        return out @ Wo + bo

    def _L1_attn_b_ref(inputs, W_rkv, b_rkv, W_o, b_o, nu_log, gamma_log):
        import jax, jax.numpy as jnp
        import numpy as np
        B, L, H, U = (4, 512, 128, 128)
        rkv = jnp.einsum('blh,hu->blu', inputs, W_rkv) + b_rkv
        r, k, v = jnp.split(rkv, 3, axis=-1)
        r = jax.nn.sigmoid(r)
        k = jnp.exp(k)
        kv = k * v
        u = jnp.concatenate([kv, k], axis=-1)
        nu = jnp.exp(jnp.concatenate([nu_log, nu_log]))
        gamma = jnp.exp(nu_log + gamma_log) - 1.0
        lam = jnp.exp(-nu)
        a = jnp.broadcast_to(lam, u.shape)

        def combine(c1, c2):
            a1, x1 = c1
            a2, x2 = c2
            return (a1 * a2, x1 * a2 + x2)
        _, y = jax.lax.associative_scan(combine, (a, u), axis=1)
        u1, u2 = jnp.split(y, 2, axis=-1)
        x = (u1 + gamma * kv) / (u2 + gamma * k + 1e-06) * r
        return jnp.einsum('blu,uh->blh', x, W_o) + b_o

    def _L1_ffn_ref(x, Wq, routers, leaf_keys, leaf_values, Wout_w, Wout_b):
        import jax, jax.numpy as jnp
        import numpy as np
        D_MODEL = 128
        DEPTH = 8
        M = 2 ** DEPTH
        N_INTERNAL = M - 1
        B, T = (8, 512)

        def _leaf_probs(gate):
            BT = gate.shape[0]
            lp = jnp.ones((BT, M), dtype=gate.dtype)
            for level in range(DEPTH):
                n = 2 ** level
                half = M // (2 * n)
                g = gate[:, n - 1:2 * n - 1]
                f = jnp.stack([1.0 - g, g], axis=-1)
                f = jnp.broadcast_to(f[..., None], (BT, n, 2, half))
                lp = lp * f.reshape(BT, M)
            return lp
        Bv, Tv, d = x.shape
        q = jnp.einsum('btd,ed->bte', x, Wq)
        q_flat = q.reshape(Bv * Tv, d)
        gate = jax.nn.sigmoid(q_flat @ routers.T)
        leaf_prob = _leaf_probs(gate)
        ret = (leaf_prob @ leaf_values).reshape(Bv, Tv, d)
        return jnp.einsum('btd,ed->bte', ret, Wout_w) + Wout_b
    x = L0_attn_a_x
    x = x + _L0_attn_a_ref(_layernorm(x, axis=-1), L0_attn_a_ln1_g, L0_attn_a_ln1_b, L0_attn_a_ln2_g, L0_attn_a_ln2_b, L0_attn_a_tm_mu_k, L0_attn_a_tm_mu_v, L0_attn_a_tm_mu_r, L0_attn_a_time_decay, L0_attn_a_time_first, L0_attn_a_Wk, L0_attn_a_Wv, L0_attn_a_Wr, L0_attn_a_Wo, L0_attn_a_router_w, L0_attn_a_cm_mu_k, L0_attn_a_cm_mu_r, L0_attn_a_eWk, L0_attn_a_eWv, L0_attn_a_eWr)
    x = x + _L0_ffn_ref(_layernorm(x, axis=-1), L0_ffn_mix_kernel, L0_ffn_W1, L0_ffn_b1, L0_ffn_W2, L0_ffn_b2, L0_ffn_Wo1, L0_ffn_bo1, L0_ffn_Wo2, L0_ffn_bo2, L0_ffn_gamma, L0_ffn_beta)
    x = x + _L0_attn_b_ref(_layernorm(x, axis=-1), L0_attn_b_Wq, L0_attn_b_Wk, L0_attn_b_Wv, L0_attn_b_Wo, L0_attn_b_bo, L0_attn_b_proj)
    x = x + _L0_ffn_ref(_layernorm(x, axis=-1), L0_ffn_mix_kernel, L0_ffn_W1, L0_ffn_b1, L0_ffn_W2, L0_ffn_b2, L0_ffn_Wo1, L0_ffn_bo1, L0_ffn_Wo2, L0_ffn_bo2, L0_ffn_gamma, L0_ffn_beta)
    x = x + _L1_attn_a_ref(_layernorm(x, axis=-1), L1_attn_a_Wq, L1_attn_a_bq, L1_attn_a_Wk, L1_attn_a_bk, L1_attn_a_Wv, L1_attn_a_bv, L1_attn_a_Wo, L1_attn_a_bo)
    x = x + _L1_ffn_ref(_layernorm(x, axis=-1), L1_ffn_Wq, L1_ffn_routers, L1_ffn_leaf_keys, L1_ffn_leaf_values, L1_ffn_Wout_w, L1_ffn_Wout_b)
    x = x + _L1_attn_b_ref(_layernorm(x, axis=-1), L1_attn_b_W_rkv, L1_attn_b_b_rkv, L1_attn_b_W_o, L1_attn_b_b_o, L1_attn_b_nu_log, L1_attn_b_gamma_log)
    x = x + _L1_ffn_ref(_layernorm(x, axis=-1), L1_ffn_Wq, L1_ffn_routers, L1_ffn_leaf_keys, L1_ffn_leaf_values, L1_ffn_Wout_w, L1_ffn_Wout_b)
    return x

_drawn_inputs = setup_inputs


def setup_inputs(seed=0):
    import zlib

    import numpy as np

    out = dict(_drawn_inputs(seed))
    spreads = {'L0_attn_a_ln1_g': (1.0, 0.6),
     'L0_attn_a_ln1_b': (0.0, 0.617),
     'L0_attn_a_ln2_g': (1.0, 0.6),
     'L0_attn_a_ln2_b': (0.0, 0.539),
     'L0_attn_b_bo': (0.0, 0.311),
     'L0_ffn_b1': (0.0, 0.346),
     'L0_ffn_b2': (0.0, 0.31),
     'L0_ffn_bo1': (0.0, 0.1),
     'L0_ffn_bo2': (0.0, 0.1),
     'L0_ffn_gamma': (1.0, 0.2),
     'L0_ffn_beta': (0.0, 0.1),
     'L1_attn_a_bq': (0.0, 2.0),
     'L1_attn_a_bk': (0.0, 2.0),
     'L1_attn_a_bv': (0.0, 0.311),
     'L1_attn_a_bo': (0.0, 0.284),
     'L1_attn_b_b_rkv': (0.0, 0.578),
     'L1_attn_b_b_o': (0.0, 0.3),
     'L1_attn_b_gamma_log': (0.0, 2.0)}
    factors = {'L0_attn_a_tm_mu_k': 7.45,
     'L0_attn_a_tm_mu_v': 4.116,
     'L0_attn_a_tm_mu_r': 6.772,
     'L0_attn_a_time_decay': 8.0,
     'L0_attn_a_time_first': 7.953,
     'L0_attn_a_Wk': 6.396,
     'L0_attn_a_Wr': 7.577,
     'L0_attn_a_router_w': 3.176,
     'L0_attn_a_cm_mu_k': 3.585,
     'L0_attn_a_cm_mu_r': 8.0,
     'L0_attn_a_eWk': 3.441,
     'L0_attn_a_eWv': 2.837,
     'L0_attn_a_eWr': 7.911,
     'L0_attn_b_Wq': 2.871,
     'L0_attn_b_proj': 9.412,
     'L1_attn_b_nu_log': 34.944,
     'L1_ffn_Wq': 8.0,
     'L1_ffn_routers': 8.0,
     'L1_ffn_leaf_values': 8.0,
     'L1_ffn_Wout_w': 8.0,
     'L1_ffn_Wout_b': 5.06}
    for name, (base, spread) in spreads.items():
        noise = np.random.default_rng([zlib.crc32(name.encode()), seed]).standard_normal(out[name].shape)
        drawn = base * np.exp(spread * noise) if base else spread * noise
        out[name] = jnp.asarray(drawn.astype(out[name].dtype))
    for name, factor in factors.items():
        out[name] = (out[name] * factor).astype(out[name].dtype)
    return out
```

```python
from contextlib import ExitStack

import concourse.bass as bass
from concourse import mybir

STAGES = "ABCDEFGH"
ALU = mybir.AluOpType
ACT = mybir.ActivationFunctionType
F32 = mybir.dt.float32
BF16 = mybir.dt.bfloat16
AX = mybir.AxisListType

P = 128
B, L = 4, 1024
NT = B * L
CH = 512
NCH = NT // CH
W = 4
PADL = L + 2
E = 8
NP = 9
DM = 32
EPS_LN = 1e-5

VROWS = ["ln1_g", "ln1_b", "ln2_g", "ln2_b", "mu_k", "mu_v", "mu_r", "decay", "first"] \
    + [f"cm_k{e}" for e in range(E)] + [f"cm_r{e}" for e in range(E)] \
    + ["favor_bo", "mix0", "mix1", "mix2", "gamma", "beta", "bq", "bk", "bv", "bo", "br", "bkk", "bvv", "lru_bo",
       "nu_log", "gamma_log", "wout_b", "b1_0", "b1_1", "b1_2", "bo1"]
VI = {n: i for i, n in enumerate(VROWS)}


def wait_apart(eng, k, semaphore, value):
    eng.wait_ge(semaphore, value)
    eng.sem_inc(k.passed, 1)


class Chip:
    pass


def begin_stage(nc, ctx, names):
    sems = [ctx.enter_context(nc.semaphore(name)) for name in names]
    with nc.Block() as block:
        @block.vector
        def _(dve):
            for name, semaphore in zip(names, sems):
                if name in PRIMED:
                    dve.sem_inc(semaphore, PRIMED[name])
    return sems


def end_stage(nc, sems):
    with nc.Block() as block:
        @block.vector
        def _(dve):
            for semaphore in sems:
                dve.sem_clear(semaphore)


def plain(buf, it, c):
    return buf[:, bass.ds(it * (W * CH) + c * CH, CH)]


def padded(buf, it, c, shift=0):
    return buf[:, bass.ds(it * (W // 2 * PADL) + (c // 2) * PADL + 1 + (c % 2) * CH + shift, CH)]


def layernorm(nc, k, call, src, dst, gain=None, bias=None, residual=None):
    n0 = call * NCH
    with nc.Block() as block:
        @block.tensor
        def _(pe):
            with pe.Fori(0, NCH // W) as it:
                g = it * W + n0
                for c in range(W):
                    pe.wait_ge(k.ln_out, g + (c + 1))
                    nc.tensor.matmul(k.bank[c][:], k.center[:], src(it, c), start=True, stop=True).then_inc(k.ln_centered, 1)
                for c in range(W):
                    pe.wait_ge(k.ln_squared, g + (c + 1))
                    nc.tensor.matmul(k.bank[4 + c][:], k.mean[:], k.ln_sq[:, c, :], start=True, stop=True).then_inc(k.ln_var, 1)

        @block.scalar
        def _(act):
            act.preload_act_table_set("natural_log_exp_and_others")
            with act.Fori(0, NCH // W) as it:
                g = it * W + n0
                for c in range(W):
                    act.wait_ge(k.ln_centered, g + (c + 1))
                    nc.scalar.activation(k.ln_sq[:, c, :], k.bank[c][:], ACT.Square).then_inc(k.ln_squared, 1)
                for c in range(W):
                    act.wait_ge(k.ln_var, g + (c + 1))
                    nc.scalar.activation(k.ln_std[:, c, :], k.bank[4 + c][:], ACT.Ln, bias=k.eps[:, 0:1]).then_inc(k.ln_logs, 1)
                for c in range(W):
                    act.wait_ge(k.ln_logs, g + (c + 1))
                    nc.scalar.activation(k.ln_std[:, c, :], k.ln_std[:, c, :], ACT.Exp, scale=-0.5).then_inc(k.ln_rstd, 1)

        @block.vector
        def _(dve):
            with dve.Fori(0, NCH // W) as it:
                g = it * W + n0
                for c in range(W):
                    dve.wait_ge(k.ln_rstd, g + (c + 1))
                    out = dst(it, c) if residual is None else k.ln_sq[:, c, :]
                    op = nc.vector.tensor_tensor(out, k.bank[c][:], k.ln_std[:, c, :], ALU.mult)
                    if gain is not None:
                        op.then_inc(k.ln_scaled, 1)
                        dve.wait_ge(k.ln_scaled, (it * W + k.ln_scaled_0) + (c + 1))
                        op = nc.vector.tensor_scalar(out, out, k.vec(gain), k.vec(bias), ALU.mult, ALU.add)
                    if residual is not None:
                        op.then_inc(k.ln_biased, 1)
                        dve.wait_ge(k.ln_biased, (it * W + k.ln_biased_0) + (c + 1))
                        op = nc.vector.tensor_tensor(residual(it, c), residual(it, c), out, ALU.add)
                    op.then_inc(k.ln_out, 1)
    if gain is not None:
        k.ln_scaled_0 += NCH
    if residual is not None:
        k.ln_biased_0 += NCH


def rwkv_mix(nc, k, a):
    Wk, Wv, Wr, Wo = (k.wA[:, j, :] for j in range(4))
    K, V, R = k.big[0], k.big[1], k.big[2]
    with nc.Block() as block:
        @block.sync
        def _(sp):
            for j, w in enumerate((a["L0_attn_a_Wk"], a["L0_attn_a_Wv"], a["L0_attn_a_Wr"], a["L0_attn_a_Wo"])):
                sp.dma_start(k.wA[:, j, :], w).then_inc(k.wA_in, 16)
            sp.dma_start(k.router[:], a["L0_attn_a_router_w"]).then_inc(k.moe_w_in, 16)
            sp.dma_start(k.eWk[:], a["L0_attn_a_eWk"].rearrange("e d f -> d e f")).then_inc(k.moe_w_in, 16)
            sp.dma_start(k.eWv[:], a["L0_attn_a_eWv"].rearrange("e (h f) d -> f e h d", h=2)).then_inc(k.moe_w_in, 16)
            sp.dma_start(k.eWr[:], a["L0_attn_a_eWr"].rearrange("e d g -> d e g")).then_inc(k.moe_w_in, 16)

        @block.vector
        def _(dve):
            with dve.Fori(0, NCH // 2) as it:
                for c in range(2):
                    g = it * 2 + c
                    now = k.N[:, bass.ds(it * PADL + 1 + c * CH, CH)]
                    before = k.N[:, bass.ds(it * PADL + c * CH, CH)]
                    dve.wait_ge(k.kvr, g * 3 + 3)
                    nc.vector.tensor_tensor(k.diff[:, c, :], now, before, ALU.subtract).then_inc(k.mix_diff, 1)
                    dve.wait_ge(k.mix_diff, g + 1)
                    for j, mu in enumerate(("mu_k", "mu_v", "mu_r")):
                        nc.vector.scalar_tensor_tensor(k.mixed[:, c, j, :], k.diff[:, c, :], k.vec(mu), before,
                                                       ALU.mult, ALU.add).then_inc(k.mix_in, 1)

        @block.tensor
        def _(pe):
            pe.wait_ge(k.wA_in, 64)
            with pe.Fori(0, NCH // 2) as it:
                for c in range(2):
                    g = it * 2 + c
                    for j, w in enumerate((Wk, Wv, Wr)):
                        pe.wait_ge(k.mix_in, g * 3 + (j + 1))
                        pe.wait_ge(k.kvr_out, g * 3 + (j + 1))
                        op = nc.tensor.matmul(k.bank[3 * c + j][:], w, k.mixed[:, c, j, :], start=True, stop=True)
                        op.then_inc(k.kvr, 1)

        @block.scalar
        def _(act):
            with act.Fori(0, NCH // 2) as it:
                for c in range(2):
                    at = bass.ds(it * L + c * CH, CH)
                    for j in range(3):
                        act.wait_ge(k.kvr, it * 6 + (c * 3 + j + 1 + PRIMED["kvr"]))
                        dst = (K, V, R)[j]
                        nc.scalar.activation(dst[:, at], k.bank[3 * c + j][:], (ACT.Copy, ACT.Copy, ACT.Tanh)[j],
                                             scale=(1.0, 1.0, 0.5)[j]).then_inc(k.kvr_out, 1)


def wkv(nc, k, a):
    K, V, R = k.big[0], k.big[1], k.big[2]
    T = k.big[3]
    U = k.big[4]
    pp, aa, bb = k.pp, k.aa, k.bb
    t = [T[:, j * L:(j + 1) * L] for j in range(4)]
    u = [U[:, j * L:(j + 1) * L] for j in range(4)]
    with nc.Block() as block:
        @block.scalar
        def _(act):
            nc.scalar.activation(k.wdec[:], k.vec("decay"), ACT.Exp).then_inc(k.wkv_w, 1)
            with act.Fori(0, B) as b:
                act.wait_ge(k.wkv_e2v, b + 1)
                nc.scalar.activation(k.vb, V[:, bass.ds(b * L, L)], ACT.Copy).then_inc(k.wkv_v, 1)
                for j in range(4):
                    act.wait_ge(k.wkv_arg, b * 4 + (j + 1))
                    nc.scalar.activation(t[j], t[j], ACT.Exp).then_inc(k.wkv_exp, 1)
                act.wait_ge(k.wkv_den, b + 1)
                nc.scalar.activation(u[3], u[2], ACT.Ln).then_inc(k.wkv_ln, 1)
                act.wait_ge(k.wkv_ln, b + 1)
                nc.scalar.activation(u[3], u[3], ACT.Exp, scale=-1.0).then_inc(k.wkv_rden, 1)

        @block.gpsimd
        def _(pool):
            nc.gpsimd.memset(pp[:, 0:1], -1e30).then_inc(k.wkv_init, 1)
            nc.gpsimd.memset(aa[:, 0:1], 0.0).then_inc(k.wkv_init, 1)
            nc.gpsimd.memset(bb[:, 0:1], 0.0).then_inc(k.wkv_init, 1)
            with pool.Fori(0, B) as b:
                pool.wait_ge(k.wkv_v, b + 1)
                pool.wait_ge(k.wkv_exp, b * 4 + 2)
                nc.gpsimd.tensor_tensor(u[0], t[1], k.vb, ALU.mult).then_inc(k.wkv_e2bv, 1)
                pool.wait_ge(k.wkv_exp, b * 4 + 4)
                nc.gpsimd.tensor_tensor(u[1], t[3], k.vb, ALU.mult).then_inc(k.wkv_e2v, 1)

        @block.vector
        def _(dve):
            dve.wait_ge(k.wkv_w, 1)
            nc.vector.tensor_scalar(k.wneg[:], k.wdec[:], -1.0, None, ALU.mult).then_inc(k.wkv_step, 1)
            dve.wait_ge(k.wkv_step, 1)
            nc.vector.tensor_copy(k.lam, k.wneg[:, 0:1].to_broadcast([P, L])).then_inc(k.wkv_step, 1)
            dve.wait_ge(k.wkv_step, 2)
            dve.wait_ge(k.wkv_init, 3)
            with dve.Fori(0, B) as b:
                at = bass.ds(b * L, L)
                s = b * 9 + 2
                nc.vector.tensor_tensor_scan(pp[:, 1:L + 1], k.lam, K[:, at], -1e30, ALU.add, ALU.max).then_inc(k.wkv_step, 1)
                dve.wait_ge(k.wkv_step, s + 1)
                nc.vector.scalar_tensor_tensor(t[0], pp[:, 0:L], k.wneg[:, 0:1], pp[:, 1:L + 1], ALU.add, ALU.subtract).then_inc(k.wkv_arg, 1)
                nc.vector.tensor_tensor(t[1], K[:, at], pp[:, 1:L + 1], ALU.subtract).then_inc(k.wkv_arg, 1)
                nc.vector.scalar_tensor_tensor(u[2], K[:, at], k.vec("first"), pp[:, 0:L], ALU.add, ALU.max).then_inc(k.wkv_step, 1)
                dve.wait_ge(k.wkv_step, s + 2)
                nc.vector.tensor_tensor(t[2], pp[:, 0:L], u[2], ALU.subtract).then_inc(k.wkv_arg, 1)
                nc.vector.scalar_tensor_tensor(t[3], K[:, at], k.vec("first"), u[2], ALU.add, ALU.subtract).then_inc(k.wkv_arg, 1)
                dve.wait_ge(k.wkv_exp, b * 4 + 2)
                nc.vector.tensor_tensor_scan(bb[:, 1:L + 1], t[0], t[1], 0.0, ALU.mult, ALU.add).then_inc(k.wkv_step, 1)
                dve.wait_ge(k.wkv_e2bv, b + 1)
                nc.vector.tensor_tensor_scan(aa[:, 1:L + 1], t[0], u[0], 0.0, ALU.mult, ALU.add).then_inc(k.wkv_step, 1)
                dve.wait_ge(k.wkv_step, s + 3)
                dve.wait_ge(k.wkv_exp, b * 4 + 4)
                nc.vector.tensor_tensor(u[2], t[2], bb[:, 0:L], ALU.mult).then_inc(k.wkv_step, 1)
                dve.wait_ge(k.wkv_step, s + 5)
                nc.vector.tensor_tensor(u[2], u[2], t[3], ALU.add).then_inc(k.wkv_den, 1)
                nc.vector.tensor_tensor(u[0], t[2], aa[:, 0:L], ALU.mult).then_inc(k.wkv_step, 1)
                dve.wait_ge(k.wkv_e2v, b + 2)
                dve.wait_ge(k.wkv_step, s + 6)
                nc.vector.tensor_tensor(u[1], u[0], u[1], ALU.add).then_inc(k.wkv_step, 1)
                dve.wait_ge(k.wkv_step, s + 7)
                nc.vector.scalar_tensor_tensor(u[1], R[:, at], 1.0, u[1], ALU.add, ALU.mult).then_inc(k.wkv_step, 1)
                dve.wait_ge(k.wkv_step, s + 8)
                dve.wait_ge(k.wkv_rden, b + 1)
                nc.vector.scalar_tensor_tensor(R[:, at], u[1], 0.5, u[3], ALU.mult, ALU.mult).then_inc(k.wkv_step, 1)
                dve.wait_ge(k.wkv_step, s + 9)


def project_add(nc, k, call, lhsT, src, dst, bias=None):
    n0 = call * NCH
    with nc.Block() as block:
        @block.tensor
        def _(pe):
            with pe.Fori(0, NCH // W) as it:
                for c in range(W):
                    pe.wait_ge(k.pa_added, it * W + (n0 + c + 1))
                    nc.tensor.matmul(k.bank[c][:], lhsT, src(it, c), start=True, stop=True).then_inc(k.pa_prod, 1)

        @block.vector
        def _(dve):
            with dve.Fori(0, NCH // W) as it:
                for c in range(W):
                    dve.wait_ge(k.pa_prod, it * W + (n0 + c + 1))
                    if bias is None:
                        nc.vector.tensor_tensor(dst(it, c), dst(it, c), k.bank[c][:], ALU.add).then_inc(k.pa_added, 1)
                    else:
                        nc.vector.scalar_tensor_tensor(dst(it, c), k.bank[c][:], bias, dst(it, c), ALU.add, ALU.add).then_inc(k.pa_added, 1)


def route(nc, k, a):
    NTI = NT // P
    lg, ex, wt = k.rt_logit, k.rt_exp, k.rt_w
    one, cand, two = k.rt_one, k.rt_cand, k.rt_two
    col = lambda t: t[:, :, None].to_broadcast([P, NTI, E])
    with nc.Block() as block:
        @block.tensor
        def _(pe):
            pe.wait_ge(k.moe_w_in, 64)
            with pe.Fori(0, NCH // W) as it:
                for c in range(W):
                    pe.wait_ge(k.rt_copied, it * W + (c + 1))
                    nc.tensor.matmul(k.bank[c][0:E, :], k.router[:], padded(k.N, it, c), start=True, stop=True).then_inc(k.rt_prod, 1)
            pe.wait_ge(k.rt_copied, NCH + PRIMED["rt_copied"])
            for t in range(NTI):
                op = nc.tensor.transpose(k.bank[4][:, t * E:(t + 1) * E], k.logitT[:, t * P:(t + 1) * P], k.ident[0:E, 0:E])
            op.then_inc(k.rt_turned, 1)
            pe.wait_ge(k.rt_parts, 3)
            for t in range(NTI):
                if t % 4 == 0 and t >= 16:
                    pe.wait_ge(k.rt_wT, t // 4 - 3)
                op = nc.tensor.transpose(k.bank[t // 4 % 4][0:3 * E, (t % 4) * P:(t % 4 + 1) * P],
                                         k.rt_part[:, t, :, :].rearrange("p e s -> p (e s)"), k.ident[:])
                if t % 4 == 3:
                    op.then_inc(k.rt_back, 1)

        @block.scalar
        def _(act):
            with act.Fori(0, NCH // W) as it:
                for c in range(W):
                    act.wait_ge(k.rt_prod, it * W + (c + 1))
                    nc.scalar.activation(k.logitT[:, bass.ds(it * W * CH + c * CH, CH)], k.bank[c][0:E, :], ACT.Copy).then_inc(k.rt_copied, 1)
            act.wait_ge(k.rt_step, 2)
            nc.scalar.activation(ex, ex, ACT.Exp).then_inc(k.rt_exps, 1)
            act.wait_ge(k.rt_sel, 4)
            for q in range(8):
                act.wait_ge(k.rt_back, q + 1)
                nc.scalar.activation(k.twT[0:3 * E, q * CH:(q + 1) * CH], k.bank[q % 4][0:3 * E, :], ACT.Copy).then_inc(k.rt_wT, 1)

        @block.gpsimd
        def _(pool):
            for e in range(E):
                nc.gpsimd.memset(k.rank[:, e:e + 1], float(E - e)).then_inc(k.rt_const, 1)
            nc.gpsimd.memset(k.twT, 0.0).then_inc(k.rt_sel, 1)
            nc.gpsimd.memset(k.sel[:], 1.0).then_inc(k.rt_sel, 1)
            pool.wait_ge(k.rt_sel, 2)
            nc.gpsimd.affine_select(out=k.sel[:], in_=k.sel[:], compare_op=ALU.is_ge, fill=0.0, base=0,
                                    pattern=[[-3, E], [0, P]], channel_multiplier=1).then_inc(k.rt_sel, 1)
            pool.wait_ge(k.rt_sel, 3)
            nc.gpsimd.affine_select(out=k.sel[:], in_=k.sel[:], compare_op=ALU.is_ge, fill=0.0, base=2,
                                    pattern=[[3, E], [0, P]], channel_multiplier=-1).then_inc(k.rt_sel, 1)

        @block.vector
        def _(dve):
            rank = k.rank[:, None, :].to_broadcast([P, NTI, E])
            step = [0]

            def then(op):
                step[0] += 1
                op.then_inc(k.rt_step, 1)
                dve.wait_ge(k.rt_step, step[0])

            dve.wait_ge(k.rt_const, E)
            dve.wait_ge(k.rt_turned, 1)
            logits = k.bank[4][:, 0:NTI * E].rearrange("p (t e) -> p t e", e=E)
            then(nc.vector.tensor_reduce(k.rt_m[:], logits, AX.X, ALU.max))
            then(nc.vector.tensor_tensor(ex, logits, col(k.rt_m[:]), ALU.subtract))
            dve.wait_ge(k.rt_exps, 1)
            then(nc.vector.tensor_reduce(k.rt_m[:], ex, AX.X, ALU.max))
            then(nc.vector.tensor_tensor(cand, ex, col(k.rt_m[:]), ALU.is_equal))
            then(nc.vector.tensor_tensor(cand, cand, rank, ALU.mult))
            then(nc.vector.tensor_reduce(k.rt_c[:], cand, AX.X, ALU.max))
            then(nc.vector.tensor_tensor(one, rank, col(k.rt_c[:]), ALU.is_equal))
            then(nc.vector.tensor_tensor(lg, ex, one, ALU.subtract))
            then(nc.vector.scalar_tensor_tensor(lg, one, -2.0, lg, ALU.mult, ALU.add))
            then(nc.vector.tensor_reduce(k.rt_m[:], lg, AX.X, ALU.max))
            then(nc.vector.tensor_tensor(cand, lg, col(k.rt_m[:]), ALU.is_equal))
            then(nc.vector.tensor_tensor(cand, cand, rank, ALU.mult))
            then(nc.vector.tensor_reduce(k.rt_c[:], cand, AX.X, ALU.max))
            then(nc.vector.tensor_tensor(two, rank, col(k.rt_c[:]), ALU.is_equal))
            then(nc.vector.tensor_tensor(one, one, two, ALU.add))
            then(nc.vector.tensor_tensor(wt, ex, one, ALU.mult))
            then(nc.vector.tensor_reduce(k.rt_m[:], wt, AX.X, ALU.add))
            then(nc.vector.reciprocal(k.rt_m[:], k.rt_m[:]))
            then(nc.vector.tensor_scalar(k.rt_m[:], k.rt_m[:], 0.5, None, ALU.mult))
            then(nc.vector.tensor_tensor(wt, wt, col(k.rt_m[:]), ALU.mult))
            for s in range(3):
                then(nc.vector.tensor_copy(k.rt_bf, wt))
                op = nc.vector.tensor_copy(k.rt_part[:, :, :, s], k.rt_bf)
                op.then_inc(k.rt_parts, 1)
                if s < 2:
                    then(nc.vector.tensor_tensor(wt, wt, k.rt_bf, ALU.subtract))


def experts(nc, k, a):
    UNITS = 2 * E
    kr, ks, er, o = k.big[0][:, 0:2 * CH], k.big[0][:, 2 * CH:6 * CH], k.big[1][:, 0:2 * CH], k.big[1][:, 2 * CH:4 * CH]

    mixed = k.big[3].rearrange("p (s a n) -> p s a n", s=4, a=2)
    acc = k.big[1][:, 4 * CH:6 * CH].rearrange("p (c n) -> p c n", c=2)

    def done(s, n):
        return n + (1 + PRIMED.get(s, 0))

    with nc.Block() as block:
        @block.vector
        def _(dve):
            def begin(it, c):
                nc.vector.tensor_copy(acc[:, c, :], k.Y[:, bass.ds(it * L + c * CH, CH)]).then_inc(k.ex_y, 1)
                now = k.N[:, bass.ds(it * PADL + 1 + c * CH, CH)]
                before = k.N[:, bass.ds(it * PADL + c * CH, CH)]
                nc.vector.tensor_tensor(k.diff[:, c, :], now, before, ALU.subtract).then_inc(k.ex_diff, 1)
                dve.wait_ge(k.ex_diff, it * 2 + (c + 1))

            def mix(it, j):
                n, c, e = it * UNITS + j, j // E, j % E
                if e == 0:
                    begin(it, c)
                before = k.N[:, bass.ds(it * PADL + c * CH, CH)]
                dve.wait_ge(k.ex_r, n + 1)
                nc.vector.scalar_tensor_tensor(mixed[:, j % 4, 0, :], k.diff[:, c, :], k.vec(f"cm_k{e}"), before, ALU.mult, ALU.add)
                nc.vector.scalar_tensor_tensor(mixed[:, j % 4, 1, :], k.diff[:, c, :], k.vec(f"cm_r{e}"), before, ALU.mult, ALU.add).then_inc(k.ex_mix, 1)

            def gate(it, j):
                n, oj = it * UNITS + j, o[:, (j % 2) * CH:(j % 2 + 1) * CH]
                dve.wait_ge(k.ex_v, done("ex_v", n))
                dve.wait_ge(k.ex_tanh, done("ex_tanh", n))
                dve.wait_ge(k.ex_added, n + 1)
                nc.vector.scalar_tensor_tensor(oj, er[:, (j % 2) * CH:(j % 2 + 1) * CH], 1.0, k.bank[4 + j % 2][:], ALU.add, ALU.mult).then_inc(k.ex_gate, 1)
                dve.wait_ge(k.ex_gate, done("ex_gate", n))
                dve.wait_ge(k.ex_tw, done("ex_tw", n))
                nc.vector.tensor_tensor(oj, oj, k.bank[7][:], ALU.mult).then_inc(k.ex_weighed, 1)

            def finish(it, c):
                at = bass.ds(it * L + c * CH, CH)
                dve.wait_ge(k.ex_added, done("ex_added", it * UNITS + (c + 1) * E - 1))
                nc.vector.tensor_tensor(k.X[:, at], k.X[:, at], acc[:, c, :], ALU.add)

            def turn(it, last):
                for j in range(UNITS):
                    gate(it, j)
                    if j + 3 < UNITS:
                        mix(it, j + 3)
                    elif not last:
                        mix(it + 1, j + 3 - UNITS)
                    if j == E:
                        finish(it, 0)
                finish(it, 1)

            for j in range(3):
                mix(0, j)
            with dve.Fori(0, B - 1) as it:
                turn(it, False)
            turn(B - 1, True)

        @block.tensor
        def _(pe):
            def up(it, j):
                n, e = it * UNITS + j, j % E
                pe.wait_ge(k.ex_mix, done("ex_mix", n))
                pe.wait_ge(k.ex_relu, n + 1)
                for h in range(2):
                    op = nc.tensor.matmul(k.bank[2 * (j % 2) + h][:], k.eWk[:, e, h * P:(h + 1) * P], mixed[:, j % 4, 0, :], start=True, stop=True)
                op.then_inc(k.ex_up, 1)
                pe.wait_ge(k.ex_tanh, n + 1)
                nc.tensor.matmul(k.bank[6][:], k.eWr[:, e, :], mixed[:, j % 4, 1, :], start=True, stop=True).then_inc(k.ex_r, 1)

            def turn(it, last):
                for j in range(UNITS):
                    n, c, e = it * UNITS + j, j // E, j % E
                    if j + 1 < UNITS:
                        up(it, j + 1)
                    elif not last:
                        up(it + 1, 0)
                    pe.wait_ge(k.ex_sq, done("ex_sq", n))
                    pe.wait_ge(k.ex_gate, n + 1)
                    for h in range(2):
                        op = nc.tensor.matmul(k.bank[4 + j % 2][:], k.eWv[:, e, h, :], ks[:, (2 * (j % 2) + h) * CH:(2 * (j % 2) + h + 1) * CH], start=(h == 0), stop=(h == 1))
                    op.then_inc(k.ex_v, 1)
                    pe.wait_ge(k.ex_weighed, n + 1)
                    nc.tensor.matmul(k.bank[7][:], k.sel[:, e, :], k.twT[:, bass.ds(it * L + c * CH, CH)], start=True, stop=True).then_inc(k.ex_tw, 1)

            up(0, 0)
            with pe.Fori(0, B - 1) as it:
                turn(it, False)
            turn(B - 1, True)

        @block.scalar
        def _(act):
            with act.Fori(0, B) as it:
                for j in range(UNITS):
                    n = it * UNITS + j
                    act.wait_ge(k.ex_up, done("ex_up", n))
                    act.wait_ge(k.ex_sq, n + 1)
                    for h in range(2):
                        op = nc.scalar.activation(kr[:, h * CH:(h + 1) * CH], k.bank[2 * (j % 2) + h][:], ACT.Relu)
                    op.then_inc(k.ex_relu, 1)
                    act.wait_ge(k.ex_r, done("ex_r", n))
                    act.wait_ge(k.ex_gate, n + 1)
                    nc.scalar.activation(er[:, (j % 2) * CH:(j % 2 + 1) * CH], k.bank[6][:], ACT.Tanh, scale=0.5).then_inc(k.ex_tanh, 1)
                    act.wait_ge(k.ex_relu, done("ex_relu", n))
                    act.wait_ge(k.ex_v, n + 1)
                    nc.scalar.activation(ks[:, (j % 2) * 2 * CH:(j % 2 + 1) * 2 * CH], kr, ACT.Square).then_inc(k.ex_sq, 1)

        @block.gpsimd
        def _(pool):
            with pool.Fori(0, B) as it:
                for j in range(UNITS):
                    n, c, e = it * UNITS + j, j // E, j % E
                    oj = o[:, (j % 2) * CH:(j % 2 + 1) * CH]
                    pool.wait_ge(k.ex_weighed, done("ex_weighed", n))
                    if e == 0:
                        pool.wait_ge(k.ex_y, it * 2 + (c + 1))
                    pool.wait_ge(k.ex_added, n + 2)
                    nc.gpsimd.tensor_tensor(acc[:, c, :], acc[:, c, :], oj, ALU.add).then_inc(k.ex_added, 1)


def stage_rwkv(nc, k, a, X, Y):
    N = lambda it, c: padded(k.N, it, c)
    with ExitStack() as ctx:
        sems = begin_stage(nc, ctx, MOE_SEMS)
        (k.mix_diff, k.mix_in, k.kvr, k.kvr_out, k.wkv_w, k.wkv_arg, k.wkv_exp, k.wkv_den, k.wkv_ln, k.wkv_rden,
         k.wkv_init, k.wkv_e2bv, k.wkv_e2v, k.wkv_v, k.wkv_step, k.rt_prod, k.rt_copied, k.rt_turned, k.rt_parts,
         k.rt_wT, k.rt_back, k.rt_step, k.rt_exps, k.rt_const, k.rt_sel, k.ex_diff, k.ex_mix, k.ex_r, k.ex_v,
         k.ex_tanh, k.ex_added, k.ex_gate, k.ex_tw, k.ex_weighed, k.ex_up, k.ex_relu, k.ex_sq, k.ex_y) = sems
        k.ln(X, Y)
        k.ln(Y, N, gain="ln1_g", bias="ln1_b")
        rwkv_mix(nc, k, a)
        wkv(nc, k, a)
        project_add(nc, k, k.pa_calls, k.wA[:, 3, :], lambda it, c: plain(k.big[2], it, c), Y)
        k.pa_calls += 1
        k.ln(Y, N, gain="ln2_g", bias="ln2_b")
        route(nc, k, a)
        experts(nc, k, a)
        end_stage(nc, sems)


def feedforward(nc, k, a, call):
    GR, GW = 3, 3 * DM
    TI = CH // P
    Z = k.big[1]
    base = call * NCH
    own = (k.bank[5], k.bank[3])
    masks = (k.bank[6], k.bank[7], k.bank[4])
    xm = [k.big[0][:, c * CH:(c + 1) * CH] for c in range(2)]
    hid = [k.big[0][:, (2 + 3 * c) * CH:(5 + 3 * c) * CH] for c in range(2)]
    hm = k.big[3][:, 0:3 * CH]
    u = [k.big[2][0:DM + 1, c * CH:(c + 1) * CH] for c in range(2)]
    sc = [k.big[2][:, (2 + c) * CH:(3 + c) * CH] for c in range(2)]
    three = [lambda c=c, j=j: sc[c][:, j * 64:j * 64 + TI * NP].rearrange("p (t e) -> p t e", e=NP) for c in range(2) for j in range(3)]
    cand, hot = [three[0](), three[3]()], [three[1](), three[4]()]
    top = [sc[c][:, 192:192 + TI] for c in range(2)]
    hotT = [k.big[2][:, 4 * CH + c * 256:4 * CH + (c + 1) * 256].bitcast(BF16) for c in range(2)]
    with nc.Block() as block:
        @block.sync
        def _(sp):
            if call == 0:
                for p in range(NP):
                    sp.dma_start(k.W1[:, p // 3, (p % 3) * DM:(p % 3 + 1) * DM], a["L0_ffn_W1"][p]).then_inc(k.ff_w_in, 16)
                sp.dma_start(k.Wo1, a["L0_ffn_Wo1"]).then_inc(k.ff_w_in, 16)
                sp.wait_ge(k.ff_zero, 1)
                sp.dma_start(k.W2[0:GW, :, :], a["L0_ffn_W2"].rearrange("(g q) m d -> (q m) g d", g=GR)).then_inc(k.ff_w_in, 16)
                sp.dma_start(k.W2[GW:GW + NP, 0, :], a["L0_ffn_b2"]).then_inc(k.ff_w_in, 16)
                sp.dma_start(k.Wo2[0:DM, :], a["L0_ffn_Wo2"]).then_inc(k.ff_w_in, 16)
                sp.dma_start(k.Wo2[DM:DM + 1, :], a["L0_ffn_bo2"].rearrange("(o n) -> o n", o=1)).then_inc(k.ff_w_in, 16)

        @block.gpsimd
        def _(pool):
            if call == 0:
                nc.gpsimd.memset(k.W1[:, :, GW:P], 0.0).then_inc(k.ff_const, 1)
                for p in range(NP):
                    nc.gpsimd.memset(k.prank[:, p:p + 1], float(NP - p)).then_inc(k.ff_const, 1)
                nc.gpsimd.memset(k.spread, 0.0).then_inc(k.ff_spread, 1)
                pool.wait_ge(k.ff_spread, 1)
                sv = k.spread[:, :, 0:GW].rearrange("p g (q m) -> p g q m", m=DM)
                nc.gpsimd.affine_select(out=sv, in_=sv, compare_op=ALU.not_equal, fill=1.0, base=0,
                                        pattern=[[-3, GR], [-1, 3], [0, DM]], channel_multiplier=1).then_inc(k.ff_spread, 1)
                so = k.spread[:, 0, GW:P]
                nc.gpsimd.affine_select(out=so, in_=so, compare_op=ALU.not_equal, fill=1.0, base=0,
                                        pattern=[[-1, P - GW]], channel_multiplier=1).then_inc(k.ff_spread, 1)
            for c in range(2):
                nc.gpsimd.memset(hotT[c], 0.0).then_inc(k.ff_hot0, 1)

        @block.vector
        def _(dve):
            for c in range(2):
                nc.vector.memset(u[c][DM:DM + 1, :], 1.0).then_inc(k.ff_hot0, 1)
            if call == 0:
                nc.vector.memset(k.W2[:, 0, :], 0.0).then_inc(k.ff_zero, 1)
                dve.wait_ge(k.ff_const, 1 + NP)
                dve.wait_ge(k.ff_spread, 3)
                nc.vector.tensor_copy(k.spread16[:], k.spread).then_inc(k.ff_spread16, 1)
            with dve.Fori(0, B) as it:
                def mix(c):
                    g = it * 2 + (base + c)
                    n = lambda s: k.N[:, bass.ds(it * PADL + 1 + c * CH + s, CH)]
                    dve.wait_ge(k.ff_h, g * 3 + 3)
                    nc.vector.tensor_scalar(xm[c], n(-1), k.vec("mix0"), None, ALU.mult).then_inc(k.ff_mix1, 1)
                    dve.wait_ge(k.ff_mix1, g + 1)
                    nc.vector.scalar_tensor_tensor(xm[c], n(0), k.vec("mix1"), xm[c], ALU.mult, ALU.add).then_inc(k.ff_mix2, 1)
                    dve.wait_ge(k.ff_mix2, g + 1)
                    nc.vector.scalar_tensor_tensor(xm[c], n(1), k.vec("mix2"), xm[c], ALU.mult, ALU.add).then_inc(k.ff_mix, 1)

                def choose(c):
                    g = it * 2 + (base + c)
                    rank = k.prank[:, None, :].to_broadcast([P, TI, NP])
                    scores = own[c][:, 0:TI * NP].rearrange("p (t e) -> p t e", e=NP)
                    col = top[c][:, :, None].to_broadcast([P, TI, NP])
                    dve.wait_ge(k.ff_score, g + 1)
                    nc.vector.tensor_reduce(top[c], scores, AX.X, ALU.max).then_inc(k.ff_step, 1)
                    dve.wait_ge(k.ff_step, g * 4 + 1)
                    nc.vector.tensor_tensor(cand[c], scores, col, ALU.is_equal).then_inc(k.ff_step, 1)
                    dve.wait_ge(k.ff_step, g * 4 + 2)
                    nc.vector.tensor_tensor(cand[c], cand[c], rank, ALU.mult).then_inc(k.ff_step, 1)
                    dve.wait_ge(k.ff_step, g * 4 + 3)
                    nc.vector.tensor_reduce(top[c], cand[c], AX.X, ALU.max).then_inc(k.ff_step, 1)
                    dve.wait_ge(k.ff_step, g * 4 + 4)
                    nc.vector.tensor_tensor(hot[c], rank, col, ALU.is_equal).then_inc(k.ff_hot, 1)

                def mask(c):
                    g = it * 2 + (base + c)
                    dve.wait_ge(k.ff_out, g + 1)
                    for j in range(GR):
                        dve.wait_ge(k.ff_hid, g * 3 + (j + 1 + PRIMED["ff_hid"]))
                        dve.wait_ge(k.ff_spreads, g * 3 + (j + 1))
                        nc.vector.tensor_tensor(hm[:, j * CH:(j + 1) * CH], hid[c][:, j * CH:(j + 1) * CH], masks[j][:], ALU.mult).then_inc(k.ff_masked, 1)

                def add(c):
                    g = it * 2 + (base + c)
                    dve.wait_ge(k.ff_out, g + (1 + PRIMED["ff_out"]))
                    nc.vector.tensor_tensor(Z[:, bass.ds(it * L + c * CH, CH)], k.N[:, bass.ds(it * PADL + 1 + c * CH, CH)], own[c][:], ALU.add).then_inc(k.ff_z, 1)

                mix(0)
                mix(1)
                choose(0)
                choose(1)
                mask(0)
                add(0)
                mask(1)
                add(1)

        @block.tensor
        def _(pe):
            if call == 0:
                pe.wait_ge(k.ff_w_in, 16 * (NP + 5))
                pe.wait_ge(k.ff_spread16, 1)
                pe.wait_ge(k.ff_const, 1 + NP)
            pe.wait_ge(k.ff_hot0, 4 * call + 4)
            with pe.Fori(0, B) as it:
                def hidden(c):
                    g = it * 2 + (base + c)
                    pe.wait_ge(k.ff_mix, g + 1)
                    pe.wait_ge(k.ff_z, g + 1)
                    nc.tensor.matmul(own[c][0:DM, :], k.Wo1, xm[c], start=True, stop=True).then_inc(k.ff_up, 1)
                    for j in range(GR):
                        pe.wait_ge(k.ff_hid, g * 3 + (j + 1))
                        nc.tensor.matmul(k.bank[j][:], k.W1[:, j, :], xm[c], start=True, stop=True).then_inc(k.ff_h, 1)

                def scores(c):
                    pe.wait_ge(k.ff_u, it * 2 + (base + c + 1))
                    for t in range(TI):
                        op = nc.tensor.matmul(own[c][:, t * NP:(t + 1) * NP], u[c][:, t * P:(t + 1) * P], k.Wo2[:], start=True, stop=True)
                    op.then_inc(k.ff_score, 1)

                def turn(c):
                    pe.wait_ge(k.ff_hot, it * 2 + (base + c + 1))
                    for t in range(TI):
                        op = nc.tensor.transpose(own[c][0:NP, t * P:(t + 1) * P], hot[c][:, t, :], k.ident[:])
                    op.then_inc(k.ff_hotT, 1)

                def spread(c):
                    g = it * 2 + (base + c)
                    pe.wait_ge(k.ff_hot16, g + 1)
                    for j in range(GR):
                        pe.wait_ge(k.ff_masked, g * 3 + (j + 1 + PRIMED["ff_masked"] - GR))
                        nc.tensor.matmul(masks[j][:], k.spread16[:, j, :], hotT[c], start=True, stop=True).then_inc(k.ff_spreads, 1)

                def down(c):
                    g = it * 2 + (base + c)
                    for j in range(GR):
                        rows = P if j == 0 else GW
                        pe.wait_ge(k.ff_masked, g * 3 + (j + 1 + PRIMED["ff_masked"]))
                        op = nc.tensor.matmul(own[c][:], k.W2[0:rows, j, :], hm[0:rows, j * CH:(j + 1) * CH], start=(j == 0), stop=(j == GR - 1))
                    op.then_inc(k.ff_out, 1)

                hidden(0)
                scores(0)
                hidden(1)
                scores(1)
                turn(0)
                spread(0)
                turn(1)
                down(0)
                spread(1)
                down(1)

        @block.scalar
        def _(act):
            with act.Fori(0, B) as it:
                for c in range(2):
                    g = it * 2 + (base + c)
                    act.wait_ge(k.ff_up, g + 1)
                    nc.scalar.activation(u[c][0:DM, :], own[c][0:DM, :], ACT.Tanh, bias=k.vec("bo1", DM)).then_inc(k.ff_u, 1)
                    for j in range(GR):
                        act.wait_ge(k.ff_h, g * 3 + (j + 1 + PRIMED["ff_h"]))
                        act.wait_ge(k.ff_masked, g * 3 + (j + 1))
                        nc.scalar.activation(hid[c][:, j * CH:(j + 1) * CH], k.bank[j][:], ACT.Identity, bias=k.vec(f"b1_{j}")).then_inc(k.ff_hid, 1)
                for c in range(2):
                    g = it * 2 + (base + c)
                    act.wait_ge(k.ff_hotT, g + 1)
                    nc.scalar.activation(hotT[c][0:NP, :], own[c][0:NP, :], ACT.Copy).then_inc(k.ff_hot16, 1)


def stage_ffn(nc, k, a, X, Y):
    call = k.ff_calls
    k.ff_calls += 1
    k.ln(X, lambda it, c: padded(k.N, it, c))
    feedforward(nc, k, a, call)
    k.ln(lambda it, c: plain(k.big[1], it, c), None, gain="gamma", bias="beta", residual=X)


def lru(nc, k, a):
    KK, KV, R = k.big[0], k.big[1], k.big[2]
    u1, u2 = k.big[3][:, 0:L + 1], k.big[3][:, L + 1:2 * L + 2]
    t1, t2 = k.big[4][:, 0:L], k.big[4][:, L:2 * L]
    W_rkv, W_o = k.lruw[:, 0:3 * P], k.lruw[:, 3 * P:4 * P]
    with nc.Block() as block:
        @block.sync
        def _(sp):
            sp.dma_start(W_rkv, a["L1_attn_b_W_rkv"]).then_inc(k.lr_w_in, 16)
            sp.dma_start(W_o, a["L1_attn_b_W_o"]).then_inc(k.lr_w_in, 16)

        @block.tensor
        def _(pe):
            pe.wait_ge(k.lr_w_in, 32)
            with pe.Fori(0, B) as it:
                for c in range(2):
                    for j in range(3):
                        n = it * 6 + (3 * c + j)
                        pe.wait_ge(k.lr_read, n + 1)
                        nc.tensor.matmul(k.bank[3 * c + j][:], W_rkv[:, j * P:(j + 1) * P], k.Y[:, bass.ds(it * L + c * CH, CH)],
                                         start=True, stop=True).then_inc(k.lr_prod, 1)

        @block.scalar
        def _(act):
            act.preload_act_table_set("natural_log_exp_and_others")
            act.wait_ge(k.lr_init, 1)
            nc.scalar.activation(k.lr_nu[:], k.vec("nu_log"), ACT.Exp).then_inc(k.lr_sc, 1)
            act.wait_ge(k.lr_sc, 1)
            nc.scalar.activation(k.lr_lam[:], k.lr_nu[:], ACT.Exp, scale=-1.0).then_inc(k.lr_sc, 1)
            nc.scalar.activation(k.lr_own[:], k.vec("nu_log"), ACT.Exp, bias=k.vec("gamma_log")).then_inc(k.lr_sc, 1)

            def exps(it):
                for c in range(2):
                    at = bass.ds(it * L + c * CH, CH)
                    n = it * 6 + 3 * c
                    wait_apart(act, k, k.lr_prod, n + 1)
                    nc.scalar.activation(R[:, at], k.bank[3 * c][:], ACT.Exp, bias=k.lr_nbr[:, 0:1], scale=-1.0).then_inc(k.lr_read, 1)
                    wait_apart(act, k, k.lr_prod, n + 2)
                    nc.scalar.activation(KK[:, at], k.bank[3 * c + 1][:], ACT.Exp, bias=k.vec("bkk")).then_inc(k.lr_read, 1)
                    wait_apart(act, k, k.lr_prod, n + 3)
                    nc.scalar.activation(KV[:, at], k.bank[3 * c + 2][:], ACT.Identity, bias=k.vec("bvv")).then_inc(k.lr_read, 1)

            def over(it):
                at = bass.ds(it * L, L)
                wait_apart(act, k, k.lr_den, it + 1)
                nc.scalar.activation(KK[:, at], KK[:, at], ACT.Ln).then_inc(k.lr_ln, 1)
                wait_apart(act, k, k.lr_ln, it + 1)
                nc.scalar.activation(KK[:, at], KK[:, at], ACT.Exp, scale=-1.0).then_inc(k.lr_rden, 1)

            exps(0)
            with act.Fori(1, B) as it:
                exps(it)
                over(it - 1)
            over(B - 1)

        @block.vector
        def _(dve):
            nc.vector.tensor_scalar(k.lr_nbr[:], k.vec("br"), -1.0, None, ALU.mult).then_inc(k.lr_init, 1)
            nc.vector.memset(u1[:, 0:1], 0.0)
            nc.vector.memset(u2[:, 0:1], 0.0)
            dve.wait_ge(k.lr_sc, 3)
            nc.vector.tensor_copy(k.lam, k.lr_lam[:, 0:1].to_broadcast([P, L])).then_inc(k.lr_init, 1)
            dve.wait_ge(k.lr_init, 2)

            def sums(it):
                at = bass.ds(it * L, L)
                s = it * 6
                dve.wait_ge(k.lr_read, it * 6 + (6 + PRIMED["lr_read"]))
                nc.vector.tensor_tensor(KV[:, at], KV[:, at], KK[:, at], ALU.mult).then_inc(k.lr_step, 1)
                dve.wait_ge(k.lr_step, s + 1)
                nc.vector.tensor_tensor_scan(u2[:, 1:L + 1], k.lam, KK[:, at], 0.0, ALU.mult, ALU.add).then_inc(k.lr_step, 1)
                nc.vector.tensor_tensor_scan(u1[:, 1:L + 1], k.lam, KV[:, at], 0.0, ALU.mult, ALU.add).then_inc(k.lr_step, 1)
                nc.vector.tensor_scalar(t2, KK[:, at], k.lr_own[:, 0:1], 1e-6, ALU.mult, ALU.add)
                nc.vector.tensor_scalar(t1, KV[:, at], k.lr_own[:, 0:1], None, ALU.mult).then_inc(k.lr_step, 1)
                dve.wait_ge(k.lr_step, s + 4)
                nc.vector.scalar_tensor_tensor(t2, u2[:, 0:L], k.lr_lam[:, 0:1], t2, ALU.mult, ALU.add).then_inc(k.lr_step, 1)
                nc.vector.scalar_tensor_tensor(KV[:, at], u1[:, 0:L], k.lr_lam[:, 0:1], t1, ALU.mult, ALU.add).then_inc(k.lr_step, 1)
                dve.wait_ge(k.lr_step, s + 6)
                nc.vector.scalar_tensor_tensor(KK[:, at], R[:, at], 1.0, t2, ALU.add, ALU.mult).then_inc(k.lr_den, 1)

            def quotient(it):
                at = bass.ds(it * L, L)
                dve.wait_ge(k.lr_rden, it + 1)
                nc.vector.tensor_tensor(R[:, at], KV[:, at], KK[:, at], ALU.mult).then_inc(k.lr_x, 1)

            sums(0)
            with dve.Fori(1, B) as it:
                sums(it)
                quotient(it - 1)
            quotient(B - 1)


def stage_lru(nc, k, a, X, Y):
    k.ln(X, Y)
    lru(nc, k, a)
    project_add(nc, k, k.pa_calls, k.lruw[:, 3 * P:4 * P], lambda it, c: plain(k.big[2], it, c), X, bias=k.vec("lru_bo"))
    k.pa_calls += 1


def tree_weights(nc, k, a):
    rows = k.big[0][:, 0:8 * P].rearrange("p (j d) -> p j d", d=P)
    turned = k.big[1][:, 0:5 * P].rearrange("p (j d) -> p j d", d=P)
    with nc.Block() as block:
        @block.sync
        def _(sp):
            sp.dma_start(rows[:, 0, :], a["L1_ffn_routers"][0:P, :]).then_inc(k.tw_in, 16)
            sp.dma_start(rows[0:P - 1, 1, :], a["L1_ffn_routers"][P:2 * P - 1, :]).then_inc(k.tw_in, 16)
            sp.dma_start(rows[:, 2:4, :], a["L1_ffn_leaf_values"].rearrange("(h m) d -> m h d", h=2)).then_inc(k.tw_in, 16)
            sp.dma_start(rows[:, 4, :], a["L1_ffn_Wout_w"]).then_inc(k.tw_in, 16)
            sp.dma_start(rows[:, 5, :], a["L1_ffn_Wq"]).then_inc(k.tw_in, 16)

        @block.tensor
        def _(pe):
            pe.wait_ge(k.tw_in, 5 * 16)
            for j in range(5):
                n = P - 1 if j == 1 else P
                nc.tensor.transpose(k.bank[j // 4][:, (j % 4) * P:(j % 4) * P + n], rows[0:n, j, :], k.ident[0:n, 0:n]).then_inc(k.tw_turned, 1)
            pe.wait_ge(k.tw_copied, 5)
            nc.tensor.matmul(k.bank[2][:, 0:2 * P], rows[:, 5, :], turned[:, 0:2, :].rearrange("p j d -> p (j d)"), start=True, stop=True).then_inc(k.tw_prod, 1)
            for h in range(2):
                nc.tensor.matmul(k.bank[3 + h][:, 0:P], turned[:, 2 + h, :], turned[:, 4, :], start=True, stop=True).then_inc(k.tw_prod, 1)

        @block.vector
        def _(dve):
            nc.vector.memset(turned[:, 1, :], 0.0).then_inc(k.tw_zero, 1)
            dve.wait_ge(k.tw_zero, 1)
            dve.wait_ge(k.tw_turned, 5)
            for j in range(5):
                n = P - 1 if j == 1 else P
                nc.vector.tensor_copy(turned[:, j, 0:n], k.bank[j // 4][:, (j % 4) * P:(j % 4) * P + n]).then_inc(k.tw_copied, 1)
            dve.wait_ge(k.tw_prod, 3)
            nc.vector.tensor_copy(k.gates, k.bank[2][:, 0:2 * P])
            for h in range(2):
                nc.vector.tensor_copy(k.leaves[:, h, :], k.bank[3 + h][:, 0:P])


def tree(nc, k, a, call):
    TI, M, DEPTH = CH // P, 256, 8
    base = call * NCH
    wide = lambda v: v.rearrange("p (t m) -> p t m", m=M)
    gr = [wide(k.big[0][:, 2 * c * CH:2 * (c + 1) * CH]) for c in range(2)]
    gl = [wide(k.big[0][:, (4 + 2 * c) * CH:(6 + 2 * c) * CH]) for c in range(2)]
    lp = [[wide(k.big[1][:, (4 * c + 2 * s) * CH:(4 * c + 2 * s + 2) * CH]) for s in range(2)] for c in range(2)]
    th = k.big[2][:, 0:2 * CH]
    ys = [k.big[2][:, (2 + c) * CH:(3 + c) * CH] for c in range(2)]
    lpT = [k.big[2][:, (4 + 2 * c) * CH:(6 + 2 * c) * CH] for c in range(2)]

    def done(s, g):
        return g + (1 + PRIMED.get(s, 0))

    with nc.Block() as block:
        @block.tensor
        def _(pe):
            def front(it):
                for c in range(2):
                    g = it * 2 + (base + c)
                    pe.wait_ge(k.tr_th, g + 1)
                    pe.wait_ge(k.tr_ys, done("tr_ys", g))
                    for t in range(TI):
                        op = nc.tensor.matmul(k.bank[2 * c + t // 2][:, (t % 2) * M:(t % 2 + 1) * M], ys[c][:, t * P:(t + 1) * P], k.gates, start=True, stop=True)
                    op.then_inc(k.tr_z, 1)

            def back(it):
                for c in range(2):
                    g = it * 2 + (base + c)
                    pe.wait_ge(k.tr_lpT, g + 1)
                    pe.wait_ge(k.tr_lp, done("tr_lp", g))
                    for h in range(2):
                        for t in range(TI):
                            op = nc.tensor.transpose(k.bank[4 + h][:, t * P:(t + 1) * P], lp[c][1][:, t, h * P:(h + 1) * P], k.ident[:])
                    op.then_inc(k.tr_turned, 1)
                    pe.wait_ge(k.tr_x, g + 1)
                    pe.wait_ge(k.tr_lpT, done("tr_lpT", g))
                    for h in range(2):
                        op = nc.tensor.matmul(k.bank[6 + c][:], k.leaves[:, h, :], lpT[c][:, h * CH:(h + 1) * CH], start=(h == 0), stop=(h == 1))
                    op.then_inc(k.tr_out, 1)

            front(0)
            with pe.Fori(1, NCH // 2) as it:
                front(it)
                back(it - 1)
            back(NCH // 2 - 1)

        @block.scalar
        def _(act):
            def front(it):
                for c in range(2):
                    g = it * 2 + (base + c)
                    act.wait_ge(k.tr_z, g + 1)
                    nc.scalar.activation(ys[c], k.Y[:, bass.ds(it * L + c * CH, CH)], ACT.Copy).then_inc(k.tr_ys, 1)
                for c in range(2):
                    g = it * 2 + (base + c)
                    act.wait_ge(k.tr_z, done("tr_z", g))
                    act.wait_ge(k.tr_g, g + 1)
                    for h in range(2):
                        op = nc.scalar.activation(th[:, h * CH:(h + 1) * CH], k.bank[2 * c + h][:], ACT.Tanh, scale=0.5)
                    op.then_inc(k.tr_th, 1)

            def back(it):
                for c in range(2):
                    g = it * 2 + (base + c)
                    act.wait_ge(k.tr_turned, done("tr_turned", g))
                    act.wait_ge(k.tr_out, g + 1)
                    for h in range(2):
                        op = nc.scalar.activation(lpT[c][:, h * CH:(h + 1) * CH], k.bank[4 + h][:], ACT.Copy)
                    op.then_inc(k.tr_lpT, 1)

            front(0)
            with act.Fori(1, NCH // 2) as it:
                front(it)
                back(it - 1)
            back(NCH // 2 - 1)

        @block.vector
        def _(dve):
            def front(it):
                for c in range(2):
                    g = it * 2 + (base + c)
                    dve.wait_ge(k.tr_th, done("tr_th", g))
                    nc.vector.tensor_scalar(gr[c], wide(th), 0.5, 0.5, ALU.mult, ALU.add)
                    nc.vector.tensor_scalar(gl[c], wide(th), -0.5, 0.5, ALU.mult, ALU.add).then_inc(k.tr_g, 1)
                    dve.wait_ge(k.tr_g, done("tr_g", g))
                    dve.wait_ge(k.tr_turned, g + 1)
                    nc.vector.tensor_copy(lp[c][0][:, :, 0:1], gl[c][:, :, 0:1])
                    nc.vector.tensor_copy(lp[c][0][:, :, 1:2], gr[c][:, :, 0:1]).then_inc(k.tr_step, 1)
                    for level in range(1, DEPTH):
                        n = 2 ** level
                        dve.wait_ge(k.tr_step, g * (DEPTH - 1) + level)
                        src, dst = lp[c][(level - 1) % 2][:, :, 0:n], lp[c][level % 2][:, :, 0:2 * n]
                        pairs = dst.rearrange("p t (n s) -> p t n s", s=2)
                        nc.vector.tensor_tensor(pairs[:, :, :, 0], src, gl[c][:, :, n - 1:2 * n - 1], ALU.mult)
                        op = nc.vector.tensor_tensor(pairs[:, :, :, 1], src, gr[c][:, :, n - 1:2 * n - 1], ALU.mult)
                        op.then_inc(k.tr_lp if level == DEPTH - 1 else k.tr_step, 1)

            def back(it):
                for c in range(2):
                    g = it * 2 + (base + c)
                    at = bass.ds(it * L + c * CH, CH)
                    dve.wait_ge(k.tr_out, done("tr_out", g))
                    nc.vector.scalar_tensor_tensor(k.X[:, at], k.bank[6 + c][:], k.vec("wout_b"), k.X[:, at], ALU.add, ALU.add).then_inc(k.tr_x, 1)

            front(0)
            with dve.Fori(1, NCH // 2) as it:
                front(it)
                back(it - 1)
            back(NCH // 2 - 1)


def stage_tree(nc, k, a, X, Y):
    call = k.tr_calls
    k.tr_calls += 1
    k.ln(X, Y)
    if call == 0:
        tree_weights(nc, k, a)
    tree(nc, k, a, call)


def favor_weights(nc, k, a):
    H, M, DK, G = 16, 32, 8, 4
    rows = k.arena[:, 0:4 * P].rearrange("p (j d) -> p j d", d=P)
    proj = k.arena[:, 4 * P:4 * P + G * DK].rearrange("p (g d) -> p g d", g=G)
    mask = k.arena[:, 5 * P:5 * P + G * H].rearrange("p (g h) -> p g h", g=G)
    wide = k.arena[:, 6 * P:10 * P].rearrange("p (g n) -> p g n", g=G)
    diag = k.arena[:, 10 * P:14 * P]
    with nc.Block() as block:
        @block.sync
        def _(sp):
            for j, w in enumerate((a["L0_attn_b_Wq"], a["L0_attn_b_Wk"], a["L0_attn_b_Wv"], a["L0_attn_b_Wo"])):
                sp.dma_start(rows[:, j, :], w).then_inc(k.fw_in, 16)
            sp.dma_start(proj, a["L0_attn_b_proj"].rearrange("(g h) m d -> (h m) g d", g=G)).then_inc(k.fw_in, 16)

        @block.gpsimd
        def _(pool):
            nc.gpsimd.memset(mask, 1.0).then_inc(k.fw_mask, 1)
            nc.gpsimd.memset(k.fv_own, 1.0 / M).then_inc(k.fw_mask, 1)
            pool.wait_ge(k.fw_mask, 2)
            nc.gpsimd.affine_select(out=mask, in_=mask, compare_op=ALU.is_ge, fill=0.0, base=0,
                                    pattern=[[4 * M, G], [-M, H]], channel_multiplier=1).then_inc(k.fw_mask, 1)
            nc.gpsimd.affine_select(out=k.fv_own, in_=k.fv_own, compare_op=ALU.is_ge, fill=0.0, base=0,
                                    pattern=[[-M, 4]], channel_multiplier=1).then_inc(k.fw_mask, 1)
            pool.wait_ge(k.fw_mask, 4)
            nc.gpsimd.affine_select(out=mask, in_=mask, compare_op=ALU.is_ge, fill=0.0, base=M - 1,
                                    pattern=[[-4 * M, G], [M, H]], channel_multiplier=-1).then_inc(k.fw_mask, 1)
            nc.gpsimd.affine_select(out=k.fv_own, in_=k.fv_own, compare_op=ALU.is_ge, fill=0.0, base=M - 1,
                                    pattern=[[M, 4]], channel_multiplier=-1).then_inc(k.fw_mask, 1)
            nc.gpsimd.memset(k.eps6[:], 1e-6).then_inc(k.fw_mask, 1)

        @block.tensor
        def _(pe):
            pe.wait_ge(k.fw_in, 5 * 16)
            for j in range(4):
                nc.tensor.transpose(k.bank[0][:, j * P:(j + 1) * P], rows[:, j, :], k.ident[:]).then_inc(k.fw_turned, 1)
            pe.wait_ge(k.fw_wide, 1)
            for g in range(G):
                nc.tensor.transpose(k.bank[1][:, g * P:(g + 1) * P], wide[:, g, :], k.ident[:]).then_inc(k.fw_turned, 1)
            pe.wait_ge(k.fw_copied, 2)
            for j in range(2):
                nc.tensor.matmul(k.bank[2 + j][:], rows[:, j, :], diag, start=True, stop=True).then_inc(k.fw_prod, 1)

        @block.vector
        def _(dve):
            dve.wait_ge(k.fw_in, 5 * 16)
            dve.wait_ge(k.fw_mask, 7)
            for g in range(G):
                op = nc.vector.tensor_tensor(wide[:, g, :].rearrange("p (h d) -> p h d", d=DK), proj[:, g:g + 1, :].to_broadcast([P, H, DK]),
                                             mask[:, g, :, None].to_broadcast([P, H, DK]), ALU.mult)
            op.then_inc(k.fw_wide, 1)
            dve.wait_ge(k.fw_turned, 4)
            nc.vector.tensor_copy(k.fv_wT, k.bank[0][:]).then_inc(k.fw_copied, 1)
            dve.wait_ge(k.fw_turned, 8)
            nc.vector.tensor_copy(diag, k.bank[1][:]).then_inc(k.fw_copied, 1)
            for j in range(2):
                dve.wait_ge(k.fw_prod, j + 1)
                nc.vector.tensor_scalar(k.fv_feat[:, j, :], k.bank[2 + j][:], DK ** -0.5, None, ALU.mult)


def favor(nc, k, a):
    H, M, DK, G = 16, 32, 8, 4
    TT = L // P
    ar = k.arena
    ys = [ar[:, c * CH:(c + 1) * CH] for c in range(2)]
    sq = [ar[:, 1024 + s * P:1024 + (s + 1) * P] for s in range(2)]
    va = [ar[:, 1280 + s * 144:1280 + (s + 1) * 144].rearrange("p (h n) -> p h n", n=9) for s in range(2)]
    mx = [ar[:, 1600 + s * H:1600 + (s + 1) * H] for s in range(2)]
    nm = [ar[:, 1632 + s * H:1632 + (s + 1) * H] for s in range(2)]
    rd = [ar[:, 1664 + s * H:1664 + (s + 1) * H] for s in range(2)]
    kv = ar[:, 1696:1696 + B * 144]
    ex = [ar[:, 2560 + s * CH:2560 + (s + 1) * CH] for s in range(2)]
    exT = [ar[:, 3584 + s * CH:3584 + (s + 1) * CH] for s in range(2)]
    o = [ar[:, 4608 + s * P:4608 + (s + 1) * P] for s in range(2)]
    oT = ar[:, 5120:5120 + CH]
    wT = k.fv_wT

    def done(s, n):
        return n + (1 + PRIMED.get(s, 0))

    def copies(act, b, n):
        act.wait_ge(k.fv_proj, b * TT + n + PRIMED["fv_proj"])
        for c in range(2):
            op = nc.scalar.activation(ys[c], k.Y[:, bass.ds(b * L + c * CH, CH)], ACT.Copy)
        op.then_inc(k.fv_ys, 1)

    def statistics(dve, n, s, xw):
        heads = xw.rearrange("p (h m) -> p h m", m=M)
        dve.wait_ge(k.fv_proj, done("fv_proj", n))
        nc.vector.tensor_reduce(mx[s], heads, AX.X, ALU.max).then_inc(k.fv_max, 1)
        dve.wait_ge(k.fv_sq, done("fv_sq", n))
        nc.vector.tensor_reduce(nm[s], sq[s].rearrange("p (h d) -> p h d", d=DK), AX.X, ALU.add).then_inc(k.fv_max, 1)
        dve.wait_ge(k.fv_max, n * 2 + 2)
        nc.vector.tensor_tensor(mx[s], mx[s], nm[s], ALU.add).then_inc(k.fv_off, 1)
        dve.wait_ge(k.fv_off, n + 1)
        dve.wait_ge(k.fv_used, n + 1)
        nc.vector.tensor_tensor(ex[s].rearrange("p (h m) -> p h m", m=M), heads, mx[s][:, :, None].to_broadcast([P, H, M]),
                                ALU.subtract).then_inc(k.fv_arg, 1)

    with nc.Block() as block:
        @block.tensor
        def _(pe):
            with pe.Fori(0, B) as b:
                def project(t):
                    n, s = b * TT + t, t % 2
                    y = ys[t // 4][:, (t % 4) * P:(t % 4 + 1) * P]
                    if t == 0:
                        pe.wait_ge(k.fv_ys, b + 1)
                    pe.wait_ge(k.fv_va, n + 1)
                    nc.tensor.matmul(k.bank[s][:, 0:2 * P], y, wT[:, P:3 * P], start=True, stop=True)
                    pe.wait_ge(k.fv_arg, n + 1)
                    nc.tensor.matmul(k.bank[2 + s][:], y, k.fv_feat[:, 1, :], start=True, stop=True).then_inc(k.fv_proj, 1)

                def gather(t):
                    n, s = b * TT + t, t % 2
                    if t == 0:
                        pe.wait_ge(k.fv_kv, b + 1)
                    pe.wait_ge(k.fv_phi, n + 1)
                    for g in range(G):
                        op = nc.tensor.matmul(k.bank[4][:, g * 36:(g + 1) * 36], ex[s][:, g * P:(g + 1) * P],
                                              va[s][:, 4 * g:4 * g + 4, :].rearrange("p h n -> p (h n)"),
                                              start=(t == 0 and g == 0), stop=(t == TT - 1), skip_group_check=True)
                    op.then_inc(k.fv_used, 1)

                for t in range(TT + 1):
                    if t < TT:
                        project(t)
                    if t >= 1:
                        gather(t - 1)

        @block.scalar
        def _(act):
            act.preload_act_table_set("exp_and_others")
            with act.Fori(0, B) as b:
                copies(act, b, 0)
                for t in range(TT):
                    n, s = b * TT + t, t % 2
                    act.wait_ge(k.fv_proj, done("fv_proj", n))
                    nc.scalar.activation(sq[s], k.bank[s][:, 0:P], ACT.Square, scale=(0.5 / DK) ** 0.5).then_inc(k.fv_sq, 1)
                    act.wait_ge(k.fv_used, n + 1)
                    nc.scalar.activation(va[s][:, :, 0:DK], k.bank[s][:, P:2 * P].rearrange("p (h d) -> p h d", d=DK), ACT.Copy).then_inc(k.fv_va, 1)
                    act.wait_ge(k.fv_arg, done("fv_arg", n))
                    nc.scalar.activation(ex[s], ex[s], ACT.Exp).then_inc(k.fv_exp, 1)

        @block.gpsimd
        def _(pool):
            for s in range(2):
                nc.gpsimd.memset(va[s][:, :, DK:DK + 1], 1.0).then_inc(k.fv_ones, 1)

        @block.vector
        def _(dve):
            dve.wait_ge(k.fv_ones, 2)
            with dve.Fori(0, B) as b:
                def features(t):
                    n, s = b * TT + t, t % 2
                    dve.wait_ge(k.fv_exp, n + 1)
                    nc.vector.tensor_scalar(ex[s], ex[s], 1e-6, None, ALU.add).then_inc(k.fv_phi, 1)

                for t in range(TT + 1):
                    if t < TT:
                        statistics(dve, b * TT + t, t % 2, k.bank[2 + t % 2][:])
                    if t >= 1:
                        features(t - 1)
                dve.wait_ge(k.fv_used, done("fv_used", b * TT + (TT - 1)))
                nc.vector.tensor_tensor(kv[:, bass.ds(b * 144, 144)].rearrange("p (g h n) -> p g h n", g=G, h=4),
                                        k.bank[4][:, 0:144].rearrange("p (g h n) -> p g h n", g=G, h=4),
                                        k.fv_own[:, None, :, None].to_broadcast([P, G, 4, 9]), ALU.mult).then_inc(k.fv_kv, 1)

    n0 = B * TT
    with nc.Block() as block:
        @block.tensor
        def _(pe):
            with pe.Fori(0, B) as b:
                def project(t):
                    n, s = b * TT + (n0 + t), t % 2
                    y = ys[t // 4][:, (t % 4) * P:(t % 4 + 1) * P]
                    if t == 0:
                        pe.wait_ge(k.fv_ys, b + (1 + B))
                    pe.wait_ge(k.fv_sq, n + 1)
                    nc.tensor.matmul(k.bank[s][:, 0:P], y, wT[:, 0:P], start=True, stop=True)
                    pe.wait_ge(k.fv_arg, n + 1)
                    nc.tensor.matmul(k.bank[2 + s][:], y, k.fv_feat[:, 0, :], start=True, stop=True).then_inc(k.fv_proj, 1)

                def turn(t):
                    n, s = b * TT + t, t % 2
                    pe.wait_ge(k.fv_exp, n + (n0 + 1))
                    pe.wait_ge(k.fv_exT, n + 1)
                    for g in range(G):
                        op = nc.tensor.transpose(k.bank[4][:, g * P:(g + 1) * P], ex[s][:, g * P:(g + 1) * P], k.ident[:])
                    op.then_inc(k.fv_used, 1)

                def sums(t):
                    n, s = b * TT + t, t % 2
                    pe.wait_ge(k.fv_exT, done("fv_exT", n))
                    pe.wait_ge(k.fv_o, n + 1)
                    for g in range(G):
                        op = nc.tensor.matmul(k.bank[5][:, g * 36:(g + 1) * 36], exT[s][:, g * P:(g + 1) * P],
                                              kv[:, bass.ds(b * 144 + g * 36, 36)], start=True, stop=True)
                    op.then_inc(k.fv_sums, 1)

                def back(t):
                    n, s = b * TT + t, t % 2
                    pe.wait_ge(k.fv_o, done("fv_o", n))
                    if t % 4 == 0:
                        pe.wait_ge(k.fv_oT, b * 2 + (t // 4 + 1))
                    nc.tensor.transpose(k.bank[6][:, (t % 4) * P:(t % 4 + 1) * P], o[s], k.ident[:]).then_inc(k.fv_back, 1)

                def output(c):
                    g = b * 2 + c
                    pe.wait_ge(k.fv_oT, done("fv_oT", g))
                    pe.wait_ge(k.fv_x, g + 1)
                    nc.tensor.matmul(k.bank[7][:], wT[:, 3 * P:4 * P], oT, start=True, stop=True).then_inc(k.fv_out, 1)

                for t in range(TT + 4):
                    if t < TT:
                        project(t)
                    if 1 <= t < TT + 1:
                        turn(t - 1)
                    if 2 <= t < TT + 2:
                        sums(t - 2)
                    if 3 <= t < TT + 3:
                        back(t - 3)
                    if t in (7, 11):
                        output(t // 8)

        @block.scalar
        def _(act):
            with act.Fori(0, B) as b:
                def squares(t):
                    n, s = b * TT + (n0 + t), t % 2
                    act.wait_ge(k.fv_proj, done("fv_proj", n))
                    nc.scalar.activation(sq[s], k.bank[s][:, 0:P], ACT.Square, scale=(0.5 / DK) ** 0.5).then_inc(k.fv_sq, 1)
                    act.wait_ge(k.fv_arg, done("fv_arg", n))
                    nc.scalar.activation(ex[s], ex[s], ACT.Exp).then_inc(k.fv_exp, 1)

                def turned(t):
                    n, s = b * TT + t, t % 2
                    act.wait_ge(k.fv_used, done("fv_used", n + n0))
                    act.wait_ge(k.fv_sums, n + 1)
                    nc.scalar.activation(exT[s], k.bank[4][:], ACT.Identity, bias=k.eps6[:, 0:1]).then_inc(k.fv_exT, 1)

                def heads(c):
                    g = b * 2 + c
                    act.wait_ge(k.fv_back, g * 4 + 4)
                    act.wait_ge(k.fv_out, g + 1)
                    nc.scalar.activation(oT, k.bank[6][:], ACT.Copy).then_inc(k.fv_oT, 1)

                copies(act, b, n0)
                for t in range(TT + 4):
                    if t < TT:
                        squares(t)
                    if 1 <= t < TT + 1:
                        turned(t - 1)
                    if t in (6, 10):
                        heads(t // 8)

        @block.vector
        def _(dve):
            with dve.Fori(0, B) as b:
                def quotient(t):
                    n, s = b * TT + t, t % 2
                    sums = k.bank[5][:, 0:144].rearrange("p (h n) -> p h n", n=9)
                    dve.wait_ge(k.fv_sums, done("fv_sums", n))
                    nc.vector.tensor_scalar(rd[s], sums[:, :, DK], 1e-6, None, ALU.add).then_inc(k.fv_rd, 1)
                    dve.wait_ge(k.fv_rd, n * 2 + 1)
                    nc.vector.reciprocal(rd[s], rd[s]).then_inc(k.fv_rd, 1)
                    dve.wait_ge(k.fv_rd, n * 2 + 2)
                    nc.vector.tensor_tensor(o[s].rearrange("p (h d) -> p h d", d=DK), sums[:, :, 0:DK],
                                            rd[s][:, :, None].to_broadcast([P, H, DK]), ALU.mult).then_inc(k.fv_o, 1)

                def add(c):
                    g = b * 2 + c
                    at = bass.ds(b * L + c * CH, CH)
                    dve.wait_ge(k.fv_out, done("fv_out", g))
                    nc.vector.scalar_tensor_tensor(k.X[:, at], k.bank[7][:], k.vec("favor_bo"), k.X[:, at], ALU.add, ALU.add).then_inc(k.fv_x, 1)

                for t in range(TT + 4):
                    if t < TT:
                        statistics(dve, b * TT + (n0 + t), t % 2, k.bank[2 + t % 2][:])
                    if 2 <= t < TT + 2:
                        quotient(t - 2)
                    if t in (7, 11):
                        add(t // 8)


def stage_favor(nc, k, a, X, Y):
    k.ln(X, Y)
    with ExitStack() as ctx:
        sems = begin_stage(nc, ctx, FAVOR_SEMS)
        (k.fw_in, k.fw_mask, k.fw_turned, k.fw_wide, k.fw_copied, k.fw_prod, k.fv_ys, k.fv_proj, k.fv_sq, k.fv_va,
         k.fv_max, k.fv_off, k.fv_arg, k.fv_exp, k.fv_phi, k.fv_used, k.fv_kv, k.fv_ones, k.fv_exT, k.fv_sums, k.fv_o,
         k.fv_rd, k.fv_back, k.fv_oT, k.fv_out, k.fv_x) = sems
        favor_weights(nc, k, a)
        favor(nc, k, a)
        end_stage(nc, sems)


def segment_weights(nc, k, a):
    H, DK, G = 16, 8, 4
    brow = k.arena[0:2 * G, 0:P]
    wide = lambda v: v.rearrange("p (g j d) -> p g j d", g=G, d=DK)
    with nc.Block() as block:
        @block.sync
        def _(sp):
            for j, w in enumerate((a["L1_attn_a_Wq"], a["L1_attn_a_Wk"], a["L1_attn_a_Wv"], a["L1_attn_a_Wo"])):
                sp.dma_start(k.sg_w[:, j, :], w).then_inc(k.sw_in, 16)
            sp.wait_ge(k.sw_zero, 3)
            for j, b in enumerate((a["L1_attn_a_bq"], a["L1_attn_a_bk"])):
                sp.dma_start(brow[j * G:(j + 1) * G, :].rearrange("g (j n) -> g j n", j=4)[:, :, 0:DK],
                             b.rearrange("(g j d) -> g j d", g=G, d=DK)).then_inc(k.sw_in, 16)

        @block.vector
        def _(dve):
            nc.vector.memset(brow, 0.0).then_inc(k.sw_zero, 1)
            nc.vector.memset(k.sg_wide[:, 0], 0.0).then_inc(k.sw_zero, 1)
            nc.vector.memset(k.sg_wide[:, 1], 0.0).then_inc(k.sw_zero, 1)
            dve.wait_ge(k.sw_zero, 3)
            dve.wait_ge(k.sw_in, 6 * 16)
            for j in range(2):
                nc.vector.tensor_copy(k.sg_wide[:, j].rearrange("p g (j n) -> p g j n", j=4)[:, :, :, 0:DK], wide(k.sg_w[:, j, :]))
            dve.wait_ge(k.sw_turned, 1)
            nc.vector.tensor_scalar(k.sg_bias[:, 0:G], k.bank[0][:, 0:G], DK ** -0.5, None, ALU.mult)
            nc.vector.tensor_copy(k.sg_bias[:, G:2 * G], k.bank[0][:, G:2 * G])

        @block.tensor
        def _(pe):
            pe.wait_ge(k.sw_in, 6 * 16)
            nc.tensor.transpose(k.bank[0][:, 0:2 * G], brow, k.ident[0:2 * G, 0:2 * G]).then_inc(k.sw_turned, 1)


def segments(nc, k, a):
    H, DK, G, SEG, PAD = 16, 8, 4, 64, 2
    NSEG = L // SEG
    TT = NSEG // 2
    ar = k.arena
    take = [0]

    def part(n):
        take[0] += n
        return ar[:, take[0] - n:take[0]]

    q4 = part(G * L).rearrange("p (g n) -> p g n", g=G)
    k4 = part(G * (NSEG + 2 * PAD) * SEG).rearrange("p (g s n) -> p g s n", g=G, n=SEG)
    vT = part((NSEG + 2 * PAD) * SEG)
    qs = [part(2 * P).rearrange("p (g n) -> p g n", g=2) for _ in range(2)]
    kc = [part(4 * P).rearrange("p (g s n) -> p g s n", g=2, s=2) for _ in range(2)]
    vc = part(2 * P).rearrange("p (s n) -> p s n", s=2)
    vt = part(2 * P).rearrange("p (s n) -> p s n", s=2)
    pr = [part(8 * P) for _ in range(2)]
    pT = part(8 * P)
    mx = [part(64) for _ in range(2)]
    sm = [part(64) for _ in range(2)]
    wt = part(64)
    o, oT = part(P), part(P)
    wide = lambda v: v.rearrange("p (g n) -> p g n", n=16)
    four = lambda v: v.rearrange("p (h g) -> p h g", g=8)

    def done(s, n):
        return n + (1 + PRIMED.get(s, 0))

    def head(s, slot):
        return (2 * s + slot % 2) * 4 + slot // 2

    with nc.Block() as block:
        @block.tensor
        def _(pe):
            def project(b):
                for i in range(18):
                    c, j = i // 9, i % 9
                    w = k.sg_wide[:, j // 4, j % 4, :] if j < 8 else k.sg_w[:, 2, :]
                    if i == 0:
                        pe.wait_ge(k.sg_x, b * TT + 1)
                    if i >= 8:
                        pe.wait_ge(k.sg_took, b * 18 + (i - 7))
                    nc.tensor.matmul(k.bank[i % 8][:], w, k.Y[:, bass.ds(b * L + c * CH, CH)], start=True, stop=True).then_inc(k.sg_proj, 1)
                pe.wait_ge(k.sg_took, b * 18 + 18)

            def scores(T, s):
                n = T * 2 + s
                pe.wait_ge(k.sg_fill, n + 1)
                pe.wait_ge(k.sg_arg, n + 1)
                for half in range(2):
                    if half:
                        pe.wait_ge(k.sg_half, n + 1)
                    for slot in (2 * half, 2 * half + 1, 2 * half + 4, 2 * half + 5):
                        g, j = slot % 2, 2 * (slot // 4) + half
                        for seg in range(2):
                            op = nc.tensor.matmul(k.bank[2 * s + slot // 4][64 * seg:64 * seg + 64, (slot % 4) * P:(slot % 4 + 1) * P],
                                                  qs[s][32 * j:32 * j + DK, g, 64 * seg:64 * seg + 64], kc[s][32 * j:32 * j + DK, g, seg, :],
                                                  start=True, stop=True)
                    if not half:
                        op.then_inc(k.sg_half, 1)
                op.then_inc(k.sg_score, 1)

            def values(T):
                pe.wait_ge(k.sg_vc, T + 1)
                pe.wait_ge(k.sg_x, T + 1)
                for seg in range(2):
                    op = nc.tensor.transpose(k.bank[7][:, seg * P:(seg + 1) * P], vc[:, seg, :], k.ident[:])
                op.then_inc(k.sg_vT, 1)

            def back(T, s):
                n = T * 2 + s
                pe.wait_ge(k.sg_mul, n + 1)
                for q in range(2):
                    pe.wait_ge(k.sg_pT, n * 2 + (q + 1))
                    for h in range(4):
                        op = nc.tensor.transpose(k.bank[4 + q][:, h * P:(h + 1) * P], pr[s][:, (4 * q + h) * P:(4 * q + h + 1) * P], k.ident[:])
                    op.then_inc(k.sg_turned, 1)
                if s == 0:
                    pe.wait_ge(k.sg_vt, T + 1)
                    pe.wait_ge(k.sg_o, T + 1)
                for q in range(2):
                    pe.wait_ge(k.sg_pT, n * 2 + (q + 1 + PRIMED["sg_pT"]))
                    for h in range(4 * q, 4 * q + 4):
                        col = head(s, h) * DK
                        for seg in range(2):
                            op = nc.tensor.matmul(k.bank[6][64 * seg:64 * seg + 64, col:col + DK], pT[:, h * P + 64 * seg:h * P + 64 * seg + 64],
                                                  vt[:, seg, col:col + DK], start=True, stop=True)
                op.then_inc(k.sg_pv, 1)

            def turn(T):
                pe.wait_ge(k.sg_o, done("sg_o", T))
                nc.tensor.transpose(k.bank[7][:, 2 * P:3 * P], o, k.ident[:]).then_inc(k.sg_oturn, 1)

            def output(T):
                pe.wait_ge(k.sg_oT, T + 1)
                nc.tensor.matmul(k.bank[7][:, 3 * P:4 * P], k.sg_w[:, 3, :], oT, start=True, stop=True).then_inc(k.sg_out, 1)

            with pe.Fori(0, B) as b:
                project(b)
                scores(b * TT, 0)
                values(b * TT)
                scores(b * TT, 1)
                back(b * TT, 0)
                with pe.Fori(1, TT) as t:
                    T = b * TT + t
                    scores(T, 0)
                    back(T - 1, 1)
                    turn(T - 1)
                    output(T - 1)
                    scores(T, 1)
                    values(T)
                    back(T, 0)
                back(b * TT + (TT - 1), 1)
                turn(b * TT + (TT - 1))
                output(b * TT + (TT - 1))

        @block.gpsimd
        def _(pool):
            nc.gpsimd.memset(k4[:, :, 0:PAD, :], 0.0).then_inc(k.sg_const, 1)
            nc.gpsimd.memset(k4[:, :, NSEG + PAD:, :], 0.0).then_inc(k.sg_const, 1)
            nc.gpsimd.memset(vT[:, 0:PAD * SEG], 0.0).then_inc(k.sg_const, 1)
            nc.gpsimd.memset(vT[:, (NSEG + PAD) * SEG:], 0.0).then_inc(k.sg_const, 1)
            nc.gpsimd.memset(four(wt)[:, :, 0:4], 1.0).then_inc(k.sg_const, 1)
            nc.gpsimd.memset(four(wt)[:, :, 4:8], 0.25).then_inc(k.sg_const, 1)
            pool.wait_ge(k.sg_const, 6)

            def fill(b, t, s):
                n = (b * TT + t) * 2 + s
                wait_apart(pool, k, k.sg_score, n + 1)
                gs = slice(2 * s, 2 * s + 2)
                nc.gpsimd.tensor_copy(qs[s], q4[:, gs, bass.ds(t * P, P)])
                for seg in range(2):
                    nc.gpsimd.tensor_copy(kc[s][:, :, seg, 0:SEG], k4[:, gs, bass.ds(t * 2 + (seg + PAD), 1), :].rearrange("p g o n -> p g (o n)"))
                    for side in range(2):
                        first = seg + 3 * side
                        for g in range(2):
                            op = nc.gpsimd.tensor_copy(kc[s][:, g, seg, SEG + 32 * side:SEG + 32 * side + 32].rearrange("p (q n) -> p q n", q=2),
                                                       k4[:, 2 * s + g, bass.ds(t * 2 + first, 2), 0:SEG:4])
                op.then_inc(k.sg_fill, 1)

            def values(b, t):
                T = b * TT + t
                vs = vT.rearrange("p (s n) -> p s n", n=SEG)
                wait_apart(pool, k, k.sg_vT, T + 1)
                for seg in range(2):
                    nc.gpsimd.tensor_copy(vc[:, seg, 0:SEG], vs[:, bass.ds(t * 2 + (seg + PAD), 1), :].rearrange("p o n -> p (o n)"))
                    for side in range(2):
                        first = seg + 3 * side
                        op = nc.gpsimd.tensor_copy(vc[:, seg, SEG + 32 * side:SEG + 32 * side + 32].rearrange("p (q n) -> p q n", q=2),
                                                   vs[:, bass.ds(t * 2 + first, 2), 0:SEG:4])
                op.then_inc(k.sg_vc, 1)

            def weigh(T, s):
                n = T * 2 + s
                pool.wait_ge(k.sg_weight, n + 1)
                nc.gpsimd.tensor_tensor(wide(pr[s]), wide(pr[s]), sm[s][:, :, None].to_broadcast([P, 64, 16]), ALU.mult).then_inc(k.sg_mul, 1)

            with pool.Fori(0, B) as b:
                pool.wait_ge(k.sg_took, b * 18 + 18)
                fill(b, 0, 0)
                values(b, 0)
                fill(b, 0, 1)
                weigh(b * TT, 0)
                with pool.Fori(1, TT) as t:
                    fill(b, t, 0)
                    weigh(b * TT + (t - 1), 1)
                    fill(b, t, 1)
                    values(b, t)
                    weigh(b * TT + t, 0)
                weigh(b * TT + (TT - 1), 1)

        @block.scalar
        def _(act):
            act.preload_act_table_set("exp_and_others")

            def take_in(b):
                for i in range(18):
                    c, j = i // 9, i % 9
                    act.wait_ge(k.sg_proj, b * 18 + (i + 1))
                    if j < 4:
                        dst = q4[:, j, c * CH:(c + 1) * CH]
                    elif j < 8:
                        dst = k4[:, j - 4, PAD + 8 * c:PAD + 8 * c + 8, :].rearrange("p s n -> p (s n)")
                    else:
                        dst = vT[:, PAD * SEG + c * CH:PAD * SEG + (c + 1) * CH]
                    nc.scalar.activation(dst, k.bank[i % 8][:], ACT.Identity, bias=k.sg_bias[:, j:j + 1] if j < 8 else k.vec("bv"),
                                         scale=DK ** -0.5 if j < 4 else 1.0).then_inc(k.sg_took, 1)

            def exp(T, s):
                n = T * 2 + s
                act.wait_ge(k.sg_arg, done("sg_arg", n))
                nc.scalar.activation(pr[s], pr[s], ACT.Exp).then_inc(k.sg_exp, 1)

            def turned(T, s):
                n = T * 2 + s
                for q in range(2):
                    act.wait_ge(k.sg_turned, n * 2 + (q + 1))
                    nc.scalar.activation(pT[:, q * 4 * P:(q + 1) * 4 * P], k.bank[4 + q][:], ACT.Copy).then_inc(k.sg_pT, 1)

            def values(T):
                act.wait_ge(k.sg_vT, done("sg_vT", T))
                nc.scalar.activation(vt.rearrange("p s n -> p (s n)"), k.bank[7][:, 0:2 * P], ACT.Copy).then_inc(k.sg_vt, 1)

            def heads(T):
                act.wait_ge(k.sg_pv, T * 2 + 2)
                nc.scalar.activation(o, k.bank[6][:, 0:P], ACT.Copy).then_inc(k.sg_o, 1)

            def heads_turned(T):
                act.wait_ge(k.sg_oturn, T + 1)
                nc.scalar.activation(oT, k.bank[7][:, 2 * P:3 * P], ACT.Copy).then_inc(k.sg_oT, 1)

            with act.Fori(0, B) as b:
                take_in(b)
                exp(b * TT, 0)
                values(b * TT)
                exp(b * TT, 1)
                turned(b * TT, 0)
                with act.Fori(1, TT) as t:
                    T = b * TT + t
                    exp(T, 0)
                    turned(T - 1, 1)
                    heads(T - 1)
                    heads_turned(T - 1)
                    exp(T, 1)
                    values(T)
                    turned(T, 0)
                turned(b * TT + (TT - 1), 1)
                heads(b * TT + (TT - 1))
                heads_turned(b * TT + (TT - 1))

        @block.vector
        def _(dve):
            def shift(T, s):
                n = T * 2 + s
                m = four(mx[s])
                dve.wait_ge(k.sg_score, done("sg_score", n))
                for q in range(2):
                    op = nc.vector.tensor_reduce(mx[s][:, q * 32:(q + 1) * 32], k.bank[2 * s + q][:].rearrange("p (g n) -> p g n", n=16), AX.X, ALU.max)
                op.then_inc(k.sg_step, 1)
                dve.wait_ge(k.sg_step, n * 4 + 1)
                nc.vector.tensor_reduce(sm[s][:, 0:8], m[:, :, 0:4], AX.X, ALU.max).then_inc(k.sg_step, 1)
                dve.wait_ge(k.sg_step, n * 4 + 2)
                nc.vector.tensor_copy(m[:, :, 0:4], sm[s][:, 0:8, None].to_broadcast([P, 8, 4])).then_inc(k.sg_step, 1)
                dve.wait_ge(k.sg_step, n * 4 + 3)
                for q in range(2):
                    op = nc.vector.tensor_tensor(wide(pr[s][:, q * 4 * P:(q + 1) * 4 * P]), k.bank[2 * s + q][:].rearrange("p (g n) -> p g n", n=16),
                                                 mx[s][:, q * 32:(q + 1) * 32, None].to_broadcast([P, 32, 16]), ALU.subtract)
                op.then_inc(k.sg_arg, 1)

            def weight(T, s):
                n = T * 2 + s
                m = four(sm[s])
                dve.wait_ge(k.sg_exp, n + 1)
                nc.vector.tensor_reduce(sm[s], wide(pr[s]), AX.X, ALU.add).then_inc(k.sg_w1, 1)
                dve.wait_ge(k.sg_w1, n * 3 + 1)
                nc.vector.tensor_reduce(mx[s][:, 0:8], m[:, :, 0:4], AX.X, ALU.add).then_inc(k.sg_w1, 1)
                dve.wait_ge(k.sg_w1, n * 3 + 2)
                nc.vector.tensor_copy(m[:, :, 0:4], mx[s][:, 0:8, None].to_broadcast([P, 8, 4])).then_inc(k.sg_w1, 1)
                dve.wait_ge(k.sg_w1, n * 3 + 3)
                nc.vector.reciprocal(sm[s], sm[s]).then_inc(k.sg_step, 1)
                dve.wait_ge(k.sg_step, n * 4 + 4)
                nc.vector.tensor_tensor(sm[s], sm[s], wt, ALU.mult).then_inc(k.sg_weight, 1)

            def add(T):
                at = bass.ds(T * P, P)
                dve.wait_ge(k.sg_out, T + 1)
                nc.vector.scalar_tensor_tensor(k.X[:, at], k.bank[7][:, 3 * P:4 * P], k.vec("bo"), k.X[:, at], ALU.add, ALU.add).then_inc(k.sg_x, 1)

            dve.wait_ge(k.sg_const, 6)
            with dve.Fori(0, B) as b:
                shift(b * TT, 0)
                weight(b * TT, 0)
                shift(b * TT, 1)
                with dve.Fori(1, TT) as t:
                    T = b * TT + t
                    weight(T - 1, 1)
                    shift(T, 0)
                    add(T - 1)
                    weight(T, 0)
                    shift(T, 1)
                weight(b * TT + (TT - 1), 1)
                add(b * TT + (TT - 1))


def stage_segments(nc, k, a, X, Y):
    k.ln(X, Y)
    with ExitStack() as ctx:
        sems = begin_stage(nc, ctx, SEGMENT_SEMS)
        (k.sw_in, k.sw_zero, k.sw_turned, k.sg_took, k.sg_proj, k.sg_fill, k.sg_arg, k.sg_score, k.sg_half, k.sg_vc,
         k.sg_x, k.sg_vT, k.sg_mul, k.sg_pT, k.sg_turned, k.sg_vt, k.sg_o, k.sg_pv, k.sg_oturn, k.sg_oT, k.sg_out,
         k.sg_const, k.sg_weight, k.sg_exp, k.sg_step, k.sg_w1) = sems
        segment_weights(nc, k, a)
        segments(nc, k, a)
        end_stage(nc, sems)


SEMS = ["passed", "weights_in", "ident_zero", "ident_one", "consts_set", "vrows_set", "vecs_in", "vecs_turned", "vecs_ready",
        "x_turned", "x_ready", "wt_turned", "wt_ready", "ln_centered", "ln_squared", "ln_var", "ln_logs", "ln_rstd",
        "ln_scaled", "ln_biased", "ln_out", "y_turned", "y_rows", "stored", "wA_in", "moe_w_in", "pa_prod", "pa_added",
        "ff_w_in", "ff_zero", "ff_const", "ff_spread", "ff_spread16", "ff_hot0", "ff_mix1", "ff_mix2", "ff_mix", "ff_up",
        "ff_u", "ff_h", "ff_hid", "ff_score", "ff_step", "ff_hot", "ff_hotT", "ff_hot16", "ff_spreads", "ff_masked", "ff_out",
        "ff_z", "lr_w_in", "lr_prod", "lr_read", "lr_init", "lr_sc", "lr_den", "lr_ln", "lr_rden", "lr_step", "lr_x", "tw_in",
        "tw_turned", "tw_zero", "tw_copied", "tw_prod", "tr_ys", "tr_z", "tr_th", "tr_g", "tr_step", "tr_lp", "tr_turned",
        "tr_lpT", "tr_out", "tr_x"]
MOE_SEMS = ["mix_diff", "mix_in", "kvr", "kvr_out", "wkv_w", "wkv_arg", "wkv_exp", "wkv_den", "wkv_ln", "wkv_rden", "wkv_init",
            "wkv_e2bv", "wkv_e2v", "wkv_v", "wkv_step", "rt_prod", "rt_copied", "rt_turned", "rt_parts", "rt_wT", "rt_back",
            "rt_step", "rt_exps", "rt_const", "rt_sel", "ex_diff", "ex_mix", "ex_r", "ex_v", "ex_tanh", "ex_added", "ex_gate",
            "ex_tw", "ex_weighed", "ex_up", "ex_relu", "ex_sq", "ex_y"]
FAVOR_SEMS = ["fw_in", "fw_mask", "fw_turned", "fw_wide", "fw_copied", "fw_prod", "fv_ys", "fv_proj", "fv_sq", "fv_va", "fv_max",
              "fv_off", "fv_arg", "fv_exp", "fv_phi", "fv_used", "fv_kv", "fv_ones", "fv_exT", "fv_sums", "fv_o", "fv_rd",
              "fv_back", "fv_oT", "fv_out", "fv_x"]
SEGMENT_SEMS = ["sw_in", "sw_zero", "sw_turned", "sg_took", "sg_proj", "sg_fill", "sg_arg", "sg_score", "sg_half", "sg_vc", "sg_x", "sg_vT",
                "sg_mul", "sg_pT", "sg_turned", "sg_vt", "sg_o", "sg_pv", "sg_oturn", "sg_oT", "sg_out", "sg_const", "sg_weight",
                "sg_exp", "sg_step", "sg_w1"]
PRIMED = {"ln_out": 4, "pa_added": 4, "rt_copied": 4, "kvr": 6, "kvr_out": 6,
          "ex_r": 4, "ex_relu": 2, "ex_v": 2, "ex_gate": 2, "ex_added": 2, "ex_tanh": 1, "ex_weighed": 1, "wkv_e2v": 1, "ex_sq": 1,
          "ff_h": 6, "ff_out": 1, "ff_hid": 3, "ff_masked": 6, "ff_z": 2, "lr_read": 6,
          "tr_th": 2, "tr_lpT": 1, "tr_x": 2, "tr_z": 2, "tr_g": 1, "tr_turned": 2, "tr_out": 2,
          "fv_proj": 2, "fv_sq": 2, "fv_arg": 2, "fv_used": 2, "fv_va": 2, "fv_kv": 1, "fv_exT": 1, "fv_o": 1, "fv_sums": 2,
          "fv_oT": 1, "fv_x": 1, "fv_out": 1,
          "sg_x": 1, "sg_arg": 2, "sg_pT": 2, "sg_o": 1, "sg_score": 2, "sg_vT": 1}


def load(nc, k, a):
    with nc.Block() as block:
        @block.sync
        def _(sp):
            xin = a["L0_attn_a_x"].rearrange("b l d -> (b l) d").rearrange("(p t) d -> p t d", t=NT // P)
            for q in range(4):
                sp.dma_start(k.rows[:, 8 * q:8 * q + 8, :], xin[:, 8 * q:8 * q + 8, :]).then_inc(k.loaded[q], 16)

        @block.gpsimd
        def _(pool):
            nc.gpsimd.memset(k.ident[:], 0.0).then_inc(k.ident_zero, 1)
            pool.wait_ge(k.ident_zero, 1)
            nc.gpsimd.affine_select(out=k.ident[:], in_=k.ident[:], compare_op=ALU.not_equal, fill=1.0, base=0,
                                    pattern=[[-1, P]], channel_multiplier=1).then_inc(k.ident_one, 1)
            nc.gpsimd.memset(k.mean[:], 1.0 / P).then_inc(k.consts_set, 1)
            nc.gpsimd.memset(k.eps[:], EPS_LN).then_inc(k.consts_set, 1)
            for b in range(B):
                nc.gpsimd.memset(k.N[:, b * PADL:b * PADL + 1], 0.0).then_inc(k.consts_set, 1)
                nc.gpsimd.memset(k.N[:, (b + 1) * PADL - 1:(b + 1) * PADL], 0.0).then_inc(k.consts_set, 1)

        @block.scalar
        def _(act):
            act.wait_ge(k.vrows_set, 1)
            row = lambda v: v.rearrange("(o n) -> o n", o=1)
            table = [
                ("ln1_g", row(a["L0_attn_a_ln1_g"])), ("ln1_b", row(a["L0_attn_a_ln1_b"])),
                ("ln2_g", row(a["L0_attn_a_ln2_g"])), ("ln2_b", row(a["L0_attn_a_ln2_b"])),
                ("mu_k", row(a["L0_attn_a_tm_mu_k"])), ("mu_v", row(a["L0_attn_a_tm_mu_v"])), ("mu_r", row(a["L0_attn_a_tm_mu_r"])),
                ("decay", row(a["L0_attn_a_time_decay"])), ("first", row(a["L0_attn_a_time_first"])),
                ("cm_k0", a["L0_attn_a_cm_mu_k"]), ("cm_r0", a["L0_attn_a_cm_mu_r"]),
                ("favor_bo", row(a["L0_attn_b_bo"])), ("mix0", a["L0_ffn_mix_kernel"]),
                ("gamma", row(a["L0_ffn_gamma"])), ("beta", row(a["L0_ffn_beta"])),
                ("bq", row(a["L1_attn_a_bq"])), ("bk", row(a["L1_attn_a_bk"])), ("bv", row(a["L1_attn_a_bv"])), ("bo", row(a["L1_attn_a_bo"])),
                ("br", a["L1_attn_b_b_rkv"].rearrange("(o n) -> o n", n=P)), ("lru_bo", row(a["L1_attn_b_b_o"])),
                ("nu_log", row(a["L1_attn_b_nu_log"])), ("gamma_log", row(a["L1_attn_b_gamma_log"])),
                ("wout_b", row(a["L1_ffn_Wout_b"])), ("b1_0", a["L0_ffn_b1"].rearrange("(o q) m -> o (q m)", q=3)),
                ("bo1", row(a["L0_ffn_bo1"]))]
            for name, src in table:
                n, width = src.shape
                act.dma_start(k.vrows[VI[name]:VI[name] + n, 0:width], src).then_inc(k.vecs_in, 16)
            k.n_vec_loads = len(table)

        @block.tensor
        def _(pe):
            pe.wait_ge(k.ident_one, 1)
            pe.wait_ge(k.vecs_in, 16 * k.n_vec_loads)
            nc.tensor.transpose(k.bank[7][:, 0:len(VROWS)], k.vrows[:], k.ident[0:len(VROWS), 0:len(VROWS)]).then_inc(k.vecs_turned, 1)
            for q in range(8):
                pe.wait_ge(k.loaded[q // 2], 16)
                if q >= 4:
                    pe.wait_ge(k.x_ready, q - 3)
                for t in range(4):
                    op = nc.tensor.transpose(k.bank[q % 4][:, t * P:(t + 1) * P], k.rows[:, 4 * q + t, :], k.ident[:])
                op.then_inc(k.x_turned, 1)

        @block.vector
        def _(dve):
            for name, semaphore in zip(SEMS, k.sems):
                if name in PRIMED:
                    dve.sem_inc(semaphore, PRIMED[name])
            nc.vector.memset(k.vrows[:], 1.0).then_inc(k.vrows_set, 1)
            dve.wait_ge(k.ident_one, 1)
            dve.wait_ge(k.consts_set, 1)
            nc.vector.tensor_tensor(k.center[:], k.ident[:], k.mean[:], ALU.subtract).then_inc(k.consts_set, 1)
            dve.wait_ge(k.vecs_turned, 1)
            nc.vector.tensor_copy(k.vecs[:], k.bank[7][:, 0:len(VROWS)]).then_inc(k.vecs_ready, 1)
            xv = k.X[:].rearrange("d (p t) -> d t p", t=NT // P)
            for q in range(8):
                dve.wait_ge(k.x_turned, q + 1)
                nc.vector.tensor_copy(xv[:, 4 * q:4 * q + 4, :],
                                      k.bank[q % 4][:].rearrange("d (t p) -> d t p", t=4)).then_inc(k.x_ready, 1)


def store(nc, k, out):
    with nc.Block() as block:
        @block.tensor
        def _(pe):
            xv = k.X[:].rearrange("d (p t) -> d t p", t=NT // P)
            for q in range(8):
                if q >= 4:
                    pe.wait_ge(k.y_rows, q - 3)
                for t in range(4):
                    op = nc.tensor.transpose(k.bank[q % 4][:, t * P:(t + 1) * P], xv[:, 4 * q + t, :], k.ident[:])
                op.then_inc(k.y_turned, 1)

        @block.vector
        def _(dve):
            for q in range(8):
                dve.wait_ge(k.y_turned, q + 1)
                nc.vector.tensor_copy(k.rows[:, 4 * q:4 * q + 4, :],
                                      k.bank[q % 4][:].rearrange("p (t d) -> p t d", t=4)).then_inc(k.y_rows, 1)

        @block.sync
        def _(sp):
            yout = out.rearrange("b l d -> (b l) d").rearrange("(p t) d -> p t d", t=NT // P)
            for q in range(4):
                sp.wait_ge(k.y_rows, 2 * q + 2)
                sp.dma_start(yout[:, 8 * q:8 * q + 8, :], k.rows[:, 8 * q:8 * q + 8, :]).then_inc(k.stored, 16)
            sp.wait_ge(k.stored, 4 * 16)


def build(nc, a, out):
    with ExitStack() as ctx:
        def sb(name, shape, dt=F32):
            return ctx.enter_context(nc.sbuf_tensor(name, shape, dt))

        k = Chip()
        k.sems = [ctx.enter_context(nc.semaphore(name)) for name in SEMS]
        (k.passed, k.weights_in, k.ident_zero, k.ident_one, k.consts_set, k.vrows_set, k.vecs_in, k.vecs_turned,
         k.vecs_ready, k.x_turned, k.x_ready, k.wt_turned, k.wt_ready, k.ln_centered, k.ln_squared, k.ln_var,
         k.ln_logs, k.ln_rstd, k.ln_scaled, k.ln_biased, k.ln_out, k.y_turned, k.y_rows, k.stored, k.wA_in, k.moe_w_in,
         k.pa_prod, k.pa_added, k.ff_w_in, k.ff_zero, k.ff_const, k.ff_spread, k.ff_spread16, k.ff_hot0, k.ff_mix1,
         k.ff_mix2, k.ff_mix, k.ff_up, k.ff_u, k.ff_h, k.ff_hid, k.ff_score, k.ff_step, k.ff_hot, k.ff_hotT,
         k.ff_hot16, k.ff_spreads, k.ff_masked, k.ff_out, k.ff_z, k.lr_w_in, k.lr_prod, k.lr_read, k.lr_init, k.lr_sc,
         k.lr_den, k.lr_ln, k.lr_rden, k.lr_step, k.lr_x, k.tw_in, k.tw_turned, k.tw_zero, k.tw_copied, k.tw_prod,
         k.tr_ys, k.tr_z, k.tr_th, k.tr_g, k.tr_step, k.tr_lp, k.tr_turned, k.tr_lpT, k.tr_out, k.tr_x) = k.sems
        k.loaded = [ctx.enter_context(nc.semaphore(f"loaded{q}")) for q in range(4)]
        k.bank = [ctx.enter_context(nc.psum_tensor(f"bank{i}", [P, CH], F32)) for i in range(8)]
        k.ident, k.mean, k.center, k.eps = sb("ident", [P, P]), sb("mean", [P, P]), sb("center", [P, P]), sb("eps", [P, 1])
        k.vrows, k.vecs = sb("vrows", [len(VROWS), P]), sb("vecs", [P, len(VROWS)])
        k.vec = lambda name, n=P: k.vecs[0:n, VI[name]:VI[name] + 1]
        k.X, k.Y, k.N = sb("X", [P, NT]), sb("Y", [P, NT]), sb("N", [P, B * PADL])
        k.ln_sq, k.ln_std = sb("ln_sq", [P, W, CH]), sb("ln_std", [P, W, CH])
        k.ln_scaled_0 = k.ln_biased_0 = 0
        k.arena = sb("arena", [P, 5 * NT])
        k.big = [k.arena[:, i * NT:(i + 1) * NT] for i in range(5)]
        k.rows = k.big[0].rearrange("p (t d) -> p t d", d=P)
        k.ln_calls = k.pa_calls = k.ff_calls = k.tr_calls = 0
        k.weights = sb("weights", [P, 5120])
        k.eWk = k.weights[:, 0:2048].rearrange("p (e f) -> p e f", e=E)
        k.eWv = k.weights[:, 2048:4096].rearrange("p (e h d) -> p e h d", e=E, h=2)
        k.eWr = k.weights[:, 4096:5120].rearrange("p (e g) -> p e g", e=E)
        k.wA, k.router = sb("wA", [P, 4, P]), sb("router", [P, E])
        k.diff, k.mixed = sb("diff", [P, 2, CH]), sb("mixed", [P, 2, 3, CH])
        k.wdec, k.wneg = sb("wdec", [P, 1]), sb("wneg", [P, 1])
        mixed = k.mixed[:].rearrange("p a j n -> p (a j n)")
        k.pp = k.ln_sq[:].rearrange("p a n -> p (a n)")[:, 0:L + 1]
        k.aa = k.ln_std[:].rearrange("p a n -> p (a n)")[:, 0:L + 1]
        k.bb, k.lam = mixed[:, 0:L + 1], mixed[:, L + 1:2 * L + 1]
        k.logitT = k.big[3][0:E, :]
        k.twT = k.big[4][:, 0:NT // 2].bitcast(BF16)
        view = lambda j, n=256: k.big[0][:, j * 256:j * 256 + n].rearrange("p (t e) -> p t e", e=E)
        k.rt_logit, k.rt_exp, k.rt_w, k.rt_one, k.rt_cand, k.rt_two = (view(j) for j in range(6))
        k.rt_part = k.big[0][:, 6 * 256:9 * 256].rearrange("p (t e s) -> p t e s", e=E, s=3)
        k.rt_bf = k.big[0][:, 9 * 256:9 * 256 + 128].bitcast(BF16).rearrange("p (t e) -> p t e", e=E)
        k.rt_m, k.rt_c, k.rank = sb("rt_m", [P, NT // P]), sb("rt_c", [P, NT // P]), sb("rank", [P, E])
        k.sel = sb("sel", [P, E, P], BF16)
        ffw = sb("ffw", [P, 6 * P + DM])
        k.W1 = ffw[:, 0:3 * P].rearrange("p (g n) -> p g n", g=3)
        k.W2 = ffw[:, 3 * P:6 * P].rearrange("p (g n) -> p g n", g=3)
        k.Wo1 = ffw[:, 6 * P:6 * P + DM]
        k.Wo2, k.prank = sb("Wo2", [DM + 1, NP]), sb("prank", [P, NP])
        k.spread = k.big[4][:, 0:3 * P].rearrange("p (g n) -> p g n", g=3)
        k.spread16 = sb("spread16", [P, 3, P], BF16)
        k.lruw = k.weights[:, 0:4 * P]
        k.gates = k.weights[:, 4 * P:6 * P]
        k.leaves = k.weights[:, 6 * P:8 * P].rearrange("p (h d) -> p h d", h=2)
        k.lr_nu, k.lr_lam, k.lr_own, k.lr_nbr = (sb(n, [P, 1]) for n in ("lr_nu", "lr_lam", "lr_own", "lr_nbr"))
        k.fv_wT = k.weights[:, 0:4 * P]
        k.fv_feat = k.weights[:, 4 * P:12 * P].rearrange("p (j n) -> p j n", j=2)
        k.fv_own, k.eps6 = k.weights[:, 12 * P:12 * P + 4], sb("eps6", [P, 1])
        k.sg_w = k.weights[:, 0:4 * P].rearrange("p (j n) -> p j n", j=4)
        k.sg_wide = k.weights[:, 4 * P:12 * P].rearrange("p (j g n) -> p j g n", j=2, g=4)
        k.sg_bias = k.weights[:, 12 * P:12 * P + 8]
        k.vb = k.diff[:].rearrange("p a n -> p (a n)")

        def ln(src, dst, **kw):
            layernorm(nc, k, k.ln_calls, src, dst, **kw)
            k.ln_calls += 1

        k.ln = ln
        X, Y = (lambda it, c: plain(k.X, it, c)), (lambda it, c: plain(k.Y, it, c))
        load(nc, k, a)
        for st in STAGES:
            STAGE[st](nc, k, a, X, Y)
        store(nc, k, out)


STAGE = {"A": stage_rwkv, "B": stage_ffn, "C": stage_favor, "D": stage_ffn, "E": stage_segments, "F": stage_tree, "G": stage_lru, "H": stage_tree}
_OUTS = [((4, 1024, 128), 'float32')]


def kernel(**inputs):
    import numpy as _np
    import concourse.bacc as _bacc
    from concourse import mybir as _mybir
    from concourse.bass_utils import run_bass_kernel_spmd as _run

    nc = _bacc.Bacc("TRN2", target_bir_lowering=False, num_devices=1)
    arrays, args = {}, {}
    for name in inputs:
        a = _np.ascontiguousarray(inputs[name])
        arrays[f"in_{name}_dram"] = a
        args[name] = nc.dram_tensor(f"in_{name}_dram", a.shape, _mybir.dt.from_np(a.dtype), kind="ExternalInput").ap()
    outs = []
    for i, (shape, dtype) in enumerate(_OUTS):
        dt = _mybir.dt.from_np(_np.dtype(dtype))
        outs.append(nc.dram_tensor(f"out_{i}_dram", shape, dt, kind="ExternalOutput").ap())
    build(nc, args, outs[0])
    r = _run(nc, [arrays], core_ids=[0])
    return r.results[0]["out_0_dram"]
```

```python
from contextlib import ExitStack

import concourse.bass as bass
from concourse import mybir

STAGES = "ABCDEFGH"
ALU = mybir.AluOpType
ACT = mybir.ActivationFunctionType
F32 = mybir.dt.float32
BF16 = mybir.dt.bfloat16
AX = mybir.AxisListType

P = 128
B, L = 4, 1024
NT = B * L
CH = 512
NCH = NT // CH
W = 4
PADL = L + 2
E = 8
NP = 9
DM = 32
EPS_LN = 1e-5

VROWS = ["ln1_g", "ln1_b", "ln2_g", "ln2_b", "mu_k", "mu_v", "mu_r", "decay", "first"] \
    + [f"cm_k{e}" for e in range(E)] + [f"cm_r{e}" for e in range(E)] \
    + ["favor_bo", "mix0", "mix1", "mix2", "gamma", "beta", "bq", "bk", "bv", "bo", "br", "bkk", "bvv", "lru_bo",
       "nu_log", "gamma_log", "wout_b", "b1_0", "b1_1", "b1_2", "bo1"]
VI = {n: i for i, n in enumerate(VROWS)}


def wait_apart(eng, k, semaphore, value):
    eng.wait_ge(semaphore, value)
    eng.sem_inc(k.passed, 1)


class Chip:
    pass


def begin_stage(nc, ctx, names):
    sems = [ctx.enter_context(nc.semaphore(name)) for name in names]
    with nc.Block() as block:
        @block.vector
        def _(dve):
            for name, semaphore in zip(names, sems):
                if name in PRIMED:
                    dve.sem_inc(semaphore, PRIMED[name])
    return sems


def end_stage(nc, sems):
    with nc.Block() as block:
        @block.vector
        def _(dve):
            for semaphore in sems:
                dve.sem_clear(semaphore)


def plain(buf, it, c):
    return buf[:, bass.ds(it * (W * CH) + c * CH, CH)]


def padded(buf, it, c, shift=0):
    return buf[:, bass.ds(it * (W // 2 * PADL) + (c // 2) * PADL + 1 + (c % 2) * CH + shift, CH)]


def layernorm(nc, k, call, src, dst, gain=None, bias=None, residual=None):
    n0 = call * NCH
    with nc.Block() as block:
        @block.tensor
        def _(pe):
            with pe.Fori(0, NCH // W) as it:
                g = it * W + n0
                for c in range(W + 2):
                    if c < W:
                        pe.wait_ge(k.ln_out, g + (c + 1))
                        nc.tensor.matmul(k.bank[c][:], k.center[:], src(it, c), start=True, stop=True).then_inc(k.ln_centered, 1)
                    if c >= 2:
                        pe.wait_ge(k.ln_squared, g + (c - 1))
                        nc.tensor.matmul(k.bank[2 + c][:], k.mean[:], k.ln_sq[:, c - 2, :], start=True, stop=True).then_inc(k.ln_var, 1)

        @block.scalar
        def _(act):
            act.preload_act_table_set("natural_log_exp_and_others")
            with act.Fori(0, NCH // W) as it:
                g = it * W + n0
                def square(c):
                    act.wait_ge(k.ln_centered, g + (c + 1))
                    nc.scalar.activation(k.ln_sq[:, c, :], k.bank[c][:], ACT.Square).then_inc(k.ln_squared, 1)

                square(0)
                square(1)
                for c in range(W):
                    if c + 2 < W:
                        square(c + 2)
                    act.wait_ge(k.ln_var, g + (c + 1))
                    nc.scalar.activation(k.ln_std[:, c, :], k.bank[4 + c][:], ACT.Ln, bias=k.eps[:, 0:1]).then_inc(k.ln_logs, 1)
                    act.wait_ge(k.ln_logs, g + (c + 1))
                    nc.scalar.activation(k.ln_std[:, c, :], k.ln_std[:, c, :], ACT.Exp, scale=-0.5).then_inc(k.ln_rstd, 1)

        @block.vector
        def _(dve):
            with dve.Fori(0, NCH // W) as it:
                g = it * W + n0
                for c in range(W):
                    dve.wait_ge(k.ln_rstd, g + (c + 1))
                    out = dst(it, c) if residual is None else k.ln_sq[:, c, :]
                    op = nc.vector.tensor_tensor(out, k.bank[c][:], k.ln_std[:, c, :], ALU.mult)
                    if gain is not None:
                        op.then_inc(k.ln_scaled, 1)
                        dve.wait_ge(k.ln_scaled, (it * W + k.ln_scaled_0) + (c + 1))
                        op = nc.vector.tensor_scalar(out, out, k.vec(gain), k.vec(bias), ALU.mult, ALU.add)
                    if residual is not None:
                        op.then_inc(k.ln_biased, 1)
                        dve.wait_ge(k.ln_biased, (it * W + k.ln_biased_0) + (c + 1))
                        op = nc.vector.tensor_tensor(residual(it, c), residual(it, c), out, ALU.add)
                    op.then_inc(k.ln_out, 1)
    if gain is not None:
        k.ln_scaled_0 += NCH
    if residual is not None:
        k.ln_biased_0 += NCH


def rwkv_mix(nc, k, a):
    Wk, Wv, Wr, Wo = (k.wA[:, j, :] for j in range(4))
    K, V, R = k.big[0], k.big[1], k.big[2]
    with nc.Block() as block:
        @block.sync
        def _(sp):
            for j, w in enumerate((a["L0_attn_a_Wk"], a["L0_attn_a_Wv"], a["L0_attn_a_Wr"], a["L0_attn_a_Wo"])):
                sp.dma_start(k.wA[:, j, :], w).then_inc(k.wA_in, 16)
            sp.dma_start(k.router[:], a["L0_attn_a_router_w"]).then_inc(k.moe_w_in, 16)
            sp.dma_start(k.eWk[:], a["L0_attn_a_eWk"].rearrange("e d f -> d e f")).then_inc(k.moe_w_in, 16)
            sp.dma_start(k.eWv[:], a["L0_attn_a_eWv"].rearrange("e (h f) d -> f e h d", h=2)).then_inc(k.moe_w_in, 16)
            sp.dma_start(k.eWr[:], a["L0_attn_a_eWr"].rearrange("e d g -> d e g")).then_inc(k.moe_w_in, 16)

        @block.vector
        def _(dve):
            with dve.Fori(0, NCH // 2) as it:
                for c in range(2):
                    g = it * 2 + c
                    now = k.N[:, bass.ds(it * PADL + 1 + c * CH, CH)]
                    before = k.N[:, bass.ds(it * PADL + c * CH, CH)]
                    dve.wait_ge(k.kvr, g * 3 + 3)
                    nc.vector.tensor_tensor(k.diff[:, c, :], now, before, ALU.subtract).then_inc(k.mix_diff, 1)
                    dve.wait_ge(k.mix_diff, g + 1)
                    for j, mu in enumerate(("mu_k", "mu_v", "mu_r")):
                        nc.vector.scalar_tensor_tensor(k.mixed[:, c, j, :], k.diff[:, c, :], k.vec(mu), before,
                                                       ALU.mult, ALU.add).then_inc(k.mix_in, 1)

        @block.tensor
        def _(pe):
            pe.wait_ge(k.wA_in, 64)
            with pe.Fori(0, NCH // 2) as it:
                for c in range(2):
                    g = it * 2 + c
                    for j, w in enumerate((Wk, Wv, Wr)):
                        pe.wait_ge(k.mix_in, g * 3 + (j + 1))
                        pe.wait_ge(k.kvr_out, g * 3 + (j + 1))
                        op = nc.tensor.matmul(k.bank[3 * c + j][:], w, k.mixed[:, c, j, :], start=True, stop=True)
                        op.then_inc(k.kvr, 1)

        @block.scalar
        def _(act):
            with act.Fori(0, NCH // 2) as it:
                for c in range(2):
                    at = bass.ds(it * L + c * CH, CH)
                    for j in range(3):
                        act.wait_ge(k.kvr, it * 6 + (c * 3 + j + 1 + PRIMED["kvr"]))
                        dst = (K, V, R)[j]
                        nc.scalar.activation(dst[:, at], k.bank[3 * c + j][:], (ACT.Copy, ACT.Copy, ACT.Tanh)[j],
                                             scale=(1.0, 1.0, 0.5)[j]).then_inc(k.kvr_out, 1)


def wkv(nc, k, a):
    K, V, R = k.big[0], k.big[1], k.big[2]
    T = k.big[3]
    U = k.big[4]
    pp, aa, bb = k.pp, k.aa, k.bb
    t = [T[:, j * L:(j + 1) * L] for j in range(4)]
    u = [U[:, j * L:(j + 1) * L] for j in range(4)]
    with nc.Block() as block:
        @block.scalar
        def _(act):
            nc.scalar.activation(k.wdec[:], k.vec("decay"), ACT.Exp).then_inc(k.wkv_w, 1)
            with act.Fori(0, B) as b:
                act.wait_ge(k.wkv_e2v, b + 1)
                nc.scalar.activation(k.vb, V[:, bass.ds(b * L, L)], ACT.Copy).then_inc(k.wkv_v, 1)
                for j in range(4):
                    act.wait_ge(k.wkv_arg, b * 4 + (j + 1))
                    nc.scalar.activation(t[j], t[j], ACT.Exp).then_inc(k.wkv_exp, 1)
                act.wait_ge(k.wkv_den, b + 1)
                nc.scalar.activation(u[3], u[2], ACT.Ln).then_inc(k.wkv_ln, 1)
                act.wait_ge(k.wkv_ln, b + 1)
                nc.scalar.activation(u[3], u[3], ACT.Exp, scale=-1.0).then_inc(k.wkv_rden, 1)

        @block.gpsimd
        def _(pool):
            nc.gpsimd.memset(pp[:, 0:1], -1e30).then_inc(k.wkv_init, 1)
            nc.gpsimd.memset(aa[:, 0:1], 0.0).then_inc(k.wkv_init, 1)
            nc.gpsimd.memset(bb[:, 0:1], 0.0).then_inc(k.wkv_init, 1)
            with pool.Fori(0, B) as b:
                pool.wait_ge(k.wkv_v, b + 1)
                pool.wait_ge(k.wkv_exp, b * 4 + 2)
                nc.gpsimd.tensor_tensor(u[0], t[1], k.vb, ALU.mult).then_inc(k.wkv_e2bv, 1)
                pool.wait_ge(k.wkv_exp, b * 4 + 4)
                nc.gpsimd.tensor_tensor(u[1], t[3], k.vb, ALU.mult).then_inc(k.wkv_e2v, 1)

        @block.vector
        def _(dve):
            dve.wait_ge(k.wkv_w, 1)
            nc.vector.tensor_scalar(k.wneg[:], k.wdec[:], -1.0, None, ALU.mult).then_inc(k.wkv_step, 1)
            dve.wait_ge(k.wkv_step, 1)
            nc.vector.tensor_copy(k.lam, k.wneg[:, 0:1].to_broadcast([P, L])).then_inc(k.wkv_step, 1)
            dve.wait_ge(k.wkv_step, 2)
            dve.wait_ge(k.wkv_init, 3)
            with dve.Fori(0, B) as b:
                at = bass.ds(b * L, L)
                s = b * 9 + 2
                nc.vector.tensor_tensor_scan(pp[:, 1:L + 1], k.lam, K[:, at], -1e30, ALU.add, ALU.max).then_inc(k.wkv_step, 1)
                dve.wait_ge(k.wkv_step, s + 1)
                nc.vector.scalar_tensor_tensor(t[0], pp[:, 0:L], k.wneg[:, 0:1], pp[:, 1:L + 1], ALU.add, ALU.subtract).then_inc(k.wkv_arg, 1)
                nc.vector.tensor_tensor(t[1], K[:, at], pp[:, 1:L + 1], ALU.subtract).then_inc(k.wkv_arg, 1)
                nc.vector.scalar_tensor_tensor(u[2], K[:, at], k.vec("first"), pp[:, 0:L], ALU.add, ALU.max).then_inc(k.wkv_step, 1)
                dve.wait_ge(k.wkv_step, s + 2)
                nc.vector.tensor_tensor(t[2], pp[:, 0:L], u[2], ALU.subtract).then_inc(k.wkv_arg, 1)
                nc.vector.scalar_tensor_tensor(t[3], K[:, at], k.vec("first"), u[2], ALU.add, ALU.subtract).then_inc(k.wkv_arg, 1)
                dve.wait_ge(k.wkv_exp, b * 4 + 2)
                nc.vector.tensor_tensor_scan(bb[:, 1:L + 1], t[0], t[1], 0.0, ALU.mult, ALU.add).then_inc(k.wkv_step, 1)
                dve.wait_ge(k.wkv_e2bv, b + 1)
                nc.vector.tensor_tensor_scan(aa[:, 1:L + 1], t[0], u[0], 0.0, ALU.mult, ALU.add).then_inc(k.wkv_step, 1)
                dve.wait_ge(k.wkv_step, s + 3)
                dve.wait_ge(k.wkv_exp, b * 4 + 4)
                nc.vector.tensor_tensor(u[2], t[2], bb[:, 0:L], ALU.mult).then_inc(k.wkv_step, 1)
                dve.wait_ge(k.wkv_step, s + 5)
                nc.vector.tensor_tensor(u[2], u[2], t[3], ALU.add).then_inc(k.wkv_den, 1)
                nc.vector.tensor_tensor(u[0], t[2], aa[:, 0:L], ALU.mult).then_inc(k.wkv_step, 1)
                dve.wait_ge(k.wkv_e2v, b + 2)
                dve.wait_ge(k.wkv_step, s + 6)
                nc.vector.tensor_tensor(u[1], u[0], u[1], ALU.add).then_inc(k.wkv_step, 1)
                dve.wait_ge(k.wkv_step, s + 7)
                nc.vector.scalar_tensor_tensor(u[1], R[:, at], 1.0, u[1], ALU.add, ALU.mult).then_inc(k.wkv_step, 1)
                dve.wait_ge(k.wkv_step, s + 8)
                dve.wait_ge(k.wkv_rden, b + 1)
                nc.vector.scalar_tensor_tensor(R[:, at], u[1], 0.5, u[3], ALU.mult, ALU.mult).then_inc(k.wkv_step, 1)
                dve.wait_ge(k.wkv_step, s + 9)


def project_add(nc, k, call, lhsT, src, dst, bias=None):
    n0 = call * NCH
    with nc.Block() as block:
        @block.tensor
        def _(pe):
            with pe.Fori(0, NCH // W) as it:
                for c in range(W):
                    pe.wait_ge(k.pa_added, it * W + (n0 + c + 1))
                    nc.tensor.matmul(k.bank[c][:], lhsT, src(it, c), start=True, stop=True).then_inc(k.pa_prod, 1)

        @block.vector
        def _(dve):
            with dve.Fori(0, NCH // W) as it:
                for c in range(W):
                    dve.wait_ge(k.pa_prod, it * W + (n0 + c + 1))
                    if bias is None:
                        nc.vector.tensor_tensor(dst(it, c), dst(it, c), k.bank[c][:], ALU.add).then_inc(k.pa_added, 1)
                    else:
                        nc.vector.scalar_tensor_tensor(dst(it, c), k.bank[c][:], bias, dst(it, c), ALU.add, ALU.add).then_inc(k.pa_added, 1)


def route(nc, k, a):
    NTI = NT // P
    lg, ex, wt = k.rt_logit, k.rt_exp, k.rt_w
    one, cand, two = k.rt_one, k.rt_cand, k.rt_two
    col = lambda t: t[:, :, None].to_broadcast([P, NTI, E])
    with nc.Block() as block:
        @block.tensor
        def _(pe):
            pe.wait_ge(k.moe_w_in, 64)
            with pe.Fori(0, NCH // W) as it:
                for c in range(W):
                    pe.wait_ge(k.rt_copied, it * W + (c + 1))
                    nc.tensor.matmul(k.bank[c][0:E, :], k.router[:], padded(k.N, it, c), start=True, stop=True).then_inc(k.rt_prod, 1)
            pe.wait_ge(k.rt_copied, NCH + PRIMED["rt_copied"])
            for t in range(NTI):
                op = nc.tensor.transpose(k.bank[4][:, t * E:(t + 1) * E], k.logitT[:, t * P:(t + 1) * P], k.ident[0:E, 0:E])
            op.then_inc(k.rt_turned, 1)
            pe.wait_ge(k.rt_parts, 3)
            for t in range(NTI):
                if t % 4 == 0 and t >= 16:
                    pe.wait_ge(k.rt_wT, t // 4 - 3)
                op = nc.tensor.transpose(k.bank[t // 4 % 4][0:3 * E, (t % 4) * P:(t % 4 + 1) * P],
                                         k.rt_part[:, t, :, :].rearrange("p e s -> p (e s)"), k.ident[:])
                if t % 4 == 3:
                    op.then_inc(k.rt_back, 1)

        @block.scalar
        def _(act):
            with act.Fori(0, NCH // W) as it:
                for c in range(W):
                    act.wait_ge(k.rt_prod, it * W + (c + 1))
                    nc.scalar.activation(k.logitT[:, bass.ds(it * W * CH + c * CH, CH)], k.bank[c][0:E, :], ACT.Copy).then_inc(k.rt_copied, 1)
            act.wait_ge(k.rt_step, 2)
            nc.scalar.activation(ex, ex, ACT.Exp).then_inc(k.rt_exps, 1)
            act.wait_ge(k.rt_sel, 4)
            for q in range(8):
                act.wait_ge(k.rt_back, q + 1)
                nc.scalar.activation(k.twT[0:3 * E, q * CH:(q + 1) * CH], k.bank[q % 4][0:3 * E, :], ACT.Copy).then_inc(k.rt_wT, 1)

        @block.gpsimd
        def _(pool):
            for e in range(E):
                nc.gpsimd.memset(k.rank[:, e:e + 1], float(E - e)).then_inc(k.rt_const, 1)
            nc.gpsimd.memset(k.twT, 0.0).then_inc(k.rt_sel, 1)
            nc.gpsimd.memset(k.sel[:], 1.0).then_inc(k.rt_sel, 1)
            pool.wait_ge(k.rt_sel, 2)
            nc.gpsimd.affine_select(out=k.sel[:], in_=k.sel[:], compare_op=ALU.is_ge, fill=0.0, base=0,
                                    pattern=[[-3, E], [0, P]], channel_multiplier=1).then_inc(k.rt_sel, 1)
            pool.wait_ge(k.rt_sel, 3)
            nc.gpsimd.affine_select(out=k.sel[:], in_=k.sel[:], compare_op=ALU.is_ge, fill=0.0, base=2,
                                    pattern=[[3, E], [0, P]], channel_multiplier=-1).then_inc(k.rt_sel, 1)

        @block.vector
        def _(dve):
            rank = k.rank[:, None, :].to_broadcast([P, NTI, E])
            step = [0]

            def then(op):
                step[0] += 1
                op.then_inc(k.rt_step, 1)
                dve.wait_ge(k.rt_step, step[0])

            dve.wait_ge(k.rt_const, E)
            dve.wait_ge(k.rt_turned, 1)
            logits = k.bank[4][:, 0:NTI * E].rearrange("p (t e) -> p t e", e=E)
            then(nc.vector.tensor_reduce(k.rt_m[:], logits, AX.X, ALU.max))
            then(nc.vector.tensor_tensor(ex, logits, col(k.rt_m[:]), ALU.subtract))
            dve.wait_ge(k.rt_exps, 1)
            then(nc.vector.tensor_reduce(k.rt_m[:], ex, AX.X, ALU.max))
            then(nc.vector.tensor_tensor(cand, ex, col(k.rt_m[:]), ALU.is_equal))
            then(nc.vector.tensor_tensor(cand, cand, rank, ALU.mult))
            then(nc.vector.tensor_reduce(k.rt_c[:], cand, AX.X, ALU.max))
            then(nc.vector.tensor_tensor(one, rank, col(k.rt_c[:]), ALU.is_equal))
            then(nc.vector.tensor_tensor(lg, ex, one, ALU.subtract))
            then(nc.vector.scalar_tensor_tensor(lg, one, -2.0, lg, ALU.mult, ALU.add))
            then(nc.vector.tensor_reduce(k.rt_m[:], lg, AX.X, ALU.max))
            then(nc.vector.tensor_tensor(cand, lg, col(k.rt_m[:]), ALU.is_equal))
            then(nc.vector.tensor_tensor(cand, cand, rank, ALU.mult))
            then(nc.vector.tensor_reduce(k.rt_c[:], cand, AX.X, ALU.max))
            then(nc.vector.tensor_tensor(two, rank, col(k.rt_c[:]), ALU.is_equal))
            then(nc.vector.tensor_tensor(one, one, two, ALU.add))
            then(nc.vector.tensor_tensor(wt, ex, one, ALU.mult))
            then(nc.vector.tensor_reduce(k.rt_m[:], wt, AX.X, ALU.add))
            then(nc.vector.reciprocal(k.rt_m[:], k.rt_m[:]))
            then(nc.vector.tensor_scalar(k.rt_m[:], k.rt_m[:], 0.5, None, ALU.mult))
            then(nc.vector.tensor_tensor(wt, wt, col(k.rt_m[:]), ALU.mult))
            for s in range(3):
                then(nc.vector.tensor_copy(k.rt_bf, wt))
                op = nc.vector.tensor_copy(k.rt_part[:, :, :, s], k.rt_bf)
                op.then_inc(k.rt_parts, 1)
                if s < 2:
                    then(nc.vector.tensor_tensor(wt, wt, k.rt_bf, ALU.subtract))


def experts(nc, k, a):
    UNITS = 2 * E
    kr, ks, er, o = k.big[0][:, 0:2 * CH], k.big[0][:, 2 * CH:6 * CH], k.big[1][:, 0:2 * CH], k.big[1][:, 2 * CH:4 * CH]

    mixed = k.big[3].rearrange("p (s a n) -> p s a n", s=4, a=2)
    acc = k.big[1][:, 4 * CH:6 * CH].rearrange("p (c n) -> p c n", c=2)

    def done(s, n):
        return n + (1 + PRIMED.get(s, 0))

    with nc.Block() as block:
        @block.vector
        def _(dve):
            def begin(it, c):
                nc.vector.tensor_copy(acc[:, c, :], k.Y[:, bass.ds(it * L + c * CH, CH)]).then_inc(k.ex_y, 1)
                now = k.N[:, bass.ds(it * PADL + 1 + c * CH, CH)]
                before = k.N[:, bass.ds(it * PADL + c * CH, CH)]
                nc.vector.tensor_tensor(k.diff[:, c, :], now, before, ALU.subtract).then_inc(k.ex_diff, 1)
                dve.wait_ge(k.ex_diff, it * 2 + (c + 1))

            def mix(it, j):
                n, c, e = it * UNITS + j, j // E, j % E
                if e == 0:
                    begin(it, c)
                before = k.N[:, bass.ds(it * PADL + c * CH, CH)]
                dve.wait_ge(k.ex_r, n + 1)
                nc.vector.scalar_tensor_tensor(mixed[:, j % 4, 0, :], k.diff[:, c, :], k.vec(f"cm_k{e}"), before, ALU.mult, ALU.add)
                nc.vector.scalar_tensor_tensor(mixed[:, j % 4, 1, :], k.diff[:, c, :], k.vec(f"cm_r{e}"), before, ALU.mult, ALU.add).then_inc(k.ex_mix, 1)

            def gate(it, j):
                n, oj = it * UNITS + j, o[:, (j % 2) * CH:(j % 2 + 1) * CH]
                dve.wait_ge(k.ex_v, done("ex_v", n))
                dve.wait_ge(k.ex_tanh, done("ex_tanh", n))
                dve.wait_ge(k.ex_added, n + 1)
                nc.vector.scalar_tensor_tensor(oj, er[:, (j % 2) * CH:(j % 2 + 1) * CH], 1.0, k.bank[4 + j % 2][:], ALU.add, ALU.mult).then_inc(k.ex_gate, 1)
                dve.wait_ge(k.ex_gate, done("ex_gate", n))
                dve.wait_ge(k.ex_tw, done("ex_tw", n))
                nc.vector.tensor_tensor(oj, oj, k.bank[7][:], ALU.mult).then_inc(k.ex_weighed, 1)

            def finish(it, c):
                at = bass.ds(it * L + c * CH, CH)
                dve.wait_ge(k.ex_added, done("ex_added", it * UNITS + (c + 1) * E - 1))
                nc.vector.tensor_tensor(k.X[:, at], k.X[:, at], acc[:, c, :], ALU.add)

            def turn(it, last):
                for j in range(UNITS):
                    gate(it, j)
                    if j + 3 < UNITS:
                        mix(it, j + 3)
                    elif not last:
                        mix(it + 1, j + 3 - UNITS)
                    if j == E:
                        finish(it, 0)
                finish(it, 1)

            for j in range(3):
                mix(0, j)
            with dve.Fori(0, B - 1) as it:
                turn(it, False)
            turn(B - 1, True)

        @block.tensor
        def _(pe):
            def up(it, j):
                n, e = it * UNITS + j, j % E
                pe.wait_ge(k.ex_mix, done("ex_mix", n))
                pe.wait_ge(k.ex_relu, n + 1)
                for h in range(2):
                    op = nc.tensor.matmul(k.bank[2 * (j % 2) + h][:], k.eWk[:, e, h * P:(h + 1) * P], mixed[:, j % 4, 0, :], start=True, stop=True)
                op.then_inc(k.ex_up, 1)
                pe.wait_ge(k.ex_tanh, n + 1)
                nc.tensor.matmul(k.bank[6][:], k.eWr[:, e, :], mixed[:, j % 4, 1, :], start=True, stop=True).then_inc(k.ex_r, 1)

            def turn(it, last):
                for j in range(UNITS):
                    n, c, e = it * UNITS + j, j // E, j % E
                    if j + 1 < UNITS:
                        up(it, j + 1)
                    elif not last:
                        up(it + 1, 0)
                    pe.wait_ge(k.ex_sq, done("ex_sq", n))
                    pe.wait_ge(k.ex_gate, n + 1)
                    for h in range(2):
                        op = nc.tensor.matmul(k.bank[4 + j % 2][:], k.eWv[:, e, h, :], ks[:, (2 * (j % 2) + h) * CH:(2 * (j % 2) + h + 1) * CH], start=(h == 0), stop=(h == 1))
                    op.then_inc(k.ex_v, 1)
                    pe.wait_ge(k.ex_weighed, n + 1)
                    nc.tensor.matmul(k.bank[7][:], k.sel[:, e, :], k.twT[:, bass.ds(it * L + c * CH, CH)], start=True, stop=True).then_inc(k.ex_tw, 1)

            up(0, 0)
            with pe.Fori(0, B - 1) as it:
                turn(it, False)
            turn(B - 1, True)

        @block.scalar
        def _(act):
            with act.Fori(0, B) as it:
                for j in range(UNITS):
                    n = it * UNITS + j
                    act.wait_ge(k.ex_up, done("ex_up", n))
                    act.wait_ge(k.ex_sq, n + 1)
                    for h in range(2):
                        op = nc.scalar.activation(kr[:, h * CH:(h + 1) * CH], k.bank[2 * (j % 2) + h][:], ACT.Relu)
                    op.then_inc(k.ex_relu, 1)
                    act.wait_ge(k.ex_r, done("ex_r", n))
                    act.wait_ge(k.ex_gate, n + 1)
                    nc.scalar.activation(er[:, (j % 2) * CH:(j % 2 + 1) * CH], k.bank[6][:], ACT.Tanh, scale=0.5).then_inc(k.ex_tanh, 1)
                    act.wait_ge(k.ex_relu, done("ex_relu", n))
                    act.wait_ge(k.ex_v, n + 1)
                    nc.scalar.activation(ks[:, (j % 2) * 2 * CH:(j % 2 + 1) * 2 * CH], kr, ACT.Square).then_inc(k.ex_sq, 1)

        @block.gpsimd
        def _(pool):
            with pool.Fori(0, B) as it:
                for j in range(UNITS):
                    n, c, e = it * UNITS + j, j // E, j % E
                    oj = o[:, (j % 2) * CH:(j % 2 + 1) * CH]
                    pool.wait_ge(k.ex_weighed, done("ex_weighed", n))
                    if e == 0:
                        pool.wait_ge(k.ex_y, it * 2 + (c + 1))
                    pool.wait_ge(k.ex_added, n + 2)
                    nc.gpsimd.tensor_tensor(acc[:, c, :], acc[:, c, :], oj, ALU.add).then_inc(k.ex_added, 1)


def stage_rwkv(nc, k, a, X, Y):
    N = lambda it, c: padded(k.N, it, c)
    with ExitStack() as ctx:
        sems = begin_stage(nc, ctx, MOE_SEMS)
        (k.mix_diff, k.mix_in, k.kvr, k.kvr_out, k.wkv_w, k.wkv_arg, k.wkv_exp, k.wkv_den, k.wkv_ln, k.wkv_rden,
         k.wkv_init, k.wkv_e2bv, k.wkv_e2v, k.wkv_v, k.wkv_step, k.rt_prod, k.rt_copied, k.rt_turned, k.rt_parts,
         k.rt_wT, k.rt_back, k.rt_step, k.rt_exps, k.rt_const, k.rt_sel, k.ex_diff, k.ex_mix, k.ex_r, k.ex_v,
         k.ex_tanh, k.ex_added, k.ex_gate, k.ex_tw, k.ex_weighed, k.ex_up, k.ex_relu, k.ex_sq, k.ex_y) = sems
        k.ln(X, Y)
        k.ln(Y, N, gain="ln1_g", bias="ln1_b")
        rwkv_mix(nc, k, a)
        wkv(nc, k, a)
        project_add(nc, k, k.pa_calls, k.wA[:, 3, :], lambda it, c: plain(k.big[2], it, c), Y)
        k.pa_calls += 1
        k.ln(Y, N, gain="ln2_g", bias="ln2_b")
        route(nc, k, a)
        experts(nc, k, a)
        end_stage(nc, sems)


def feedforward(nc, k, a, call):
    GR, GW = 3, 3 * DM
    TI = CH // P
    Z = k.big[1]
    base = call * NCH
    own = (k.bank[5], k.bank[3])
    masks = (k.bank[6], k.bank[7], k.bank[4])
    xm = [k.big[0][:, c * CH:(c + 1) * CH] for c in range(2)]
    hid = [k.big[0][:, (2 + 3 * c) * CH:(5 + 3 * c) * CH] for c in range(2)]
    hm = k.big[3][:, 0:3 * CH]
    u = [k.big[2][0:DM + 1, c * CH:(c + 1) * CH] for c in range(2)]
    sc = [k.big[2][:, (2 + c) * CH:(3 + c) * CH] for c in range(2)]
    cand, hot = ([sc[c][:, j * 64:j * 64 + TI * NP].rearrange("p (t e) -> p t e", e=NP) for c in range(2)] for j in range(2))
    top = [sc[c][:, 192:192 + TI] for c in range(2)]
    hotT = [k.big[2][:, 4 * CH + c * 256:4 * CH + (c + 1) * 256].bitcast(BF16) for c in range(2)]
    with nc.Block() as block:
        @block.sync
        def _(sp):
            if call == 0:
                for p in range(NP):
                    sp.dma_start(k.W1[:, p // 3, (p % 3) * DM:(p % 3 + 1) * DM], a["L0_ffn_W1"][p]).then_inc(k.ff_w_in, 16)
                sp.dma_start(k.Wo1, a["L0_ffn_Wo1"]).then_inc(k.ff_w_in, 16)
                sp.wait_ge(k.ff_zero, 1)
                sp.dma_start(k.W2[0:GW, :, :], a["L0_ffn_W2"].rearrange("(g q) m d -> (q m) g d", g=GR)).then_inc(k.ff_w_in, 16)
                sp.dma_start(k.W2[GW:GW + NP, 0, :], a["L0_ffn_b2"]).then_inc(k.ff_w_in, 16)
                sp.dma_start(k.Wo2[0:DM, :], a["L0_ffn_Wo2"]).then_inc(k.ff_w_in, 16)
                sp.dma_start(k.Wo2[DM:DM + 1, :], a["L0_ffn_bo2"].rearrange("(o n) -> o n", o=1)).then_inc(k.ff_w_in, 16)

        @block.gpsimd
        def _(pool):
            if call == 0:
                nc.gpsimd.memset(k.W1[:, :, GW:P], 0.0).then_inc(k.ff_const, 1)
                for p in range(NP):
                    nc.gpsimd.memset(k.prank[:, p:p + 1], float(NP - p)).then_inc(k.ff_const, 1)
                nc.gpsimd.memset(k.spread, 0.0).then_inc(k.ff_spread, 1)
                pool.wait_ge(k.ff_spread, 1)
                sv = k.spread[:, :, 0:GW].rearrange("p g (q m) -> p g q m", m=DM)
                nc.gpsimd.affine_select(out=sv, in_=sv, compare_op=ALU.not_equal, fill=1.0, base=0,
                                        pattern=[[-3, GR], [-1, 3], [0, DM]], channel_multiplier=1).then_inc(k.ff_spread, 1)
                so = k.spread[:, 0, GW:P]
                nc.gpsimd.affine_select(out=so, in_=so, compare_op=ALU.not_equal, fill=1.0, base=0,
                                        pattern=[[-1, P - GW]], channel_multiplier=1).then_inc(k.ff_spread, 1)
            for c in range(2):
                nc.gpsimd.memset(hotT[c], 0.0).then_inc(k.ff_hot0, 1)

        @block.vector
        def _(dve):
            for c in range(2):
                nc.vector.memset(u[c][DM:DM + 1, :], 1.0).then_inc(k.ff_hot0, 1)
            if call == 0:
                nc.vector.memset(k.W2[:, 0, :], 0.0).then_inc(k.ff_zero, 1)
                dve.wait_ge(k.ff_const, 1 + NP)
                dve.wait_ge(k.ff_spread, 3)
                nc.vector.tensor_copy(k.spread16[:], k.spread).then_inc(k.ff_spread16, 1)
            def mix(it, c):
                g = it * 2 + (base + c)
                n = lambda s: k.N[:, bass.ds(it * PADL + 1 + c * CH + s, CH)]
                dve.wait_ge(k.ff_h, g * 3 + 3)
                nc.vector.tensor_scalar(xm[c], n(-1), k.vec("mix0"), None, ALU.mult).then_inc(k.ff_mix1, 1)
                dve.wait_ge(k.ff_mix1, g + 1)
                nc.vector.scalar_tensor_tensor(xm[c], n(0), k.vec("mix1"), xm[c], ALU.mult, ALU.add).then_inc(k.ff_mix2, 1)
                dve.wait_ge(k.ff_mix2, g + 1)
                nc.vector.scalar_tensor_tensor(xm[c], n(1), k.vec("mix2"), xm[c], ALU.mult, ALU.add).then_inc(k.ff_mix, 1)

            def choose(it, c):
                g = it * 2 + (base + c)
                rank = k.prank[:, None, :].to_broadcast([P, TI, NP])
                scores = own[c][:, 0:TI * NP].rearrange("p (t e) -> p t e", e=NP)
                col = top[c][:, :, None].to_broadcast([P, TI, NP])
                dve.wait_ge(k.ff_score, g + 1)
                nc.vector.tensor_reduce(top[c], scores, AX.X, ALU.max).then_inc(k.ff_step, 1)
                dve.wait_ge(k.ff_step, g * 4 + 1)
                nc.vector.tensor_tensor(cand[c], scores, col, ALU.is_equal).then_inc(k.ff_step, 1)
                dve.wait_ge(k.ff_step, g * 4 + 2)
                nc.vector.tensor_tensor(cand[c], cand[c], rank, ALU.mult).then_inc(k.ff_step, 1)
                dve.wait_ge(k.ff_step, g * 4 + 3)
                nc.vector.tensor_reduce(top[c], cand[c], AX.X, ALU.max).then_inc(k.ff_step, 1)
                dve.wait_ge(k.ff_step, g * 4 + 4)
                nc.vector.tensor_tensor(hot[c], rank, col, ALU.is_equal).then_inc(k.ff_hot, 1)

            def mask(it, c):
                g = it * 2 + (base + c)
                dve.wait_ge(k.ff_out, g + 1)
                for j in range(GR):
                    dve.wait_ge(k.ff_hid, g * 3 + (j + 1 + PRIMED["ff_hid"]))
                    dve.wait_ge(k.ff_spreads, g * 3 + (j + 1))
                    nc.vector.tensor_tensor(hm[:, j * CH:(j + 1) * CH], hid[c][:, j * CH:(j + 1) * CH], masks[j][:], ALU.mult).then_inc(k.ff_masked, 1)

            def add(it, c):
                g = it * 2 + (base + c)
                dve.wait_ge(k.ff_out, g + (1 + PRIMED["ff_out"]))
                nc.vector.tensor_tensor(Z[:, bass.ds(it * L + c * CH, CH)], k.N[:, bass.ds(it * PADL + 1 + c * CH, CH)], own[c][:], ALU.add).then_inc(k.ff_z, 1)

            def turn(it, first, last):
                for c in range(2):
                    before = (it - 1, 1) if c == 0 else (it, 0)
                    if not (first and c == 0):
                        mask(*before)
                    choose(it, c)
                    if not (first and c == 0):
                        add(*before)
                    if not last:
                        mix(it + 1, c)

            mix(0, 0)
            mix(0, 1)
            turn(0, True, False)
            with dve.Fori(1, B - 1) as it:
                turn(it, False, False)
            turn(B - 1, False, True)
            mask(B - 1, 1)
            add(B - 1, 1)

        @block.tensor
        def _(pe):
            if call == 0:
                pe.wait_ge(k.ff_w_in, 16 * (NP + 5))
                pe.wait_ge(k.ff_spread16, 1)
                pe.wait_ge(k.ff_const, 1 + NP)
            pe.wait_ge(k.ff_hot0, 4 * call + 4)
            def hidden(it, c):
                g = it * 2 + (base + c)
                pe.wait_ge(k.ff_mix, g + 1)
                for j in range(GR):
                    pe.wait_ge(k.ff_hid, g * 3 + (j + 1))
                    nc.tensor.matmul(k.bank[j][:], k.W1[:, j, :], xm[c], start=True, stop=True).then_inc(k.ff_h, 1)
                    if j == 0:
                        pe.wait_ge(k.ff_z, g + 1)
                        nc.tensor.matmul(own[c][0:DM, :], k.Wo1, xm[c], start=True, stop=True).then_inc(k.ff_up, 1)

            def scores(it, c):
                pe.wait_ge(k.ff_u, it * 2 + (base + c + 1))
                for t in range(TI):
                    op = nc.tensor.matmul(own[c][:, t * NP:(t + 1) * NP], u[c][:, t * P:(t + 1) * P], k.Wo2[:], start=True, stop=True)
                op.then_inc(k.ff_score, 1)

            def turned(it, c):
                pe.wait_ge(k.ff_hot, it * 2 + (base + c + 1))
                for t in range(TI):
                    op = nc.tensor.transpose(own[c][0:NP, t * P:(t + 1) * P], hot[c][:, t, :], k.ident[:])
                op.then_inc(k.ff_hotT, 1)

            def spread(it, c):
                g = it * 2 + (base + c)
                pe.wait_ge(k.ff_hot16, g + 1)
                for j in range(GR):
                    pe.wait_ge(k.ff_masked, g * 3 + (j + 1 + PRIMED["ff_masked"] - GR))
                    nc.tensor.matmul(masks[j][:], k.spread16[:, j, :], hotT[c], start=True, stop=True).then_inc(k.ff_spreads, 1)

            def down(it, c):
                g = it * 2 + (base + c)
                for j in range(GR):
                    rows = P if j == 0 else GW
                    pe.wait_ge(k.ff_masked, g * 3 + (j + 1 + PRIMED["ff_masked"]))
                    op = nc.tensor.matmul(own[c][:], k.W2[0:rows, j, :], hm[0:rows, j * CH:(j + 1) * CH], start=(j == 0), stop=(j == GR - 1))
                op.then_inc(k.ff_out, 1)

            def turn(it, first):
                for c in range(2):
                    before = (it - 1, 1) if c == 0 else (it, 0)
                    if not (first and c == 0):
                        turned(*before)
                    hidden(it, c)
                    if not (first and c == 0):
                        spread(*before)
                    scores(it, c)
                    if not (first and c == 0):
                        down(*before)

            turn(0, True)
            with pe.Fori(1, B) as it:
                turn(it, False)
            turned(B - 1, 1)
            spread(B - 1, 1)
            down(B - 1, 1)

        @block.scalar
        def _(act):
            def hidden(it, c):
                g = it * 2 + (base + c)
                for j in range(GR):
                    act.wait_ge(k.ff_h, g * 3 + (j + 1 + PRIMED["ff_h"]))
                    act.wait_ge(k.ff_masked, g * 3 + (j + 1))
                    nc.scalar.activation(hid[c][:, j * CH:(j + 1) * CH], k.bank[j][:], ACT.Identity, bias=k.vec(f"b1_{j}")).then_inc(k.ff_hid, 1)
                    if j == 0:
                        act.wait_ge(k.ff_up, g + 1)
                        nc.scalar.activation(u[c][0:DM, :], own[c][0:DM, :], ACT.Tanh, bias=k.vec("bo1", DM)).then_inc(k.ff_u, 1)

            def choice(it, c):
                act.wait_ge(k.ff_hotT, it * 2 + (base + c + 1))
                nc.scalar.activation(hotT[c][0:NP, :], own[c][0:NP, :], ACT.Copy).then_inc(k.ff_hot16, 1)

            def turn(it, first):
                for c in range(2):
                    if not (first and c == 0):
                        choice(*((it - 1, 1) if c == 0 else (it, 0)))
                    hidden(it, c)

            turn(0, True)
            with act.Fori(1, B) as it:
                turn(it, False)
            choice(B - 1, 1)


def stage_ffn(nc, k, a, X, Y):
    call = k.ff_calls
    k.ff_calls += 1
    k.ln(X, lambda it, c: padded(k.N, it, c))
    feedforward(nc, k, a, call)
    k.ln(lambda it, c: plain(k.big[1], it, c), None, gain="gamma", bias="beta", residual=X)


def lru(nc, k, a):
    KK, KV, R = k.big[0], k.big[1], k.big[2]
    u1, u2 = k.big[3][:, 0:L + 1], k.big[3][:, L + 1:2 * L + 2]
    t1, t2 = k.big[4][:, 0:L], k.big[4][:, L:2 * L]
    W_rkv, W_o = k.lruw[:, 0:3 * P], k.lruw[:, 3 * P:4 * P]
    with nc.Block() as block:
        @block.sync
        def _(sp):
            sp.dma_start(W_rkv, a["L1_attn_b_W_rkv"]).then_inc(k.lr_w_in, 16)
            sp.dma_start(W_o, a["L1_attn_b_W_o"]).then_inc(k.lr_w_in, 16)

        @block.tensor
        def _(pe):
            pe.wait_ge(k.lr_w_in, 32)
            with pe.Fori(0, B) as it:
                for c in range(2):
                    for j in range(3):
                        n = it * 6 + (3 * c + j)
                        pe.wait_ge(k.lr_read, n + 1)
                        nc.tensor.matmul(k.bank[3 * c + j][:], W_rkv[:, j * P:(j + 1) * P], k.Y[:, bass.ds(it * L + c * CH, CH)],
                                         start=True, stop=True).then_inc(k.lr_prod, 1)

        @block.scalar
        def _(act):
            act.preload_act_table_set("natural_log_exp_and_others")
            act.wait_ge(k.lr_init, 1)
            nc.scalar.activation(k.lr_nu[:], k.vec("nu_log"), ACT.Exp).then_inc(k.lr_sc, 1)
            act.wait_ge(k.lr_sc, 1)
            nc.scalar.activation(k.lr_lam[:], k.lr_nu[:], ACT.Exp, scale=-1.0).then_inc(k.lr_sc, 1)
            nc.scalar.activation(k.lr_own[:], k.vec("nu_log"), ACT.Exp, bias=k.vec("gamma_log")).then_inc(k.lr_sc, 1)

            def exps(it):
                for c in range(2):
                    at = bass.ds(it * L + c * CH, CH)
                    n = it * 6 + 3 * c
                    wait_apart(act, k, k.lr_prod, n + 1)
                    nc.scalar.activation(R[:, at], k.bank[3 * c][:], ACT.Exp, bias=k.lr_nbr[:, 0:1], scale=-1.0).then_inc(k.lr_read, 1)
                    wait_apart(act, k, k.lr_prod, n + 2)
                    nc.scalar.activation(KK[:, at], k.bank[3 * c + 1][:], ACT.Exp, bias=k.vec("bkk")).then_inc(k.lr_read, 1)
                    wait_apart(act, k, k.lr_prod, n + 3)
                    nc.scalar.activation(KV[:, at], k.bank[3 * c + 2][:], ACT.Identity, bias=k.vec("bvv")).then_inc(k.lr_read, 1)

            def over(it):
                at = bass.ds(it * L, L)
                wait_apart(act, k, k.lr_den, it + 1)
                nc.scalar.activation(KK[:, at], KK[:, at], ACT.Ln).then_inc(k.lr_ln, 1)
                wait_apart(act, k, k.lr_ln, it + 1)
                nc.scalar.activation(KK[:, at], KK[:, at], ACT.Exp, scale=-1.0).then_inc(k.lr_rden, 1)

            exps(0)
            with act.Fori(1, B) as it:
                exps(it)
                over(it - 1)
            over(B - 1)

        @block.vector
        def _(dve):
            nc.vector.tensor_scalar(k.lr_nbr[:], k.vec("br"), -1.0, None, ALU.mult).then_inc(k.lr_init, 1)
            nc.vector.memset(u1[:, 0:1], 0.0)
            nc.vector.memset(u2[:, 0:1], 0.0)
            dve.wait_ge(k.lr_sc, 3)
            nc.vector.tensor_copy(k.lam, k.lr_lam[:, 0:1].to_broadcast([P, L])).then_inc(k.lr_init, 1)
            dve.wait_ge(k.lr_init, 2)

            def sums(it):
                at = bass.ds(it * L, L)
                s = it * 6
                dve.wait_ge(k.lr_read, it * 6 + (6 + PRIMED["lr_read"]))
                nc.vector.tensor_tensor(KV[:, at], KV[:, at], KK[:, at], ALU.mult).then_inc(k.lr_step, 1)
                dve.wait_ge(k.lr_step, s + 1)
                nc.vector.tensor_tensor_scan(u2[:, 1:L + 1], k.lam, KK[:, at], 0.0, ALU.mult, ALU.add).then_inc(k.lr_step, 1)
                nc.vector.tensor_tensor_scan(u1[:, 1:L + 1], k.lam, KV[:, at], 0.0, ALU.mult, ALU.add).then_inc(k.lr_step, 1)
                nc.vector.tensor_scalar(t2, KK[:, at], k.lr_own[:, 0:1], 1e-6, ALU.mult, ALU.add)
                nc.vector.tensor_scalar(t1, KV[:, at], k.lr_own[:, 0:1], None, ALU.mult).then_inc(k.lr_step, 1)
                dve.wait_ge(k.lr_step, s + 4)
                nc.vector.scalar_tensor_tensor(t2, u2[:, 0:L], k.lr_lam[:, 0:1], t2, ALU.mult, ALU.add).then_inc(k.lr_step, 1)
                nc.vector.scalar_tensor_tensor(KV[:, at], u1[:, 0:L], k.lr_lam[:, 0:1], t1, ALU.mult, ALU.add).then_inc(k.lr_step, 1)
                dve.wait_ge(k.lr_step, s + 6)
                nc.vector.scalar_tensor_tensor(KK[:, at], R[:, at], 1.0, t2, ALU.add, ALU.mult).then_inc(k.lr_den, 1)

            def quotient(it):
                at = bass.ds(it * L, L)
                dve.wait_ge(k.lr_rden, it + 1)
                nc.vector.tensor_tensor(R[:, at], KV[:, at], KK[:, at], ALU.mult).then_inc(k.lr_x, 1)

            sums(0)
            with dve.Fori(1, B) as it:
                sums(it)
                quotient(it - 1)
            quotient(B - 1)


def stage_lru(nc, k, a, X, Y):
    k.ln(X, Y)
    lru(nc, k, a)
    project_add(nc, k, k.pa_calls, k.lruw[:, 3 * P:4 * P], lambda it, c: plain(k.big[2], it, c), X, bias=k.vec("lru_bo"))
    k.pa_calls += 1


def tree_weights(nc, k, a):
    rows = k.big[0][:, 0:8 * P].rearrange("p (j d) -> p j d", d=P)
    turned = k.big[1][:, 0:5 * P].rearrange("p (j d) -> p j d", d=P)
    with nc.Block() as block:
        @block.sync
        def _(sp):
            sp.dma_start(rows[:, 0, :], a["L1_ffn_routers"][0:P, :]).then_inc(k.tw_in, 16)
            sp.dma_start(rows[0:P - 1, 1, :], a["L1_ffn_routers"][P:2 * P - 1, :]).then_inc(k.tw_in, 16)
            sp.dma_start(rows[:, 2:4, :], a["L1_ffn_leaf_values"].rearrange("(h m) d -> m h d", h=2)).then_inc(k.tw_in, 16)
            sp.dma_start(rows[:, 4, :], a["L1_ffn_Wout_w"]).then_inc(k.tw_in, 16)
            sp.dma_start(rows[:, 5, :], a["L1_ffn_Wq"]).then_inc(k.tw_in, 16)

        @block.tensor
        def _(pe):
            pe.wait_ge(k.tw_in, 5 * 16)
            for j in range(5):
                n = P - 1 if j == 1 else P
                nc.tensor.transpose(k.bank[j // 4][:, (j % 4) * P:(j % 4) * P + n], rows[0:n, j, :], k.ident[0:n, 0:n]).then_inc(k.tw_turned, 1)
            pe.wait_ge(k.tw_copied, 5)
            nc.tensor.matmul(k.bank[2][:, 0:2 * P], rows[:, 5, :], turned[:, 0:2, :].rearrange("p j d -> p (j d)"), start=True, stop=True).then_inc(k.tw_prod, 1)
            for h in range(2):
                nc.tensor.matmul(k.bank[3 + h][:, 0:P], turned[:, 2 + h, :], turned[:, 4, :], start=True, stop=True).then_inc(k.tw_prod, 1)

        @block.vector
        def _(dve):
            nc.vector.memset(turned[:, 1, :], 0.0).then_inc(k.tw_zero, 1)
            dve.wait_ge(k.tw_zero, 1)
            dve.wait_ge(k.tw_turned, 5)
            for j in range(5):
                n = P - 1 if j == 1 else P
                nc.vector.tensor_copy(turned[:, j, 0:n], k.bank[j // 4][:, (j % 4) * P:(j % 4) * P + n]).then_inc(k.tw_copied, 1)
            dve.wait_ge(k.tw_prod, 3)
            nc.vector.tensor_copy(k.gates, k.bank[2][:, 0:2 * P])
            for h in range(2):
                nc.vector.tensor_copy(k.leaves[:, h, :], k.bank[3 + h][:, 0:P])


def tree(nc, k, a, call):
    TI, M, DEPTH = CH // P, 256, 8
    base = call * NCH
    wide = lambda v: v.rearrange("p (t m) -> p t m", m=M)
    gr = [wide(k.big[0][:, 2 * c * CH:2 * (c + 1) * CH]) for c in range(2)]
    gl = [wide(k.big[0][:, (4 + 2 * c) * CH:(6 + 2 * c) * CH]) for c in range(2)]
    lp = [[wide(k.big[1][:, (4 * c + 2 * s) * CH:(4 * c + 2 * s + 2) * CH]) for s in range(2)] for c in range(2)]
    th = k.big[2][:, 0:2 * CH]
    ys = [k.big[2][:, (2 + c) * CH:(3 + c) * CH] for c in range(2)]
    lpT = [k.big[2][:, (4 + 2 * c) * CH:(6 + 2 * c) * CH] for c in range(2)]

    def done(s, g):
        return g + (1 + PRIMED.get(s, 0))

    with nc.Block() as block:
        @block.tensor
        def _(pe):
            def front(it):
                for c in range(2):
                    g = it * 2 + (base + c)
                    pe.wait_ge(k.tr_th, g + 1)
                    pe.wait_ge(k.tr_ys, done("tr_ys", g))
                    for t in range(TI):
                        op = nc.tensor.matmul(k.bank[2 * c + t // 2][:, (t % 2) * M:(t % 2 + 1) * M], ys[c][:, t * P:(t + 1) * P], k.gates, start=True, stop=True)
                    op.then_inc(k.tr_z, 1)

            def back(it):
                for c in range(2):
                    g = it * 2 + (base + c)
                    pe.wait_ge(k.tr_lpT, g + 1)
                    pe.wait_ge(k.tr_lp, done("tr_lp", g))
                    for h in range(2):
                        for t in range(TI):
                            op = nc.tensor.transpose(k.bank[4 + h][:, t * P:(t + 1) * P], lp[c][1][:, t, h * P:(h + 1) * P], k.ident[:])
                    op.then_inc(k.tr_turned, 1)
                    pe.wait_ge(k.tr_x, g + 1)
                    pe.wait_ge(k.tr_lpT, done("tr_lpT", g))
                    for h in range(2):
                        op = nc.tensor.matmul(k.bank[6 + c][:], k.leaves[:, h, :], lpT[c][:, h * CH:(h + 1) * CH], start=(h == 0), stop=(h == 1))
                    op.then_inc(k.tr_out, 1)

            front(0)
            with pe.Fori(1, NCH // 2) as it:
                front(it)
                back(it - 1)
            back(NCH // 2 - 1)

        @block.scalar
        def _(act):
            def front(it):
                for c in range(2):
                    g = it * 2 + (base + c)
                    act.wait_ge(k.tr_z, g + 1)
                    nc.scalar.activation(ys[c], k.Y[:, bass.ds(it * L + c * CH, CH)], ACT.Copy).then_inc(k.tr_ys, 1)
                for c in range(2):
                    g = it * 2 + (base + c)
                    act.wait_ge(k.tr_z, done("tr_z", g))
                    act.wait_ge(k.tr_g, g + 1)
                    for h in range(2):
                        op = nc.scalar.activation(th[:, h * CH:(h + 1) * CH], k.bank[2 * c + h][:], ACT.Tanh, scale=0.5)
                    op.then_inc(k.tr_th, 1)

            def back(it):
                for c in range(2):
                    g = it * 2 + (base + c)
                    act.wait_ge(k.tr_turned, done("tr_turned", g))
                    act.wait_ge(k.tr_out, g + 1)
                    for h in range(2):
                        op = nc.scalar.activation(lpT[c][:, h * CH:(h + 1) * CH], k.bank[4 + h][:], ACT.Copy)
                    op.then_inc(k.tr_lpT, 1)

            front(0)
            with act.Fori(1, NCH // 2) as it:
                front(it)
                back(it - 1)
            back(NCH // 2 - 1)

        @block.vector
        def _(dve):
            def front(it):
                for c in range(2):
                    g = it * 2 + (base + c)
                    dve.wait_ge(k.tr_th, done("tr_th", g))
                    nc.vector.tensor_scalar(gr[c], wide(th), 0.5, 0.5, ALU.mult, ALU.add)
                    nc.vector.tensor_scalar(gl[c], wide(th), -0.5, 0.5, ALU.mult, ALU.add).then_inc(k.tr_g, 1)
                    dve.wait_ge(k.tr_g, done("tr_g", g))
                    dve.wait_ge(k.tr_turned, g + 1)
                    nc.vector.tensor_copy(lp[c][0][:, :, 0:1], gl[c][:, :, 0:1])
                    nc.vector.tensor_copy(lp[c][0][:, :, 1:2], gr[c][:, :, 0:1]).then_inc(k.tr_step, 1)
                    for level in range(1, DEPTH):
                        n = 2 ** level
                        dve.wait_ge(k.tr_step, g * (DEPTH - 1) + level)
                        src, dst = lp[c][(level - 1) % 2][:, :, 0:n], lp[c][level % 2][:, :, 0:2 * n]
                        pairs = dst.rearrange("p t (n s) -> p t n s", s=2)
                        nc.vector.tensor_tensor(pairs[:, :, :, 0], src, gl[c][:, :, n - 1:2 * n - 1], ALU.mult)
                        op = nc.vector.tensor_tensor(pairs[:, :, :, 1], src, gr[c][:, :, n - 1:2 * n - 1], ALU.mult)
                        op.then_inc(k.tr_lp if level == DEPTH - 1 else k.tr_step, 1)

            def back(it):
                for c in range(2):
                    g = it * 2 + (base + c)
                    at = bass.ds(it * L + c * CH, CH)
                    dve.wait_ge(k.tr_out, done("tr_out", g))
                    nc.vector.scalar_tensor_tensor(k.X[:, at], k.bank[6 + c][:], k.vec("wout_b"), k.X[:, at], ALU.add, ALU.add).then_inc(k.tr_x, 1)

            front(0)
            with dve.Fori(1, NCH // 2) as it:
                front(it)
                back(it - 1)
            back(NCH // 2 - 1)


def stage_tree(nc, k, a, X, Y):
    call = k.tr_calls
    k.tr_calls += 1
    k.ln(X, Y)
    if call == 0:
        tree_weights(nc, k, a)
    tree(nc, k, a, call)


def favor_weights(nc, k, a):
    H, M, DK, G = 16, 32, 8, 4
    rows = k.arena[:, 0:4 * P].rearrange("p (j d) -> p j d", d=P)
    proj = k.arena[:, 4 * P:4 * P + G * DK].rearrange("p (g d) -> p g d", g=G)
    mask = k.arena[:, 5 * P:5 * P + G * H].rearrange("p (g h) -> p g h", g=G)
    wide = k.arena[:, 6 * P:10 * P].rearrange("p (g n) -> p g n", g=G)
    diag = k.arena[:, 10 * P:14 * P]
    with nc.Block() as block:
        @block.sync
        def _(sp):
            for j, w in enumerate((a["L0_attn_b_Wq"], a["L0_attn_b_Wk"], a["L0_attn_b_Wv"], a["L0_attn_b_Wo"])):
                sp.dma_start(rows[:, j, :], w).then_inc(k.fw_in, 16)
            sp.dma_start(proj, a["L0_attn_b_proj"].rearrange("(g h) m d -> (h m) g d", g=G)).then_inc(k.fw_in, 16)

        @block.gpsimd
        def _(pool):
            nc.gpsimd.memset(mask, 1.0).then_inc(k.fw_mask, 1)
            nc.gpsimd.memset(k.fv_own, 1.0 / M).then_inc(k.fw_mask, 1)
            pool.wait_ge(k.fw_mask, 2)
            nc.gpsimd.affine_select(out=mask, in_=mask, compare_op=ALU.is_ge, fill=0.0, base=0,
                                    pattern=[[4 * M, G], [-M, H]], channel_multiplier=1).then_inc(k.fw_mask, 1)
            nc.gpsimd.affine_select(out=k.fv_own, in_=k.fv_own, compare_op=ALU.is_ge, fill=0.0, base=0,
                                    pattern=[[-M, 4]], channel_multiplier=1).then_inc(k.fw_mask, 1)
            pool.wait_ge(k.fw_mask, 4)
            nc.gpsimd.affine_select(out=mask, in_=mask, compare_op=ALU.is_ge, fill=0.0, base=M - 1,
                                    pattern=[[-4 * M, G], [M, H]], channel_multiplier=-1).then_inc(k.fw_mask, 1)
            nc.gpsimd.affine_select(out=k.fv_own, in_=k.fv_own, compare_op=ALU.is_ge, fill=0.0, base=M - 1,
                                    pattern=[[M, 4]], channel_multiplier=-1).then_inc(k.fw_mask, 1)
            nc.gpsimd.memset(k.eps6[:], 1e-6).then_inc(k.fw_mask, 1)

        @block.tensor
        def _(pe):
            pe.wait_ge(k.fw_in, 5 * 16)
            for j in range(4):
                nc.tensor.transpose(k.bank[0][:, j * P:(j + 1) * P], rows[:, j, :], k.ident[:]).then_inc(k.fw_turned, 1)
            pe.wait_ge(k.fw_wide, 1)
            for g in range(G):
                nc.tensor.transpose(k.bank[1][:, g * P:(g + 1) * P], wide[:, g, :], k.ident[:]).then_inc(k.fw_turned, 1)
            pe.wait_ge(k.fw_copied, 2)
            for j in range(2):
                nc.tensor.matmul(k.bank[2 + j][:], rows[:, j, :], diag, start=True, stop=True).then_inc(k.fw_prod, 1)

        @block.vector
        def _(dve):
            dve.wait_ge(k.fw_in, 5 * 16)
            dve.wait_ge(k.fw_mask, 7)
            for g in range(G):
                op = nc.vector.tensor_tensor(wide[:, g, :].rearrange("p (h d) -> p h d", d=DK), proj[:, g:g + 1, :].to_broadcast([P, H, DK]),
                                             mask[:, g, :, None].to_broadcast([P, H, DK]), ALU.mult)
            op.then_inc(k.fw_wide, 1)
            dve.wait_ge(k.fw_turned, 4)
            nc.vector.tensor_copy(k.fv_wT, k.bank[0][:]).then_inc(k.fw_copied, 1)
            dve.wait_ge(k.fw_turned, 8)
            nc.vector.tensor_copy(diag, k.bank[1][:]).then_inc(k.fw_copied, 1)
            for j in range(2):
                dve.wait_ge(k.fw_prod, j + 1)
                nc.vector.tensor_scalar(k.fv_feat[:, j, :], k.bank[2 + j][:], DK ** -0.5, None, ALU.mult)


def favor(nc, k, a):
    H, M, DK, G = 16, 32, 8, 4
    TT = L // P
    take = [0]

    def part(n):
        take[0] += n
        return k.arena[:, take[0] - n:take[0]]

    ys = [part(CH) for _ in range(2)]
    sq = [part(P) for _ in range(2)]
    va = [part(144).rearrange("p (h n) -> p h n", n=9) for _ in range(4)]
    mx = [part(H) for _ in range(2)]
    nm = [part(H) for _ in range(2)]
    rd = [part(H) for _ in range(2)]
    kv = part(B * 144)
    ex = [part(CH) for _ in range(4)]
    exT = [part(CH) for _ in range(2)]
    o = [part(P) for _ in range(2)]
    oT = part(CH)
    wT = k.fv_wT

    def done(s, n):
        return n + (1 + PRIMED.get(s, 0))

    def there(at, i):
        return at is None or 0 <= at + i < B * TT

    def run(eng, turn, steps):
        turn(0, 0, TT)
        with eng.Fori(1, B) as u:
            turn(u, None, TT)
        turn(B, B * TT, steps)

    def copy_input(pool, b, c, n0):
        if n0 or not isinstance(b, int):
            wait_apart(pool, k, k.fv_proj, b * TT + (n0 + 4 * c + 3 - TT + 1 + PRIMED["fv_proj"]))
        nc.gpsimd.tensor_copy(ys[c], k.Y[:, bass.ds(b * L + c * CH, CH)]).then_inc(k.fv_ys, 1)

    def project(pe, n, i, b, y0, width, weight, read, feat):
        if i % 4 == 0:
            pe.wait_ge(k.fv_ys, b * 2 + (y0 + i // 4 + 1))
        y = ys[i // 4][:, (i % 4) * P:(i % 4 + 1) * P]
        pe.wait_ge(read, n + 1)
        nc.tensor.matmul(k.bank[i % 2][:, 0:width], y, weight, start=True, stop=True)
        pe.wait_ge(k.fv_arg, n + 1)
        nc.tensor.matmul(k.bank[2 + i % 2][:], y, feat, start=True, stop=True).then_inc(k.fv_proj, 1)

    def square(act, n, i):
        act.wait_ge(k.fv_proj, done("fv_proj", n))
        nc.scalar.activation(sq[i % 2], k.bank[i % 2][:, 0:P], ACT.Square, scale=(0.5 / DK) ** 0.5).then_inc(k.fv_sq, 1)

    def exp(act, n, i):
        act.wait_ge(k.fv_arg, done("fv_arg", n))
        nc.scalar.activation(ex[i % 4], ex[i % 4], ACT.Exp).then_inc(k.fv_exp, 1)

    def statistics(dve, n, i):
        s = i % 2
        heads = k.bank[2 + s][:].rearrange("p (h m) -> p h m", m=M)
        dve.wait_ge(k.fv_proj, done("fv_proj", n))
        nc.vector.tensor_reduce(mx[s], heads, AX.X, ALU.max).then_inc(k.fv_max, 1)
        dve.wait_ge(k.fv_sq, done("fv_sq", n))
        nc.vector.tensor_reduce(nm[s], sq[s].rearrange("p (h d) -> p h d", d=DK), AX.X, ALU.add).then_inc(k.fv_max, 1)
        dve.wait_ge(k.fv_max, n * 2 + 2)
        nc.vector.tensor_tensor(mx[s], mx[s], nm[s], ALU.add).then_inc(k.fv_off, 1)
        dve.wait_ge(k.fv_off, n + 1)
        dve.wait_ge(k.fv_used, n + 1)
        nc.vector.tensor_tensor(ex[i % 4].rearrange("p (h m) -> p h m", m=M), heads, mx[s][:, :, None].to_broadcast([P, H, M]),
                                ALU.subtract).then_inc(k.fv_arg, 1)

    with nc.Block() as block:
        @block.tensor
        def _(pe):
            def gather(n, i, b):
                if i % TT == 0:
                    pe.wait_ge(k.fv_kv, b + 1)
                pe.wait_ge(k.fv_phi, n + 1)
                for g in range(G):
                    op = nc.tensor.matmul(k.bank[4][:, g * 36:(g + 1) * 36], ex[i % 4][:, g * P:(g + 1) * P],
                                          va[i % 4][:, 4 * g:4 * g + 4, :].rearrange("p h n -> p (h n)"),
                                          start=(i % TT == 0 and g == 0), stop=(i % TT == TT - 1), skip_group_check=True)
                op.then_inc(k.fv_used, 1)

            def turn(u, at, steps):
                for i in range(steps):
                    if there(at, i):
                        project(pe, u * TT + i, i, u, 0, 2 * P, wT[:, P:3 * P], k.fv_va, k.fv_feat[:, 1, :])
                    if there(at, i - 3):
                        gather(u * TT + (i - 3), i - 3, u)

            run(pe, turn, 3)

        @block.scalar
        def _(act):
            act.preload_act_table_set("exp_and_others")

            def values(n, i):
                act.wait_ge(k.fv_used, n + 1)
                nc.scalar.activation(va[i % 4][:, :, 0:DK], k.bank[i % 2][:, P:2 * P].rearrange("p (h d) -> p h d", d=DK), ACT.Copy).then_inc(k.fv_va, 1)

            def turn(u, at, steps):
                for i in range(steps):
                    if there(at, i):
                        square(act, u * TT + i, i)
                    if there(at, i - 1):
                        exp(act, u * TT + (i - 1), i - 1)
                    if there(at, i):
                        values(u * TT + i, i)

            run(act, turn, 1)

        @block.gpsimd
        def _(pool):
            for s in range(4):
                nc.gpsimd.memset(va[s][:, :, DK:DK + 1], 1.0)

            def turn(u, at, steps):
                for i in range(steps):
                    if i % 4 == 0 and there(at, i):
                        copy_input(pool, u, i // 4, 0)
                    if there(at, i - 2):
                        wait_apart(pool, k, k.fv_exp, u * TT + (i - 2 + 1))
                        nc.gpsimd.tensor_scalar(ex[(i - 2) % 4], ex[(i - 2) % 4], 1e-6, None, ALU.add).then_inc(k.fv_phi, 1)

            run(pool, turn, 2)

        @block.vector
        def _(dve):
            def keep(b, column):
                dve.wait_ge(k.fv_used, b * TT + (TT + PRIMED["fv_used"]))
                nc.vector.tensor_tensor(kv[:, bass.ds(column, 144)].rearrange("p (g h n) -> p g h n", g=G, h=4),
                                        k.bank[4][:, 0:144].rearrange("p (g h n) -> p g h n", g=G, h=4),
                                        k.fv_own[:, None, :, None].to_broadcast([P, G, 4, 9]), ALU.mult).then_inc(k.fv_kv, 1)

            def turn(u, at, steps):
                for i in range(steps):
                    if there(at, i):
                        statistics(dve, u * TT + i, i)
                    if i == 2 and there(at, i - 3):
                        keep(u - 1, u * 144 - 144)

            run(dve, turn, 3)

    n0 = B * TT
    with nc.Block() as block:
        @block.tensor
        def _(pe):
            def turned(n, i):
                pe.wait_ge(k.fv_exp, n + (n0 + 1))
                pe.wait_ge(k.fv_exT, n + 1)
                for g in range(G):
                    op = nc.tensor.transpose(k.bank[4][:, g * P:(g + 1) * P], ex[i % 4][:, g * P:(g + 1) * P], k.ident[:])
                op.then_inc(k.fv_used, 1)

            def sums(n, i, column):
                pe.wait_ge(k.fv_exT, done("fv_exT", n))
                pe.wait_ge(k.fv_o, n + 1)
                for g in range(G):
                    op = nc.tensor.matmul(k.bank[5][:, g * 36:(g + 1) * 36], exT[i % 2][:, g * P:(g + 1) * P],
                                          kv[:, bass.ds(column + g * 36, 36)], start=True, stop=True)
                op.then_inc(k.fv_sums, 1)

            def back(n, i, g):
                pe.wait_ge(k.fv_o, done("fv_o", n))
                if i % 4 == 0:
                    pe.wait_ge(k.fv_oT, g + 1)
                nc.tensor.transpose(k.bank[6][:, (i % 4) * P:(i % 4 + 1) * P], o[i % 2], k.ident[:]).then_inc(k.fv_back, 1)

            def output(g):
                pe.wait_ge(k.fv_oT, done("fv_oT", g))
                pe.wait_ge(k.fv_x, g + 1)
                nc.tensor.matmul(k.bank[7][:], wT[:, 3 * P:4 * P], oT, start=True, stop=True).then_inc(k.fv_out, 1)

            def turn(u, at, steps):
                for i in range(steps):
                    if there(at, i):
                        project(pe, u * TT + (n0 + i), i, u, 2 * B, P, wT[:, 0:P], k.fv_sq, k.fv_feat[:, 0, :])
                    if there(at, i - 2):
                        turned(u * TT + (i - 2), i - 2)
                    if there(at, i - 3):
                        sums(u * TT + (i - 3), i - 3, u * 144 + (i - 3) // TT * 144)
                    if there(at, i - 4):
                        back(u * TT + (i - 4), i - 4, u * 2 + (i - 4) // 4)
                    if i % 4 == 0 and there(at, i - 8):
                        output(u * 2 + (i - 8) // 4)

            run(pe, turn, 5)

        @block.scalar
        def _(act):
            def turned(n, i):
                act.wait_ge(k.fv_used, done("fv_used", n + n0))
                act.wait_ge(k.fv_sums, n + 1)
                nc.scalar.activation(exT[i % 2], k.bank[4][:], ACT.Identity, bias=k.eps6[:, 0:1]).then_inc(k.fv_exT, 1)

            def heads(g):
                act.wait_ge(k.fv_back, g * 4 + 4)
                act.wait_ge(k.fv_out, g + 1)
                nc.scalar.activation(oT, k.bank[6][:], ACT.Copy).then_inc(k.fv_oT, 1)

            def turn(u, at, steps):
                for i in range(steps):
                    if there(at, i):
                        square(act, u * TT + (n0 + i), i)
                    if there(at, i - 1):
                        exp(act, u * TT + (n0 + i - 1), i - 1)
                    if there(at, i - 2):
                        turned(u * TT + (i - 2), i - 2)
                    if i % 4 == 3 and there(at, i - 7):
                        heads(u * 2 + (i - 7) // 4)

            run(act, turn, 4)

        @block.gpsimd
        def _(pool):
            with pool.Fori(0, B) as b:
                for c in range(2):
                    copy_input(pool, b, c, n0)

        @block.vector
        def _(dve):
            def quotient(n, i):
                s = i % 2
                sums = k.bank[5][:, 0:144].rearrange("p (h n) -> p h n", n=9)
                dve.wait_ge(k.fv_sums, done("fv_sums", n))
                nc.vector.tensor_scalar(rd[s], sums[:, :, DK], 1e-6, None, ALU.add).then_inc(k.fv_rd, 1)
                dve.wait_ge(k.fv_rd, n * 2 + 1)
                nc.vector.reciprocal(rd[s], rd[s]).then_inc(k.fv_rd, 1)
                dve.wait_ge(k.fv_rd, n * 2 + 2)
                nc.vector.tensor_tensor(o[s].rearrange("p (h d) -> p h d", d=DK), sums[:, :, 0:DK],
                                        rd[s][:, :, None].to_broadcast([P, H, DK]), ALU.mult).then_inc(k.fv_o, 1)

            def add(g, column):
                at = bass.ds(column, CH)
                dve.wait_ge(k.fv_out, done("fv_out", g))
                nc.vector.scalar_tensor_tensor(k.X[:, at], k.bank[7][:], k.vec("favor_bo"), k.X[:, at], ALU.add, ALU.add).then_inc(k.fv_x, 1)

            def turn(u, at, steps):
                for i in range(steps):
                    if there(at, i):
                        statistics(dve, u * TT + (n0 + i), i)
                    if there(at, i - 3):
                        quotient(u * TT + (i - 3), i - 3)
                    if i % 4 == 1 and there(at, i - 9):
                        add(u * 2 + (i - 9) // 4, u * L + (i - 9) // 4 * CH)

            run(dve, turn, 6)


def stage_favor(nc, k, a, X, Y):
    k.ln(X, Y)
    with ExitStack() as ctx:
        sems = begin_stage(nc, ctx, FAVOR_SEMS)
        (k.fw_in, k.fw_mask, k.fw_turned, k.fw_wide, k.fw_copied, k.fw_prod, k.fv_ys, k.fv_proj, k.fv_sq, k.fv_va,
         k.fv_max, k.fv_off, k.fv_arg, k.fv_exp, k.fv_phi, k.fv_used, k.fv_kv, k.fv_exT, k.fv_sums, k.fv_o,
         k.fv_rd, k.fv_back, k.fv_oT, k.fv_out, k.fv_x) = sems
        favor_weights(nc, k, a)
        favor(nc, k, a)
        end_stage(nc, sems)


def segment_weights(nc, k, a):
    DK, HALF = 8, P // 2
    with nc.Block() as block:
        @block.sync
        def _(sp):
            for j, w in enumerate((a["L1_attn_a_Wq"], a["L1_attn_a_Wk"], a["L1_attn_a_Wv"])):
                sp.dma_start(k.sg_w[:, j, :], w).then_inc(k.sw_in, 16)
            sp.wait_ge(k.sw_zero, 1)
            for seg in range(2):
                for half in range(2):
                    sp.dma_start(k.sg_wo[seg * HALF:(seg + 1) * HALF, seg, half, :],
                                 a["L1_attn_a_Wo"][half * HALF:(half + 1) * HALF, :]).then_inc(k.sw_in, 16)

        @block.vector
        def _(dve):
            nc.vector.memset(k.sg_wo, 0.0).then_inc(k.sw_zero, 1)
            nc.vector.tensor_scalar(k.sg_bq, k.vec("bq"), DK ** -0.5, None, ALU.mult)

        @block.gpsimd
        def _(pool):
            nc.gpsimd.memset(k.sg_mask, 1.0).then_inc(k.sg_const, 1)
            pool.wait_ge(k.sg_const, 1)
            nc.gpsimd.affine_select(out=k.sg_mask, in_=k.sg_mask, compare_op=ALU.is_ge, fill=0.0, base=0,
                                    pattern=[[-DK, 8], [-HALF, 2]], channel_multiplier=1).then_inc(k.sg_const, 1)
            pool.wait_ge(k.sg_const, 2)
            nc.gpsimd.affine_select(out=k.sg_mask, in_=k.sg_mask, compare_op=ALU.is_ge, fill=0.0, base=DK - 1,
                                    pattern=[[DK, 8], [HALF, 2]], channel_multiplier=-1).then_inc(k.sg_const, 1)


def segments(nc, k, a):
    DK, SEG, PAD, UNITS = 8, 64, 2, 4
    NSEG = L // SEG
    STRIDE = NSEG + PAD
    TOTAL = B * STRIDE + PAD + 1
    TURNS = B * NSEG // UNITS
    TB = NSEG // UNITS
    HALF = P // 2
    take = [0]

    def part(n):
        take[0] += n
        return k.arena[:, take[0] - n:take[0]]

    qT = k.N[:, 0:NT]
    pr = [k.Y[:, i * 8 * P:(i + 1) * 8 * P] for i in range(4)]
    kv = part(2 * TOTAL * SEG).rearrange("p (a s n) -> p a s n", a=2, n=SEG)
    qm = [part(8 * P) for _ in range(4)]
    kvc = [part(2 * P).rearrange("p (a n) -> p a n", a=2) for _ in range(4)]
    vt = [part(2 * P).rearrange("p (s n) -> p s n", s=2) for _ in range(2)]
    pT = [part(8 * P) for _ in range(2)]
    mx = [part(40) for _ in range(2)]
    sm = [part(40) for _ in range(4)]
    wt = part(40)
    o, oT = part(P), part(P)

    def split(v, slots):
        v = v.rearrange("p (h n) -> p h n", h=slots)
        return v[:, :, 0:SEG], v[:, :, SEG:2 * SEG].rearrange("p h (g n) -> p h g n", n=16)

    def spread(v, slots):
        return v.rearrange("p (h g) -> p h g", h=slots)[:, :, :, None].to_broadcast([P, slots, 4, 16])

    zeros = lambda v: v[:, 0:B * STRIDE, :].rearrange("p (b s) n -> p b (s n)", b=B)[:, :, 0:PAD * SEG]

    def done(s, n):
        return n + (1 + PRIMED.get(s, 0))

    with nc.Block() as block:
        @block.tensor
        def _(pe):
            pe.wait_ge(k.sw_in, 7 * 16)
            with pe.Fori(0, B) as b:
                for i in range(6):
                    pe.wait_ge(k.sg_took, b * 6 + (i + 1))
                    nc.tensor.matmul(k.bank[i][:], k.sg_w[:, i % 3, :], k.Y[:, bass.ds(b * L + i // 3 * CH, CH)],
                                     start=True, stop=True).then_inc(k.sg_proj, 1)

        @block.scalar
        def _(act):
            with act.Fori(0, B) as b:
                for i in range(6):
                    c, j = i // 3, i % 3
                    act.wait_ge(k.sg_proj, b * 6 + (i + 1))
                    if j == 0:
                        dst = qT[:, bass.ds(b * L + c * CH, CH)]
                    else:
                        dst = kv[:, j - 1, bass.ds(b * STRIDE + PAD + c * (CH // SEG), CH // SEG), :].rearrange("p s n -> p (s n)")
                    nc.scalar.activation(dst, k.bank[i][:], ACT.Identity, bias=(k.sg_bq, k.vec("bk"), k.vec("bv"))[j],
                                         scale=(DK ** -0.5, 1.0, 1.0)[j]).then_inc(k.sg_took, 1)

        @block.gpsimd
        def _(pool):
            for j in range(2):
                nc.gpsimd.memset(zeros(kv[:, j]), 0.0)
                nc.gpsimd.memset(kv[:, j, B * STRIDE:, :], 0.0)
            nc.gpsimd.memset(wt[:, 0:8], 1.0)
            nc.gpsimd.memset(wt[:, 8:40], 0.25)

    def there(at, i):
        return at is None or 0 <= at + i < TURNS * UNITS

    def run(eng, turn):
        turn(0, 0)
        turn(1, UNITS)
        with eng.Fori(2, TURNS) as u:
            turn(u, None)
        turn(TURNS, TURNS * UNITS)

    STEPS = UNITS + 2

    with nc.Block() as block:
        @block.tensor
        def _(pe):
            def scores(n, i):
                pe.wait_ge(k.sg_fill, n + 1)
                pe.wait_ge(k.sg_kv, n + 1)
                pe.wait_ge(k.sg_arg, n + 1)
                for p in range(8):
                    op = nc.tensor.matmul(k.bank[2 * (i % 2) + p // 4][:, (p % 4) * P:(p % 4 + 1) * P],
                                          qm[i % 4][:, p * P:(p + 1) * P], kvc[i % 4][:, 0, :], start=True, stop=True)
                op.then_inc(k.sg_score, 1)

            def values(n, T, i):
                pe.wait_ge(k.sg_kv, n + 1)
                pe.wait_ge(k.sg_x, T + 1)
                for s in range(2):
                    op = nc.tensor.transpose(k.bank[7][:, s * P:(s + 1) * P], kvc[(i - 1 + s) % 4][:, 1, :], k.ident[:])
                op.then_inc(k.sg_vT, 1)

            def turned(n, i):
                pe.wait_ge(k.sg_mul, n + 1)
                for q in range(2):
                    pe.wait_ge(k.sg_pT, n * 2 + (q + 1))
                    for p in range(4):
                        op = nc.tensor.transpose(k.bank[4 + q][:, p * P:(p + 1) * P], pr[i % 4][:, (4 * q + p) * P:(4 * q + p + 1) * P], k.ident[:])
                    op.then_inc(k.sg_turned, 1)

            def weighed(n, T, i):
                s = i % 2
                pe.wait_ge(k.sg_pT, n * 2 + (2 + PRIMED["sg_pT"]))
                if s == 0:
                    pe.wait_ge(k.sg_vt, T + 1)
                    pe.wait_ge(k.sg_o, T + 1)
                for p in range(8):
                    out = k.bank[6][:, s * P:(s + 1) * P].rearrange("p (h n) -> p h n", h=2)[:, :, p * DK:(p + 1) * DK]
                    v = vt[i // 2 % 2][:, s, :].rearrange("p (h n) -> p h n", h=2)[:, :, p * DK:(p + 1) * DK]
                    op = nc.tensor.matmul(out, pT[s][:, p * P:(p + 1) * P], v, start=True, stop=True)
                op.then_inc(k.sg_pv, 1)

            def heads(T):
                pe.wait_ge(k.sg_o, done("sg_o", T))
                nc.tensor.transpose(k.bank[7][:, 2 * P:3 * P], o, k.ident[:]).then_inc(k.sg_oturn, 1)

            def output(T):
                pe.wait_ge(k.sg_oT, T + 1)
                for s in range(2):
                    for h in range(2):
                        op = nc.tensor.matmul(k.bank[7][:, 3 * P + s * HALF:3 * P + (s + 1) * HALF], k.sg_wo[:, s, h, :],
                                              oT[:, h * HALF:(h + 1) * HALF], start=(h == 0), stop=(h == 1))
                op.then_inc(k.sg_out, 1)

            def turn(u, at):
                for i in range(UNITS if at != TURNS * UNITS else STEPS):
                    n, T = u * UNITS, u * 2
                    if there(at, i):
                        scores(n + i, i)
                    if i % 2 == 0 and there(at, i - 6):
                        if there(at, i - 1):
                            pe.wait_ge(k.sg_vt, T + i // 2)
                        else:
                            pe.wait_ge(k.sg_x, T + (i // 2 - 3 + PRIMED["sg_x"]))
                        heads(T + (i // 2 - 3))
                    if there(at, i - 3):
                        turned(n + (i - 3), i - 3)
                    if there(at, i - 4):
                        weighed(n + (i - 4), T + (i - 4) // 2, i - 4)
                    if i % 2 == 0 and there(at, i - 6):
                        output(T + (i // 2 - 3))
                    if i % 2 == 1 and there(at, i):
                        if at is not None and at + i > 1:
                            pe.wait_ge(k.sg_vt, T + i // 2)
                        values(n + i, T + i // 2, i)

            run(pe, turn)

        @block.scalar
        def _(act):
            act.preload_act_table_set("exp_and_others")

            def values(T, i):
                act.wait_ge(k.sg_vT, T + (1 + PRIMED["sg_vT"]))
                nc.scalar.activation(vt[i // 2 % 2].rearrange("p s n -> p (s n)"), k.bank[7][:, 0:2 * P], ACT.Copy).then_inc(k.sg_vt, 1)

            def turned(n, i):
                for q in range(2):
                    act.wait_ge(k.sg_turned, n * 2 + (q + 1))
                    nc.scalar.activation(pT[i % 2][:, q * 4 * P:(q + 1) * 4 * P], k.bank[4 + q][:], ACT.Copy).then_inc(k.sg_pT, 1)

            def exp(n, i):
                act.wait_ge(k.sg_arg, done("sg_arg", n))
                nc.scalar.activation(pr[i % 4], pr[i % 4], ACT.Exp).then_inc(k.sg_exp, 1)

            def heads(T):
                act.wait_ge(k.sg_pv, T * 2 + 2)
                for h in range(2):
                    rows = slice(h * HALF, (h + 1) * HALF)
                    src = k.bank[6][rows, 0:2 * P].rearrange("p (s h n) -> p s h n", s=2, h=2)[:, :, h, :]
                    op = nc.scalar.activation(o[rows].rearrange("p (s n) -> p s n", s=2), src, ACT.Copy)
                op.then_inc(k.sg_o, 1)

            def heads_turned(T):
                act.wait_ge(k.sg_oturn, T + 1)
                nc.scalar.activation(oT, k.bank[7][:, 2 * P:3 * P], ACT.Copy).then_inc(k.sg_oT, 1)

            def gather(b, t, i):
                first = b * STRIDE + t * UNITS + i
                n = (b * TB + t) * UNITS + i
                wait_apart(act, k, k.sg_score, n + 1)
                wait_apart(act, k, k.sg_vT, (b * TB + t) * 2 + (i // 2 + 1))
                nc.scalar.activation(kvc[i][:, :, 0:SEG], kv[:, :, bass.ds(first + PAD, 1), :].rearrange("p a o n -> p a (o n)"), ACT.Copy)
                for j in range(2):
                    around = kv[:, j, bass.ds(first, 6), :].rearrange("p (side three) (n f) -> p side (three n) f", three=3, f=4)
                    op = nc.scalar.activation(kvc[i][:, j, SEG:].rearrange("p (side n) -> p side n", side=2), around[:, :, 0:2 * SEG // 4, 0], ACT.Copy)
                op.then_inc(k.sg_kv, 1)

            def turn(b, t, at):
                n, T = (b * TB + t) * UNITS, (b * TB + t) * 2
                for i in range(UNITS if at != TURNS * UNITS else STEPS + 2):
                    m = i - 2
                    if m % 2 == 0 and there(at, m - 6):
                        heads_turned(T + (m // 2 - 3))
                    if there(at, m - 3):
                        turned(n + (m - 3), m - 3)
                    if there(at, m):
                        exp(n + m, m)
                    if m % 2 == 1 and there(at, m - 5):
                        heads(T + (m // 2 - 2))
                    if m % 2 == 1 and there(at, m):
                        values(T + m // 2, m)
                    if there(at, i):
                        gather(b, t, i)

            turn(0, 0, 0)
            turn(0, 1, UNITS)
            with act.Fori(2, TB) as t:
                turn(0, t, None)
            with act.Fori(1, B) as b:
                with act.Fori(0, TB) as t:
                    turn(b, t, None)
            turn(B, 0, TURNS * UNITS)

        @block.vector
        def _(dve):
            def shift(n, i):
                s = i % 2
                dve.wait_ge(k.sg_score, done("sg_score", n))
                for q in range(2):
                    own, others = split(k.bank[2 * s + q][:], 4)
                    nc.vector.tensor_reduce(mx[s][:, 4 * q:4 * q + 4], own, AX.X, ALU.max)
                    op = nc.vector.tensor_reduce(mx[s][:, 8 + 16 * q:24 + 16 * q], others, AX.X, ALU.max)
                op.then_inc(k.sg_step, 1)
                dve.wait_ge(k.sg_step, n + 1)
                for q in range(2):
                    own, others = split(k.bank[2 * s + q][:], 4)
                    to_own, to_others = split(pr[i % 4][:, q * 4 * P:(q + 1) * 4 * P], 4)
                    nc.vector.tensor_tensor(to_own, own, mx[s][:, 4 * q:4 * q + 4, None].to_broadcast([P, 4, SEG]), ALU.subtract)
                    op = nc.vector.tensor_tensor(to_others, others, spread(mx[s][:, 8 + 16 * q:24 + 16 * q], 4), ALU.subtract)
                op.then_inc(k.sg_arg, 1)

            def weight(n, i):
                own, others = split(pr[i % 4], 8)
                dve.wait_ge(k.sg_exp, n + 1)
                nc.vector.tensor_reduce(sm[i % 4][:, 0:8], own, AX.X, ALU.add)
                nc.vector.tensor_reduce(sm[i % 4][:, 8:40], others, AX.X, ALU.add).then_inc(k.sg_wstep, 1)
                dve.wait_ge(k.sg_wstep, n * 2 + 1)
                nc.vector.reciprocal(sm[i % 4], sm[i % 4]).then_inc(k.sg_wstep, 1)
                dve.wait_ge(k.sg_wstep, n * 2 + 2)
                nc.vector.tensor_tensor(sm[i % 4], sm[i % 4], wt, ALU.mult).then_inc(k.sg_weight, 1)

            def add(T, column):
                at = bass.ds(column, P)
                dve.wait_ge(k.sg_out, T + 1)
                nc.vector.scalar_tensor_tensor(k.X[:, at], k.bank[7][:, 3 * P:4 * P], k.vec("bo"), k.X[:, at], ALU.add, ALU.add).then_inc(k.sg_x, 1)

            def turn(u, at):
                for i in range(UNITS if at != TURNS * UNITS else STEPS):
                    n, T = u * UNITS, u * 2
                    if i % 2 == 1 and there(at, i - 7):
                        add(T + (i // 2 - 3), u * (2 * P) + (i // 2 - 3) * P)
                    if there(at, i):
                        shift(n + i, i)
                    if there(at, i - 1):
                        weight(n + (i - 1), i - 1)

            run(dve, turn)

        @block.gpsimd
        def _(pool):
            def mask(n, i, column):
                wait_apart(pool, k, k.sg_score, n + 1)
                nc.gpsimd.tensor_tensor(qm[i].rearrange("p (h n) -> p h n", h=16), qT[:, None, bass.ds(column, SEG)].to_broadcast([P, 16, SEG]),
                                        k.sg_mask.rearrange("p a b -> p (a b)")[:, :, None].to_broadcast([P, 16, SEG]), ALU.mult).then_inc(k.sg_fill, 1)

            def weigh(n, i):
                own, others = split(pr[i % 4], 8)
                pool.wait_ge(k.sg_weight, n + 1)
                nc.gpsimd.tensor_tensor(own, own, sm[i % 4][:, 0:8, None].to_broadcast([P, 8, SEG]), ALU.mult)
                nc.gpsimd.tensor_tensor(others, others, spread(sm[i % 4][:, 8:40], 8), ALU.mult).then_inc(k.sg_mul, 1)

            def turn(u, at):
                for i in range(UNITS if at != TURNS * UNITS else STEPS):
                    if there(at, i):
                        mask(u * UNITS + i, i, u * (UNITS * SEG) + i * SEG)
                    if there(at, i - 3):
                        weigh(u * UNITS + (i - 3), i - 3)

            run(pool, turn)


def stage_segments(nc, k, a, X, Y):
    k.ln(X, Y)
    with ExitStack() as ctx:
        sems = begin_stage(nc, ctx, SEGMENT_SEMS)
        (k.sw_in, k.sw_zero, k.sg_took, k.sg_proj, k.sg_fill, k.sg_kv, k.sg_arg, k.sg_score,
         k.sg_x, k.sg_vT, k.sg_mul, k.sg_pT, k.sg_turned, k.sg_vt, k.sg_o, k.sg_pv, k.sg_oturn, k.sg_oT, k.sg_out,
         k.sg_const, k.sg_weight, k.sg_exp, k.sg_step, k.sg_wstep) = sems
        segment_weights(nc, k, a)
        segments(nc, k, a)
        end_stage(nc, sems)


SEMS = ["passed", "weights_in", "ident_zero", "ident_one", "consts_set", "vrows_set", "vecs_in", "vecs_turned", "vecs_ready",
        "x_turned", "x_ready", "x_ready_a", "wt_turned", "wt_ready", "ln_centered", "ln_squared", "ln_var", "ln_logs", "ln_rstd",
        "ln_scaled", "ln_biased", "ln_out", "y_turned", "y_rows", "y_rows_a", "stored", "wA_in", "moe_w_in", "pa_prod", "pa_added",
        "ff_w_in", "ff_zero", "ff_const", "ff_spread", "ff_spread16", "ff_hot0", "ff_mix1", "ff_mix2", "ff_mix", "ff_up",
        "ff_u", "ff_h", "ff_hid", "ff_score", "ff_step", "ff_hot", "ff_hotT", "ff_hot16", "ff_spreads", "ff_masked", "ff_out",
        "ff_z", "lr_w_in", "lr_prod", "lr_read", "lr_init", "lr_sc", "lr_den", "lr_ln", "lr_rden", "lr_step", "lr_x", "tw_in",
        "tw_turned", "tw_zero", "tw_copied", "tw_prod", "tr_ys", "tr_z", "tr_th", "tr_g", "tr_step", "tr_lp", "tr_turned",
        "tr_lpT", "tr_out", "tr_x"]
MOE_SEMS = ["mix_diff", "mix_in", "kvr", "kvr_out", "wkv_w", "wkv_arg", "wkv_exp", "wkv_den", "wkv_ln", "wkv_rden", "wkv_init",
            "wkv_e2bv", "wkv_e2v", "wkv_v", "wkv_step", "rt_prod", "rt_copied", "rt_turned", "rt_parts", "rt_wT", "rt_back",
            "rt_step", "rt_exps", "rt_const", "rt_sel", "ex_diff", "ex_mix", "ex_r", "ex_v", "ex_tanh", "ex_added", "ex_gate",
            "ex_tw", "ex_weighed", "ex_up", "ex_relu", "ex_sq", "ex_y"]
FAVOR_SEMS = ["fw_in", "fw_mask", "fw_turned", "fw_wide", "fw_copied", "fw_prod", "fv_ys", "fv_proj", "fv_sq", "fv_va", "fv_max",
              "fv_off", "fv_arg", "fv_exp", "fv_phi", "fv_used", "fv_kv", "fv_exT", "fv_sums", "fv_o", "fv_rd",
              "fv_back", "fv_oT", "fv_out", "fv_x"]
SEGMENT_SEMS = ["sw_in", "sw_zero", "sg_took", "sg_proj", "sg_fill", "sg_kv", "sg_arg", "sg_score", "sg_x", "sg_vT",
                "sg_mul", "sg_pT", "sg_turned", "sg_vt", "sg_o", "sg_pv", "sg_oturn", "sg_oT", "sg_out", "sg_const", "sg_weight",
                "sg_exp", "sg_step", "sg_wstep"]
PRIMED = {"ln_out": 4, "pa_added": 4, "rt_copied": 4, "kvr": 6, "kvr_out": 6,
          "ex_r": 4, "ex_relu": 2, "ex_v": 2, "ex_gate": 2, "ex_added": 2, "ex_tanh": 1, "ex_weighed": 1, "wkv_e2v": 1, "ex_sq": 1,
          "ff_h": 6, "ff_out": 1, "ff_hid": 3, "ff_masked": 6, "ff_z": 2, "lr_read": 6,
          "tr_th": 2, "tr_lpT": 1, "tr_x": 2, "tr_z": 2, "tr_g": 1, "tr_turned": 2, "tr_out": 2,
          "fv_proj": 2, "fv_sq": 2, "fv_arg": 2, "fv_used": 4, "fv_va": 2, "fv_kv": 1, "fv_exT": 1, "fv_o": 1, "fv_sums": 2,
          "fv_oT": 1, "fv_x": 1, "fv_out": 1,
          "sg_x": 3, "sg_arg": 2, "sg_pT": 2, "sg_o": 1, "sg_score": 4, "sg_vT": 2, "sg_took": 6}


def load(nc, k, a):
    row = lambda v: v.rearrange("(o n) -> o n", o=1)
    table = [
        ("ln1_g", row(a["L0_attn_a_ln1_g"])), ("ln1_b", row(a["L0_attn_a_ln1_b"])),
        ("ln2_g", row(a["L0_attn_a_ln2_g"])), ("ln2_b", row(a["L0_attn_a_ln2_b"])),
        ("mu_k", row(a["L0_attn_a_tm_mu_k"])), ("mu_v", row(a["L0_attn_a_tm_mu_v"])), ("mu_r", row(a["L0_attn_a_tm_mu_r"])),
        ("decay", row(a["L0_attn_a_time_decay"])), ("first", row(a["L0_attn_a_time_first"])),
        ("cm_k0", a["L0_attn_a_cm_mu_k"]), ("cm_r0", a["L0_attn_a_cm_mu_r"]),
        ("favor_bo", row(a["L0_attn_b_bo"])), ("mix0", a["L0_ffn_mix_kernel"]),
        ("gamma", row(a["L0_ffn_gamma"])), ("beta", row(a["L0_ffn_beta"])),
        ("bq", row(a["L1_attn_a_bq"])), ("bk", row(a["L1_attn_a_bk"])), ("bv", row(a["L1_attn_a_bv"])), ("bo", row(a["L1_attn_a_bo"])),
        ("br", a["L1_attn_b_b_rkv"].rearrange("(o n) -> o n", n=P)), ("lru_bo", row(a["L1_attn_b_b_o"])),
        ("nu_log", row(a["L1_attn_b_nu_log"])), ("gamma_log", row(a["L1_attn_b_gamma_log"])),
        ("wout_b", row(a["L1_ffn_Wout_b"])), ("b1_0", a["L0_ffn_b1"].rearrange("(o q) m -> o (q m)", q=3)),
        ("bo1", row(a["L0_ffn_bo1"]))]
    xv = k.X[:].rearrange("d (p t) -> d t p", t=NT // P)

    def vectors(eng, first):
        eng.wait_ge(k.vrows_set, 1)
        for name, src in table[first::2]:
            n, width = src.shape
            eng.dma_start(k.vrows[VI[name]:VI[name] + n, 0:width], src).then_inc(k.vecs_in, 16)

    with nc.Block() as block:
        @block.sync
        def _(sp):
            xin = a["L0_attn_a_x"].rearrange("b l d -> (b l) d").rearrange("(p t) d -> p t d", t=NT // P)
            for q in range(4):
                sp.dma_start(k.rows[:, 8 * q:8 * q + 8, :], xin[:, 8 * q:8 * q + 8, :]).then_inc(k.loaded[q], 16)
            vectors(sp, 1)

        @block.gpsimd
        def _(pool):
            nc.gpsimd.memset(k.ident[:], 0.0).then_inc(k.ident_zero, 1)
            pool.wait_ge(k.ident_zero, 1)
            nc.gpsimd.affine_select(out=k.ident[:], in_=k.ident[:], compare_op=ALU.not_equal, fill=1.0, base=0,
                                    pattern=[[-1, P]], channel_multiplier=1).then_inc(k.ident_one, 1)
            nc.gpsimd.memset(k.mean[:], 1.0 / P).then_inc(k.consts_set, 1)
            nc.gpsimd.memset(k.eps[:], EPS_LN).then_inc(k.consts_set, 1)
            for b in range(B):
                nc.gpsimd.memset(k.N[:, b * PADL:b * PADL + 1], 0.0).then_inc(k.consts_set, 1)
                nc.gpsimd.memset(k.N[:, (b + 1) * PADL - 1:(b + 1) * PADL], 0.0).then_inc(k.consts_set, 1)

        @block.scalar
        def _(act):
            vectors(act, 0)

            for q in range(1, 8, 2):
                act.wait_ge(k.x_turned, q + 1)
                nc.scalar.activation(xv[:, 4 * q:4 * q + 4, :], k.bank[q % 4][:].rearrange("d (t p) -> d t p", t=4), ACT.Copy).then_inc(k.x_ready_a, 1)

        @block.tensor
        def _(pe):
            pe.wait_ge(k.ident_one, 1)
            for q in range(8):
                pe.wait_ge(k.loaded[q // 2], 16)
                if q >= 4:
                    pe.wait_ge((k.x_ready, k.x_ready_a)[q % 2], (q - 4) // 2 + 1)
                for t in range(4):
                    op = nc.tensor.transpose(k.bank[q % 4][:, t * P:(t + 1) * P], k.rows[:, 4 * q + t, :], k.ident[:])
                op.then_inc(k.x_turned, 1)
            pe.wait_ge(k.vecs_in, 16 * len(table))
            nc.tensor.transpose(k.bank[7][:, 0:len(VROWS)], k.vrows[:], k.ident[0:len(VROWS), 0:len(VROWS)]).then_inc(k.vecs_turned, 1)

        @block.vector
        def _(dve):
            for name, semaphore in zip(SEMS, k.sems):
                if name in PRIMED:
                    dve.sem_inc(semaphore, PRIMED[name])
            nc.vector.memset(k.vrows[:], 1.0).then_inc(k.vrows_set, 1)
            dve.wait_ge(k.ident_one, 1)
            dve.wait_ge(k.consts_set, 1)
            nc.vector.tensor_tensor(k.center[:], k.ident[:], k.mean[:], ALU.subtract).then_inc(k.consts_set, 1)
            for q in range(0, 8, 2):
                dve.wait_ge(k.x_turned, q + 1)
                nc.vector.tensor_copy(xv[:, 4 * q:4 * q + 4, :], k.bank[q % 4][:].rearrange("d (t p) -> d t p", t=4)).then_inc(k.x_ready, 1)
            dve.wait_ge(k.vecs_turned, 1)
            nc.vector.tensor_copy(k.vecs[:], k.bank[7][:, 0:len(VROWS)]).then_inc(k.vecs_ready, 1)


def store(nc, k, out):
    with nc.Block() as block:
        @block.tensor
        def _(pe):
            xv = k.X[:].rearrange("d (p t) -> d t p", t=NT // P)
            for q in range(8):
                if q >= 4:
                    pe.wait_ge((k.y_rows, k.y_rows_a)[q % 2], (q - 4) // 2 + 1)
                for t in range(4):
                    op = nc.tensor.transpose(k.bank[q % 4][:, t * P:(t + 1) * P], xv[:, 4 * q + t, :], k.ident[:])
                op.then_inc(k.y_turned, 1)

        @block.vector
        def _(dve):
            for q in range(0, 8, 2):
                dve.wait_ge(k.y_turned, q + 1)
                nc.vector.tensor_copy(k.rows[:, 4 * q:4 * q + 4, :],
                                      k.bank[q % 4][:].rearrange("p (t d) -> p t d", t=4)).then_inc(k.y_rows, 1)

        @block.scalar
        def _(act):
            for q in range(1, 8, 2):
                act.wait_ge(k.y_turned, q + 1)
                nc.scalar.activation(k.rows[:, 4 * q:4 * q + 4, :],
                                     k.bank[q % 4][:].rearrange("p (t d) -> p t d", t=4), ACT.Copy).then_inc(k.y_rows_a, 1)

        @block.sync
        def _(sp):
            yout = out.rearrange("b l d -> (b l) d").rearrange("(p t) d -> p t d", t=NT // P)
            for q in range(4):
                sp.wait_ge(k.y_rows, q + 1)
                sp.wait_ge(k.y_rows_a, q + 1)
                sp.dma_start(yout[:, 8 * q:8 * q + 8, :], k.rows[:, 8 * q:8 * q + 8, :]).then_inc(k.stored, 16)
            sp.wait_ge(k.stored, 4 * 16)


def build(nc, a, out):
    with ExitStack() as ctx:
        def sb(name, shape, dt=F32):
            return ctx.enter_context(nc.sbuf_tensor(name, shape, dt))

        k = Chip()
        k.sems = [ctx.enter_context(nc.semaphore(name)) for name in SEMS]
        (k.passed, k.weights_in, k.ident_zero, k.ident_one, k.consts_set, k.vrows_set, k.vecs_in, k.vecs_turned,
         k.vecs_ready, k.x_turned, k.x_ready, k.x_ready_a, k.wt_turned, k.wt_ready, k.ln_centered, k.ln_squared, k.ln_var,
         k.ln_logs, k.ln_rstd, k.ln_scaled, k.ln_biased, k.ln_out, k.y_turned, k.y_rows, k.y_rows_a, k.stored, k.wA_in, k.moe_w_in,
         k.pa_prod, k.pa_added, k.ff_w_in, k.ff_zero, k.ff_const, k.ff_spread, k.ff_spread16, k.ff_hot0, k.ff_mix1,
         k.ff_mix2, k.ff_mix, k.ff_up, k.ff_u, k.ff_h, k.ff_hid, k.ff_score, k.ff_step, k.ff_hot, k.ff_hotT,
         k.ff_hot16, k.ff_spreads, k.ff_masked, k.ff_out, k.ff_z, k.lr_w_in, k.lr_prod, k.lr_read, k.lr_init, k.lr_sc,
         k.lr_den, k.lr_ln, k.lr_rden, k.lr_step, k.lr_x, k.tw_in, k.tw_turned, k.tw_zero, k.tw_copied, k.tw_prod,
         k.tr_ys, k.tr_z, k.tr_th, k.tr_g, k.tr_step, k.tr_lp, k.tr_turned, k.tr_lpT, k.tr_out, k.tr_x) = k.sems
        k.loaded = [ctx.enter_context(nc.semaphore(f"loaded{q}")) for q in range(4)]
        k.bank = [ctx.enter_context(nc.psum_tensor(f"bank{i}", [P, CH], F32)) for i in range(8)]
        k.ident, k.mean, k.center, k.eps = sb("ident", [P, P]), sb("mean", [P, P]), sb("center", [P, P]), sb("eps", [P, 1])
        k.vrows, k.vecs = sb("vrows", [len(VROWS), P]), sb("vecs", [P, len(VROWS)])
        k.vec = lambda name, n=P: k.vecs[0:n, VI[name]:VI[name] + 1]
        k.X, k.Y, k.N = sb("X", [P, NT]), sb("Y", [P, NT]), sb("N", [P, B * PADL])
        k.ln_sq, k.ln_std = sb("ln_sq", [P, W, CH]), sb("ln_std", [P, W, CH])
        k.ln_scaled_0 = k.ln_biased_0 = 0
        k.arena = sb("arena", [P, 5 * NT])
        k.big = [k.arena[:, i * NT:(i + 1) * NT] for i in range(5)]
        k.rows = k.big[0].rearrange("p (t d) -> p t d", d=P)
        k.ln_calls = k.pa_calls = k.ff_calls = k.tr_calls = 0
        k.weights = sb("weights", [P, 5120])
        k.eWk = k.weights[:, 0:2048].rearrange("p (e f) -> p e f", e=E)
        k.eWv = k.weights[:, 2048:4096].rearrange("p (e h d) -> p e h d", e=E, h=2)
        k.eWr = k.weights[:, 4096:5120].rearrange("p (e g) -> p e g", e=E)
        k.wA, k.router = sb("wA", [P, 4, P]), sb("router", [P, E])
        k.diff, k.mixed = sb("diff", [P, 2, CH]), sb("mixed", [P, 2, 3, CH])
        k.wdec, k.wneg = sb("wdec", [P, 1]), sb("wneg", [P, 1])
        mixed = k.mixed[:].rearrange("p a j n -> p (a j n)")
        k.pp = k.ln_sq[:].rearrange("p a n -> p (a n)")[:, 0:L + 1]
        k.aa = k.ln_std[:].rearrange("p a n -> p (a n)")[:, 0:L + 1]
        k.bb, k.lam = mixed[:, 0:L + 1], mixed[:, L + 1:2 * L + 1]
        k.logitT = k.big[3][0:E, :]
        k.twT = k.big[4][:, 0:NT // 2].bitcast(BF16)
        view = lambda j, n=256: k.big[0][:, j * 256:j * 256 + n].rearrange("p (t e) -> p t e", e=E)
        k.rt_logit, k.rt_exp, k.rt_w, k.rt_one, k.rt_cand, k.rt_two = (view(j) for j in range(6))
        k.rt_part = k.big[0][:, 6 * 256:9 * 256].rearrange("p (t e s) -> p t e s", e=E, s=3)
        k.rt_bf = k.big[0][:, 9 * 256:9 * 256 + 128].bitcast(BF16).rearrange("p (t e) -> p t e", e=E)
        k.rt_m, k.rt_c, k.rank = sb("rt_m", [P, NT // P]), sb("rt_c", [P, NT // P]), sb("rank", [P, E])
        k.sel = sb("sel", [P, E, P], BF16)
        ffw = sb("ffw", [P, 6 * P + DM])
        k.W1 = ffw[:, 0:3 * P].rearrange("p (g n) -> p g n", g=3)
        k.W2 = ffw[:, 3 * P:6 * P].rearrange("p (g n) -> p g n", g=3)
        k.Wo1 = ffw[:, 6 * P:6 * P + DM]
        k.Wo2, k.prank = sb("Wo2", [DM + 1, NP]), sb("prank", [P, NP])
        k.spread = k.big[4][:, 0:3 * P].rearrange("p (g n) -> p g n", g=3)
        k.spread16 = sb("spread16", [P, 3, P], BF16)
        k.lruw = k.weights[:, 0:4 * P]
        k.gates = k.weights[:, 4 * P:6 * P]
        k.leaves = k.weights[:, 6 * P:8 * P].rearrange("p (h d) -> p h d", h=2)
        k.lr_nu, k.lr_lam, k.lr_own, k.lr_nbr = (sb(n, [P, 1]) for n in ("lr_nu", "lr_lam", "lr_own", "lr_nbr"))
        k.fv_wT = k.weights[:, 0:4 * P]
        k.fv_feat = k.weights[:, 4 * P:12 * P].rearrange("p (j n) -> p j n", j=2)
        k.fv_own, k.eps6 = k.weights[:, 12 * P:12 * P + 4], sb("eps6", [P, 1])
        k.sg_w = k.weights[:, 0:4 * P].rearrange("p (j n) -> p j n", j=4)
        k.sg_wo = k.weights[:, 4 * P:8 * P].rearrange("p (s h n) -> p s h n", s=2, h=2)
        k.sg_bq = k.weights[:, 8 * P:8 * P + 1]
        k.sg_mask = k.weights[:, 9 * P:9 * P + 16].rearrange("p (s h) -> p s h", s=8)
        k.vb = k.diff[:].rearrange("p a n -> p (a n)")

        def ln(src, dst, **kw):
            layernorm(nc, k, k.ln_calls, src, dst, **kw)
            k.ln_calls += 1

        k.ln = ln
        X, Y = (lambda it, c: plain(k.X, it, c)), (lambda it, c: plain(k.Y, it, c))
        load(nc, k, a)
        for st in STAGES:
            STAGE[st](nc, k, a, X, Y)
        store(nc, k, out)


STAGE = {"A": stage_rwkv, "B": stage_ffn, "C": stage_favor, "D": stage_ffn, "E": stage_segments, "F": stage_tree, "G": stage_lru, "H": stage_tree}
_OUTS = [((4, 1024, 128), 'float32')]


def kernel(**inputs):
    import numpy as _np
    import concourse.bacc as _bacc
    from concourse import mybir as _mybir
    from concourse.bass_utils import run_bass_kernel_spmd as _run

    nc = _bacc.Bacc("TRN2", target_bir_lowering=False, num_devices=1)
    arrays, args = {}, {}
    for name in inputs:
        a = _np.ascontiguousarray(inputs[name])
        arrays[f"in_{name}_dram"] = a
        args[name] = nc.dram_tensor(f"in_{name}_dram", a.shape, _mybir.dt.from_np(a.dtype), kind="ExternalInput").ap()
    outs = []
    for i, (shape, dtype) in enumerate(_OUTS):
        dt = _mybir.dt.from_np(_np.dtype(dtype))
        outs.append(nc.dram_tensor(f"out_{i}_dram", shape, dt, kind="ExternalOutput").ap())
    build(nc, args, outs[0])
    r = _run(nc, [arrays], core_ids=[0])
    return r.results[0]["out_0_dram"]
```

```python
from contextlib import ExitStack

import concourse.bass as bass
from concourse import mybir

STAGES = "ABCDEFGH"
ALU = mybir.AluOpType
ACT = mybir.ActivationFunctionType
F32 = mybir.dt.float32
BF16 = mybir.dt.bfloat16
AX = mybir.AxisListType

P = 128
B, L = 4, 1024
NT = B * L
CH = 512
NCH = NT // CH
W = 4
PADL = L + 2
E = 8
NP = 9
DM = 32
EPS_LN = 1e-5

VROWS = ["ln1_g", "ln1_b", "ln2_g", "ln2_b", "mu_k", "mu_v", "mu_r", "decay", "first"] \
    + [f"cm_k{e}" for e in range(E)] + [f"cm_r{e}" for e in range(E)] \
    + ["favor_bo", "mix0", "mix1", "mix2", "gamma", "beta", "bq", "bk", "bv", "bo", "br", "bkk", "bvv", "lru_bo",
       "nu_log", "gamma_log", "wout_b", "b1_0", "b1_1", "b1_2", "bo1"]
VI = {n: i for i, n in enumerate(VROWS)}


def wait_apart(eng, k, semaphore, value):
    eng.wait_ge(semaphore, value)
    eng.sem_inc(k.passed, 1)


class Chip:
    pass


def begin_stage(nc, ctx, names):
    sems = [ctx.enter_context(nc.semaphore(name)) for name in names]
    with nc.Block() as block:
        @block.vector
        def _(dve):
            for name, semaphore in zip(names, sems):
                if name in PRIMED:
                    dve.sem_inc(semaphore, PRIMED[name])
    return sems


def end_stage(nc, sems):
    with nc.Block() as block:
        @block.vector
        def _(dve):
            for semaphore in sems:
                dve.sem_clear(semaphore)


def plain(buf, it, c):
    return buf[:, bass.ds(it * (W * CH) + c * CH, CH)]


def padded(buf, it, c, shift=0):
    return buf[:, bass.ds(it * (W // 2 * PADL) + (c // 2) * PADL + 1 + (c % 2) * CH + shift, CH)]


def layernorm(nc, k, call, src, dst, gain=None, bias=None, residual=None, ahead=None):
    n0 = call * NCH
    with nc.Block() as block:
        if ahead is not None:
            ahead(block)

        @block.tensor
        def _(pe):
            with pe.Fori(0, NCH // W) as it:
                g = it * W + n0
                for c in range(W + 2):
                    if c < W:
                        pe.wait_ge(k.ln_out, g + (c + 1))
                        nc.tensor.matmul(k.bank[c][:], k.center[:], src(it, c), start=True, stop=True).then_inc(k.ln_centered, 1)
                    if c >= 2:
                        pe.wait_ge(k.ln_squared, g + (c - 1))
                        nc.tensor.matmul(k.bank[2 + c][:], k.mean[:], k.ln_sq[:, c - 2, :], start=True, stop=True).then_inc(k.ln_var, 1)

        @block.scalar
        def _(act):
            act.preload_act_table_set("natural_log_exp_and_others")
            with act.Fori(0, NCH // W) as it:
                g = it * W + n0
                def square(c):
                    act.wait_ge(k.ln_centered, g + (c + 1))
                    nc.scalar.activation(k.ln_sq[:, c, :], k.bank[c][:], ACT.Square).then_inc(k.ln_squared, 1)

                square(0)
                square(1)
                for c in range(W):
                    if c + 2 < W:
                        square(c + 2)
                    act.wait_ge(k.ln_var, g + (c + 1))
                    nc.scalar.activation(k.ln_std[:, c, :], k.bank[4 + c][:], ACT.Ln, bias=k.eps[:, 0:1]).then_inc(k.ln_logs, 1)
                    act.wait_ge(k.ln_logs, g + (c + 1))
                    nc.scalar.activation(k.ln_std[:, c, :], k.ln_std[:, c, :], ACT.Exp, scale=-0.5).then_inc(k.ln_rstd, 1)

        @block.vector
        def _(dve):
            with dve.Fori(0, NCH // W) as it:
                g = it * W + n0
                for c in range(W):
                    dve.wait_ge(k.ln_rstd, g + (c + 1))
                    out = dst(it, c) if residual is None else k.ln_sq[:, c, :]
                    op = nc.vector.tensor_tensor(out, k.bank[c][:], k.ln_std[:, c, :], ALU.mult)
                    if gain is not None:
                        op.then_inc(k.ln_scaled, 1)
                        dve.wait_ge(k.ln_scaled, (it * W + k.ln_scaled_0) + (c + 1))
                        op = nc.vector.tensor_scalar(out, out, k.vec(gain), k.vec(bias), ALU.mult, ALU.add)
                    if residual is not None:
                        op.then_inc(k.ln_biased, 1)
                        dve.wait_ge(k.ln_biased, (it * W + k.ln_biased_0) + (c + 1))
                        op = nc.vector.tensor_tensor(residual(it, c), residual(it, c), out, ALU.add)
                    op.then_inc(k.ln_out, 1)
    if gain is not None:
        k.ln_scaled_0 += NCH
    if residual is not None:
        k.ln_biased_0 += NCH


def rwkv_loads(k, a, block):
    @block.sync
    def _(sp):
        for j, w in enumerate((a["L0_attn_a_Wk"], a["L0_attn_a_Wv"], a["L0_attn_a_Wr"], a["L0_attn_a_Wo"])):
            sp.dma_start(k.wA[:, j, :], w).then_inc(k.wA_in, 16)
        sp.dma_start(k.router[:], a["L0_attn_a_router_w"]).then_inc(k.moe_w_in, 16)
        sp.dma_start(k.eWk[:], a["L0_attn_a_eWk"].rearrange("e d f -> d e f")).then_inc(k.moe_w_in, 16)
        sp.dma_start(k.eWv[:], a["L0_attn_a_eWv"].rearrange("e (h f) d -> f e h d", h=2)).then_inc(k.moe_w_in, 16)
        sp.dma_start(k.eWr[:], a["L0_attn_a_eWr"].rearrange("e d g -> d e g")).then_inc(k.moe_w_in, 16)


def rwkv_mix(nc, k, a):
    Wk, Wv, Wr, Wo = (k.wA[:, j, :] for j in range(4))
    K, V, R = k.big[0], k.big[1], k.big[2]
    with nc.Block() as block:
        @block.vector
        def _(dve):
            with dve.Fori(0, NCH // 2) as it:
                for c in range(2):
                    g = it * 2 + c
                    now = k.N[:, bass.ds(it * PADL + 1 + c * CH, CH)]
                    before = k.N[:, bass.ds(it * PADL + c * CH, CH)]
                    dve.wait_ge(k.kvr, g * 3 + 3)
                    nc.vector.tensor_tensor(k.diff[:, c, :], now, before, ALU.subtract).then_inc(k.mix_diff, 1)
                    dve.wait_ge(k.mix_diff, g + 1)
                    for j, mu in enumerate(("mu_k", "mu_v", "mu_r")):
                        nc.vector.scalar_tensor_tensor(k.mixed[:, c, j, :], k.diff[:, c, :], k.vec(mu), before,
                                                       ALU.mult, ALU.add).then_inc(k.mix_in, 1)

        @block.tensor
        def _(pe):
            pe.wait_ge(k.wA_in, 64)
            with pe.Fori(0, NCH // 2) as it:
                for c in range(2):
                    g = it * 2 + c
                    for j, w in enumerate((Wk, Wv, Wr)):
                        pe.wait_ge(k.mix_in, g * 3 + (j + 1))
                        pe.wait_ge(k.kvr_out, g * 3 + (j + 1))
                        op = nc.tensor.matmul(k.bank[3 * c + j][:], w, k.mixed[:, c, j, :], start=True, stop=True)
                        op.then_inc(k.kvr, 1)

        @block.scalar
        def _(act):
            with act.Fori(0, NCH // 2) as it:
                for c in range(2):
                    at = bass.ds(it * L + c * CH, CH)
                    for j in range(3):
                        act.wait_ge(k.kvr, it * 6 + (c * 3 + j + 1 + PRIMED["kvr"]))
                        dst = (K, V, R)[j]
                        nc.scalar.activation(dst[:, at], k.bank[3 * c + j][:], (ACT.Copy, ACT.Copy, ACT.Tanh)[j],
                                             scale=(1.0, 1.0, 0.5)[j]).then_inc(k.kvr_out, 1)


def wkv(nc, k, a):
    K, V, R = k.big[0], k.big[1], k.big[2]
    pp, aa, bb = k.pp, k.aa, k.bb
    t = [[k.big[3][:, j * L:(j + 1) * L] for j in range(4)],
         [k.N[:, j * PADL + 1:j * PADL + 1 + L] for j in range(4)]]
    u = [[k.big[4][:, (2 * s + j) * L:(2 * s + j + 1) * L] for j in range(2)] for s in range(2)]
    at = [slice(b * L, (b + 1) * L) for b in range(B)]
    with nc.Block() as block:
        @block.tensor
        def _(pe):
            for b in range(B):
                pe.wait_ge(k.wkv_out, b + 1)
                for c in range(2):
                    nc.tensor.matmul(k.bank[2 * b + c], k.wA[:, 3, :], R[:, b * L + c * CH:b * L + (c + 1) * CH],
                                     start=True, stop=True).then_inc(k.wkv_prod, 1)

        @block.scalar
        def _(act):
            act.preload_act_table_set("natural_log_exp_and_others")
            nc.scalar.activation(k.wdec[:], k.vec("decay"), ACT.Exp).then_inc(k.wkv_w, 1)

            def over(b):
                den = t[b % 2][0]
                act.wait_ge(k.wkv_den, b + 1)
                nc.scalar.activation(den, den, ACT.Ln).then_inc(k.wkv_ln, 1)
                act.wait_ge(k.wkv_ln, b + 1)
                nc.scalar.activation(den, den, ACT.Exp, scale=-1.0).then_inc(k.wkv_rden, 1)

            for b in range(B):
                e2b, e2, e1b, e1 = (t[b % 2][j] for j in (1, 3, 0, 2))
                for ready, n, buf in ((k.wkv_sub, 2 * b + 1, e2b), (k.wkv_arg, 2 * b + 1, e1b),
                                      (k.wkv_arg, 2 * b + 2, e2), (k.wkv_sub, 2 * b + 2, e1)):
                    act.wait_ge(ready, n)
                    nc.scalar.activation(buf, buf, ACT.Exp).then_inc(k.wkv_exp, 1)
                if b >= 1:
                    over(b - 1)
            over(B - 1)

        @block.gpsimd
        def _(pool):
            def arguments(b):
                tb = t[b % 2]
                pool.wait_ge(k.wkv_pp, b + 1)
                nc.gpsimd.tensor_tensor(tb[1], K[:, at[b]], pp[b % 2][:, 1:L + 1], ALU.subtract).then_inc(k.wkv_sub, 1)
                pool.wait_ge(k.wkv_arg, 2 * b + 2)
                nc.gpsimd.tensor_tensor(tb[2], pp[b % 2][:, 0:L], tb[2], ALU.subtract).then_inc(k.wkv_sub, 1)

            def products(b):
                tb, ub = t[b % 2], u[b % 2]
                pool.wait_ge(k.wkv_exp, b * 4 + 1)
                nc.gpsimd.tensor_tensor(ub[0], tb[1], V[:, at[b]], ALU.mult).then_inc(k.wkv_e2bv, 1)
                pool.wait_ge(k.wkv_exp, b * 4 + 3)
                nc.gpsimd.tensor_tensor(ub[1], tb[3], V[:, at[b]], ALU.mult).then_inc(k.wkv_e2v, 1)

            for s in range(2):
                nc.gpsimd.memset(pp[s][:, 0:1], -1e30).then_inc(k.wkv_init, 1)
            nc.gpsimd.memset(aa[:, 0:1], 0.0).then_inc(k.wkv_init, 1)
            nc.gpsimd.memset(bb[:, 0:1], 0.0).then_inc(k.wkv_init, 1)
            for b in range(B):
                arguments(b)
                products(b)

        @block.vector
        def _(dve):
            def arguments(b):
                tb, p = t[b % 2], pp[b % 2]
                nc.vector.tensor_tensor_scan(p[:, 1:L + 1], k.lam, K[:, at[b]], -1e30, ALU.add, ALU.max).then_inc(k.wkv_pp, 1)
                dve.wait_ge(k.wkv_pp, b + 1)
                nc.vector.scalar_tensor_tensor(tb[2], K[:, at[b]], k.vec("first"), p[:, 0:L], ALU.add, ALU.max).then_inc(k.wkv_max, 1)
                nc.vector.scalar_tensor_tensor(tb[0], p[:, 0:L], k.wneg[:, 0:1], p[:, 1:L + 1], ALU.add, ALU.subtract).then_inc(k.wkv_arg, 1)
                dve.wait_ge(k.wkv_max, b + 1)
                nc.vector.scalar_tensor_tensor(tb[3], K[:, at[b]], k.vec("first"), tb[2], ALU.add, ALU.subtract).then_inc(k.wkv_arg, 1)

            def sums(b):
                (decay, e2b, e1, e2), ub = t[b % 2], u[b % 2]
                s = b * 6 + 2
                dve.wait_ge(k.wkv_exp, b * 4 + 2)
                nc.vector.tensor_tensor_scan(bb[:, 1:L + 1], decay, e2b, 0.0, ALU.mult, ALU.add).then_inc(k.wkv_step, 1)
                dve.wait_ge(k.wkv_e2bv, b + 1)
                nc.vector.tensor_tensor_scan(aa[:, 1:L + 1], decay, ub[0], 0.0, ALU.mult, ALU.add).then_inc(k.wkv_step, 1)
                dve.wait_ge(k.wkv_step, s + 2)
                dve.wait_ge(k.wkv_exp, b * 4 + 4)
                nc.vector.tensor_tensor(decay, e1, bb[:, 0:L], ALU.mult).then_inc(k.wkv_step, 1)
                nc.vector.tensor_tensor(ub[0], e1, aa[:, 0:L], ALU.mult).then_inc(k.wkv_step, 1)
                dve.wait_ge(k.wkv_step, s + 3)
                nc.vector.tensor_tensor(decay, decay, e2, ALU.add).then_inc(k.wkv_den, 1)
                dve.wait_ge(k.wkv_step, s + 4)
                dve.wait_ge(k.wkv_e2v, b + 1)
                nc.vector.tensor_tensor(ub[1], ub[0], ub[1], ALU.add).then_inc(k.wkv_step, 1)
                dve.wait_ge(k.wkv_step, s + 5)
                nc.vector.scalar_tensor_tensor(ub[1], R[:, at[b]], 1.0, ub[1], ALU.add, ALU.mult).then_inc(k.wkv_step, 1)

            def result(b):
                dve.wait_ge(k.wkv_step, b * 6 + 8)
                dve.wait_ge(k.wkv_rden, b + 1)
                nc.vector.scalar_tensor_tensor(R[:, at[b]], u[b % 2][1], 0.5, t[b % 2][0], ALU.mult, ALU.mult).then_inc(k.wkv_out, 1)

            def add(b):
                dve.wait_ge(k.wkv_prod, 2 * b + 2)
                nc.vector.tensor_tensor(k.Y[:, at[b]], k.Y[:, at[b]], k.pair[b], ALU.add)

            dve.wait_ge(k.wkv_w, 1)
            nc.vector.tensor_scalar(k.wneg[:], k.wdec[:], -1.0, None, ALU.mult).then_inc(k.wkv_step, 1)
            dve.wait_ge(k.wkv_step, 1)
            nc.vector.tensor_copy(k.lam, k.wneg[:, 0:1].to_broadcast([P, L])).then_inc(k.wkv_step, 1)
            dve.wait_ge(k.wkv_step, 2)
            dve.wait_ge(k.wkv_init, 4)
            arguments(0)
            for b in range(B):
                if b >= 1:
                    result(b - 1)
                if b + 1 < B:
                    if b >= 1:
                        dve.wait_ge(k.wkv_out, b)
                    arguments(b + 1)
                sums(b)
                if b >= 1:
                    add(b - 1)
            result(B - 1)
            add(B - 1)


def route(nc, k, a):
    NTI = NT // P
    lg, ex, wt = k.rt_logit, k.rt_exp, k.rt_w
    one, cand, two = k.rt_one, k.rt_cand, k.rt_two
    col = lambda t: t[:, :, None].to_broadcast([P, NTI, E])
    with nc.Block() as block:
        @block.tensor
        def _(pe):
            pe.wait_ge(k.moe_w_in, 64)
            with pe.Fori(0, NCH // W) as it:
                for c in range(W):
                    pe.wait_ge(k.rt_copied, it * W + (c + 1))
                    nc.tensor.matmul(k.bank[c][0:E, :], k.router[:], padded(k.N, it, c), start=True, stop=True).then_inc(k.rt_prod, 1)
            pe.wait_ge(k.rt_copied, NCH + PRIMED["rt_copied"])
            for t in range(NTI):
                op = nc.tensor.transpose(k.bank[4][:, t * E:(t + 1) * E], k.logitT[:, t * P:(t + 1) * P], k.ident[0:E, 0:E])
            op.then_inc(k.rt_turned, 1)
            pe.wait_ge(k.rt_parts, 3)
            for t in range(NTI):
                if t % 4 == 0 and t >= 16:
                    pe.wait_ge(k.rt_wT, t // 4 - 3)
                op = nc.tensor.transpose(k.bank[t // 4 % 4][0:3 * E, (t % 4) * P:(t % 4 + 1) * P],
                                         k.rt_part[:, t, :, :].rearrange("p e s -> p (e s)"), k.ident[:])
                if t % 4 == 3:
                    op.then_inc(k.rt_back, 1)

        @block.scalar
        def _(act):
            with act.Fori(0, NCH // W) as it:
                for c in range(W):
                    act.wait_ge(k.rt_prod, it * W + (c + 1))
                    nc.scalar.activation(k.logitT[:, bass.ds(it * W * CH + c * CH, CH)], k.bank[c][0:E, :], ACT.Copy).then_inc(k.rt_copied, 1)
            act.wait_ge(k.rt_step, 2)
            nc.scalar.activation(ex, ex, ACT.Exp).then_inc(k.rt_exps, 1)
            act.wait_ge(k.rt_sel, 4)
            for q in range(8):
                act.wait_ge(k.rt_back, q + 1)
                nc.scalar.activation(k.twT[0:3 * E, q * CH:(q + 1) * CH], k.bank[q % 4][0:3 * E, :], ACT.Copy).then_inc(k.rt_wT, 1)

        @block.gpsimd
        def _(pool):
            for e in range(E):
                nc.gpsimd.memset(k.rank[:, e:e + 1], float(E - e)).then_inc(k.rt_const, 1)
            nc.gpsimd.memset(k.twT, 0.0).then_inc(k.rt_sel, 1)
            nc.gpsimd.memset(k.sel[:], 1.0).then_inc(k.rt_sel, 1)
            pool.wait_ge(k.rt_sel, 2)
            nc.gpsimd.affine_select(out=k.sel[:], in_=k.sel[:], compare_op=ALU.is_ge, fill=0.0, base=0,
                                    pattern=[[-3, E], [0, P]], channel_multiplier=1).then_inc(k.rt_sel, 1)
            pool.wait_ge(k.rt_sel, 3)
            nc.gpsimd.affine_select(out=k.sel[:], in_=k.sel[:], compare_op=ALU.is_ge, fill=0.0, base=2,
                                    pattern=[[3, E], [0, P]], channel_multiplier=-1).then_inc(k.rt_sel, 1)

        @block.vector
        def _(dve):
            rank = k.rank[:, None, :].to_broadcast([P, NTI, E])
            step = [0]

            def then(op):
                step[0] += 1
                op.then_inc(k.rt_step, 1)
                dve.wait_ge(k.rt_step, step[0])

            dve.wait_ge(k.rt_const, E)
            dve.wait_ge(k.rt_turned, 1)
            logits = k.bank[4][:, 0:NTI * E].rearrange("p (t e) -> p t e", e=E)
            then(nc.vector.tensor_reduce(k.rt_m[:], logits, AX.X, ALU.max))
            then(nc.vector.tensor_tensor(ex, logits, col(k.rt_m[:]), ALU.subtract))
            dve.wait_ge(k.rt_exps, 1)
            then(nc.vector.tensor_reduce(k.rt_m[:], ex, AX.X, ALU.max))
            then(nc.vector.tensor_tensor(cand, ex, col(k.rt_m[:]), ALU.is_equal))
            then(nc.vector.tensor_tensor(cand, cand, rank, ALU.mult))
            then(nc.vector.tensor_reduce(k.rt_c[:], cand, AX.X, ALU.max))
            then(nc.vector.tensor_tensor(one, rank, col(k.rt_c[:]), ALU.is_equal))
            then(nc.vector.tensor_tensor(lg, ex, one, ALU.subtract))
            then(nc.vector.scalar_tensor_tensor(lg, one, -2.0, lg, ALU.mult, ALU.add))
            then(nc.vector.tensor_reduce(k.rt_m[:], lg, AX.X, ALU.max))
            then(nc.vector.tensor_tensor(cand, lg, col(k.rt_m[:]), ALU.is_equal))
            then(nc.vector.tensor_tensor(cand, cand, rank, ALU.mult))
            then(nc.vector.tensor_reduce(k.rt_c[:], cand, AX.X, ALU.max))
            then(nc.vector.tensor_tensor(two, rank, col(k.rt_c[:]), ALU.is_equal))
            then(nc.vector.tensor_tensor(one, one, two, ALU.add))
            then(nc.vector.tensor_tensor(wt, ex, one, ALU.mult))
            then(nc.vector.tensor_reduce(k.rt_m[:], wt, AX.X, ALU.add))
            then(nc.vector.reciprocal(k.rt_m[:], k.rt_m[:]))
            then(nc.vector.tensor_scalar(k.rt_m[:], k.rt_m[:], 0.5, None, ALU.mult))
            then(nc.vector.tensor_tensor(wt, wt, col(k.rt_m[:]), ALU.mult))
            for s in range(3):
                then(nc.vector.tensor_copy(k.rt_bf, wt))
                op = nc.vector.tensor_copy(k.rt_part[:, :, :, s], k.rt_bf)
                op.then_inc(k.rt_parts, 1)
                if s < 2:
                    then(nc.vector.tensor_tensor(wt, wt, k.rt_bf, ALU.subtract))


def experts(nc, k, a):
    UNITS = 2 * E
    kr, ks, er, o = k.big[0][:, 0:2 * CH], k.big[0][:, 2 * CH:6 * CH], k.big[1][:, 0:2 * CH], k.big[1][:, 2 * CH:4 * CH]

    mixed = k.big[3].rearrange("p (s a n) -> p s a n", s=4, a=2)
    acc = k.big[1][:, 4 * CH:6 * CH].rearrange("p (c n) -> p c n", c=2)

    def done(s, n):
        return n + (1 + PRIMED.get(s, 0))

    with nc.Block() as block:
        @block.vector
        def _(dve):
            def begin(it, c):
                nc.vector.tensor_copy(acc[:, c, :], k.Y[:, bass.ds(it * L + c * CH, CH)]).then_inc(k.ex_y, 1)
                now = k.N[:, bass.ds(it * PADL + 1 + c * CH, CH)]
                before = k.N[:, bass.ds(it * PADL + c * CH, CH)]
                nc.vector.tensor_tensor(k.diff[:, c, :], now, before, ALU.subtract).then_inc(k.ex_diff, 1)
                dve.wait_ge(k.ex_diff, it * 2 + (c + 1))

            def mix(it, j):
                n, c, e = it * UNITS + j, j // E, j % E
                if e == 0:
                    begin(it, c)
                before = k.N[:, bass.ds(it * PADL + c * CH, CH)]
                dve.wait_ge(k.ex_r, n + 1)
                nc.vector.scalar_tensor_tensor(mixed[:, j % 4, 0, :], k.diff[:, c, :], k.vec(f"cm_k{e}"), before, ALU.mult, ALU.add)
                nc.vector.scalar_tensor_tensor(mixed[:, j % 4, 1, :], k.diff[:, c, :], k.vec(f"cm_r{e}"), before, ALU.mult, ALU.add).then_inc(k.ex_mix, 1)

            def gate(it, j):
                n, oj = it * UNITS + j, o[:, (j % 2) * CH:(j % 2 + 1) * CH]
                dve.wait_ge(k.ex_v, done("ex_v", n))
                dve.wait_ge(k.ex_tanh, done("ex_tanh", n))
                dve.wait_ge(k.ex_added, n + 1)
                nc.vector.scalar_tensor_tensor(oj, er[:, (j % 2) * CH:(j % 2 + 1) * CH], 1.0, k.bank[4 + j % 2][:], ALU.add, ALU.mult).then_inc(k.ex_gate, 1)
                dve.wait_ge(k.ex_gate, done("ex_gate", n))
                dve.wait_ge(k.ex_tw, done("ex_tw", n))
                nc.vector.tensor_tensor(oj, oj, k.bank[7][:], ALU.mult).then_inc(k.ex_weighed, 1)

            def finish(it, c):
                at = bass.ds(it * L + c * CH, CH)
                dve.wait_ge(k.ex_added, done("ex_added", it * UNITS + (c + 1) * E - 1))
                nc.vector.tensor_tensor(k.X[:, at], k.X[:, at], acc[:, c, :], ALU.add)

            def turn(it, last):
                for j in range(UNITS):
                    gate(it, j)
                    if j + 3 < UNITS:
                        mix(it, j + 3)
                    elif not last:
                        mix(it + 1, j + 3 - UNITS)
                    if j == E:
                        finish(it, 0)
                finish(it, 1)

            for j in range(3):
                mix(0, j)
            with dve.Fori(0, B - 1) as it:
                turn(it, False)
            turn(B - 1, True)

        @block.tensor
        def _(pe):
            def up(it, j):
                n, e = it * UNITS + j, j % E
                pe.wait_ge(k.ex_mix, done("ex_mix", n))
                pe.wait_ge(k.ex_relu, n + 1)
                for h in range(2):
                    op = nc.tensor.matmul(k.bank[2 * (j % 2) + h][:], k.eWk[:, e, h * P:(h + 1) * P], mixed[:, j % 4, 0, :], start=True, stop=True)
                op.then_inc(k.ex_up, 1)
                pe.wait_ge(k.ex_tanh, n + 1)
                nc.tensor.matmul(k.bank[6][:], k.eWr[:, e, :], mixed[:, j % 4, 1, :], start=True, stop=True).then_inc(k.ex_r, 1)

            def turn(it, last):
                for j in range(UNITS):
                    n, c, e = it * UNITS + j, j // E, j % E
                    if j + 1 < UNITS:
                        up(it, j + 1)
                    elif not last:
                        up(it + 1, 0)
                    pe.wait_ge(k.ex_sq, done("ex_sq", n))
                    pe.wait_ge(k.ex_gate, n + 1)
                    for h in range(2):
                        op = nc.tensor.matmul(k.bank[4 + j % 2][:], k.eWv[:, e, h, :], ks[:, (2 * (j % 2) + h) * CH:(2 * (j % 2) + h + 1) * CH], start=(h == 0), stop=(h == 1))
                    op.then_inc(k.ex_v, 1)
                    pe.wait_ge(k.ex_weighed, n + 1)
                    nc.tensor.matmul(k.bank[7][:], k.sel[:, e, :], k.twT[:, bass.ds(it * L + c * CH, CH)], start=True, stop=True).then_inc(k.ex_tw, 1)

            up(0, 0)
            with pe.Fori(0, B - 1) as it:
                turn(it, False)
            turn(B - 1, True)

        @block.scalar
        def _(act):
            with act.Fori(0, B) as it:
                for j in range(UNITS):
                    n = it * UNITS + j
                    act.wait_ge(k.ex_up, done("ex_up", n))
                    act.wait_ge(k.ex_sq, n + 1)
                    for h in range(2):
                        op = nc.scalar.activation(kr[:, h * CH:(h + 1) * CH], k.bank[2 * (j % 2) + h][:], ACT.Relu)
                    op.then_inc(k.ex_relu, 1)
                    act.wait_ge(k.ex_r, done("ex_r", n))
                    act.wait_ge(k.ex_gate, n + 1)
                    nc.scalar.activation(er[:, (j % 2) * CH:(j % 2 + 1) * CH], k.bank[6][:], ACT.Tanh, scale=0.5).then_inc(k.ex_tanh, 1)
                    act.wait_ge(k.ex_relu, done("ex_relu", n))
                    act.wait_ge(k.ex_v, n + 1)
                    nc.scalar.activation(ks[:, (j % 2) * 2 * CH:(j % 2 + 1) * 2 * CH], kr, ACT.Square).then_inc(k.ex_sq, 1)

        @block.gpsimd
        def _(pool):
            with pool.Fori(0, B) as it:
                for j in range(UNITS):
                    n, c, e = it * UNITS + j, j // E, j % E
                    oj = o[:, (j % 2) * CH:(j % 2 + 1) * CH]
                    pool.wait_ge(k.ex_weighed, done("ex_weighed", n))
                    if e == 0:
                        pool.wait_ge(k.ex_y, it * 2 + (c + 1))
                    pool.wait_ge(k.ex_added, n + 2)
                    nc.gpsimd.tensor_tensor(acc[:, c, :], acc[:, c, :], oj, ALU.add).then_inc(k.ex_added, 1)


def stage_rwkv(nc, k, a, X, Y):
    N = lambda it, c: padded(k.N, it, c)
    with ExitStack() as ctx:
        sems = begin_stage(nc, ctx, MOE_SEMS)
        (k.mix_diff, k.mix_in, k.kvr, k.kvr_out, k.wkv_w, k.wkv_arg, k.wkv_exp, k.wkv_den, k.wkv_ln, k.wkv_rden,
         k.wkv_init, k.wkv_e2bv, k.wkv_e2v, k.wkv_pp, k.wkv_max, k.wkv_sub, k.wkv_out, k.wkv_prod, k.wkv_step, k.rt_prod, k.rt_copied, k.rt_turned, k.rt_parts,
         k.rt_wT, k.rt_back, k.rt_step, k.rt_exps, k.rt_const, k.rt_sel, k.ex_diff, k.ex_mix, k.ex_r, k.ex_v,
         k.ex_tanh, k.ex_added, k.ex_gate, k.ex_tw, k.ex_weighed, k.ex_up, k.ex_relu, k.ex_sq, k.ex_y) = sems
        k.ln(X, Y, ahead=lambda block: rwkv_loads(k, a, block))
        k.ln(Y, N, gain="ln1_g", bias="ln1_b")
        rwkv_mix(nc, k, a)
        wkv(nc, k, a)
        k.ln(Y, N, gain="ln2_g", bias="ln2_b")
        route(nc, k, a)
        experts(nc, k, a)
        end_stage(nc, sems)


def ffn_loads(k, a, block):
    GR, GW = 3, 3 * DM

    @block.sync
    def _(sp):
        for p in range(NP):
            sp.dma_start(k.W1[:, p // 3, (p % 3) * DM:(p % 3 + 1) * DM], a["L0_ffn_W1"][p]).then_inc(k.ff_w_in, 16)
        sp.dma_start(k.Wo1, a["L0_ffn_Wo1"]).then_inc(k.ff_w_in, 16)
        sp.dma_start(k.W2[0:GW, :, :], a["L0_ffn_W2"].rearrange("(g q) m d -> (q m) g d", g=GR)).then_inc(k.ff_w_in, 16)
        sp.dma_start(k.W2[GW:GW + NP, 0, :], a["L0_ffn_b2"]).then_inc(k.ff_w_in, 16)
        sp.dma_start(k.Wo2[0:DM, :], a["L0_ffn_Wo2"]).then_inc(k.ff_w_in, 16)
        sp.dma_start(k.Wo2[DM:DM + 1, :], a["L0_ffn_bo2"].rearrange("(o n) -> o n", o=1)).then_inc(k.ff_w_in, 16)


def feedforward(nc, k, a, call):
    GR, GW = 3, 3 * DM
    TI = CH // P
    Z = k.big[1]
    base = call * NCH
    own = (k.bank[5], k.bank[3])
    masks = (k.bank[6], k.bank[7], k.bank[4])
    xm = [k.big[0][:, c * CH:(c + 1) * CH] for c in range(2)]
    hid = [k.big[0][:, (2 + 3 * c) * CH:(5 + 3 * c) * CH] for c in range(2)]
    hm = k.big[3][:, 0:3 * CH]
    u = [k.big[2][0:DM + 1, c * CH:(c + 1) * CH] for c in range(2)]
    sc = [k.big[2][:, (2 + c) * CH:(3 + c) * CH] for c in range(2)]
    cand, hot = ([sc[c][:, j * 64:j * 64 + TI * NP].rearrange("p (t e) -> p t e", e=NP) for c in range(2)] for j in range(2))
    top = [sc[c][:, 192:192 + TI] for c in range(2)]
    hotT = [k.big[2][:, 4 * CH + c * 256:4 * CH + (c + 1) * 256].bitcast(BF16) for c in range(2)]
    with nc.Block() as block:
        @block.gpsimd
        def _(pool):
            if call == 0:
                nc.gpsimd.memset(k.W1[:, :, GW:P], 0.0).then_inc(k.ff_const, 1)
                for p in range(NP):
                    nc.gpsimd.memset(k.prank[:, p:p + 1], float(NP - p)).then_inc(k.ff_const, 1)
                nc.gpsimd.memset(k.spread, 0.0).then_inc(k.ff_spread, 1)
                pool.wait_ge(k.ff_spread, 1)
                sv = k.spread[:, :, 0:GW].rearrange("p g (q m) -> p g q m", m=DM)
                nc.gpsimd.affine_select(out=sv, in_=sv, compare_op=ALU.not_equal, fill=1.0, base=0,
                                        pattern=[[-3, GR], [-1, 3], [0, DM]], channel_multiplier=1).then_inc(k.ff_spread, 1)
                so = k.spread[:, 0, GW:P]
                nc.gpsimd.affine_select(out=so, in_=so, compare_op=ALU.not_equal, fill=1.0, base=0,
                                        pattern=[[-1, P - GW]], channel_multiplier=1).then_inc(k.ff_spread, 1)
            for c in range(2):
                nc.gpsimd.memset(hotT[c], 0.0).then_inc(k.ff_hot0, 1)

        @block.vector
        def _(dve):
            for c in range(2):
                nc.vector.memset(u[c][DM:DM + 1, :], 1.0).then_inc(k.ff_hot0, 1)
            if call == 0:
                dve.wait_ge(k.ff_const, 1 + NP)
                dve.wait_ge(k.ff_spread, 3)
                nc.vector.tensor_copy(k.spread16[:], k.spread).then_inc(k.ff_spread16, 1)
            def mix(it, c):
                g = it * 2 + (base + c)
                n = lambda s: k.N[:, bass.ds(it * PADL + 1 + c * CH + s, CH)]
                dve.wait_ge(k.ff_h, g * 3 + 3)
                nc.vector.tensor_scalar(xm[c], n(-1), k.vec("mix0"), None, ALU.mult).then_inc(k.ff_mix1, 1)
                dve.wait_ge(k.ff_mix1, g + 1)
                nc.vector.scalar_tensor_tensor(xm[c], n(0), k.vec("mix1"), xm[c], ALU.mult, ALU.add).then_inc(k.ff_mix2, 1)
                dve.wait_ge(k.ff_mix2, g + 1)
                nc.vector.scalar_tensor_tensor(xm[c], n(1), k.vec("mix2"), xm[c], ALU.mult, ALU.add).then_inc(k.ff_mix, 1)

            def choose(it, c):
                g = it * 2 + (base + c)
                rank = k.prank[:, None, :].to_broadcast([P, TI, NP])
                scores = own[c][:, 0:TI * NP].rearrange("p (t e) -> p t e", e=NP)
                col = top[c][:, :, None].to_broadcast([P, TI, NP])
                dve.wait_ge(k.ff_score, g + 1)
                nc.vector.tensor_reduce(top[c], scores, AX.X, ALU.max).then_inc(k.ff_step, 1)
                dve.wait_ge(k.ff_step, g * 4 + 1)
                nc.vector.tensor_tensor(cand[c], scores, col, ALU.is_equal).then_inc(k.ff_step, 1)
                dve.wait_ge(k.ff_step, g * 4 + 2)
                nc.vector.tensor_tensor(cand[c], cand[c], rank, ALU.mult).then_inc(k.ff_step, 1)
                dve.wait_ge(k.ff_step, g * 4 + 3)
                nc.vector.tensor_reduce(top[c], cand[c], AX.X, ALU.max).then_inc(k.ff_step, 1)
                dve.wait_ge(k.ff_step, g * 4 + 4)
                nc.vector.tensor_tensor(hot[c], rank, col, ALU.is_equal).then_inc(k.ff_hot, 1)

            def mask(it, c):
                g = it * 2 + (base + c)
                dve.wait_ge(k.ff_out, g + 1)
                for j in range(GR):
                    dve.wait_ge(k.ff_hid, g * 3 + (j + 1 + PRIMED["ff_hid"]))
                    dve.wait_ge(k.ff_spreads, g * 3 + (j + 1))
                    nc.vector.tensor_tensor(hm[:, j * CH:(j + 1) * CH], hid[c][:, j * CH:(j + 1) * CH], masks[j][:], ALU.mult).then_inc(k.ff_masked, 1)

            def add(it, c):
                g = it * 2 + (base + c)
                dve.wait_ge(k.ff_out, g + (1 + PRIMED["ff_out"]))
                nc.vector.tensor_tensor(Z[:, bass.ds(it * L + c * CH, CH)], k.N[:, bass.ds(it * PADL + 1 + c * CH, CH)], own[c][:], ALU.add).then_inc(k.ff_z, 1)

            def turn(it, first, last):
                for c in range(2):
                    before = (it - 1, 1) if c == 0 else (it, 0)
                    if not (first and c == 0):
                        mask(*before)
                    choose(it, c)
                    if not (first and c == 0):
                        add(*before)
                    if not last:
                        mix(it + 1, c)

            mix(0, 0)
            mix(0, 1)
            turn(0, True, False)
            with dve.Fori(1, B - 1) as it:
                turn(it, False, False)
            turn(B - 1, False, True)
            mask(B - 1, 1)
            add(B - 1, 1)

        @block.tensor
        def _(pe):
            if call == 0:
                pe.wait_ge(k.ff_w_in, 16 * (NP + 5))
                pe.wait_ge(k.ff_spread16, 1)
                pe.wait_ge(k.ff_const, 1 + NP)
            pe.wait_ge(k.ff_hot0, 4 * call + 4)
            def hidden(it, c):
                g = it * 2 + (base + c)
                pe.wait_ge(k.ff_mix, g + 1)
                for j in range(GR):
                    pe.wait_ge(k.ff_hid, g * 3 + (j + 1))
                    nc.tensor.matmul(k.bank[j][:], k.W1[:, j, :], xm[c], start=True, stop=True).then_inc(k.ff_h, 1)
                    if j == 0:
                        pe.wait_ge(k.ff_z, g + 1)
                        nc.tensor.matmul(own[c][0:DM, :], k.Wo1, xm[c], start=True, stop=True).then_inc(k.ff_up, 1)

            def scores(it, c):
                pe.wait_ge(k.ff_u, it * 2 + (base + c + 1))
                for t in range(TI):
                    op = nc.tensor.matmul(own[c][:, t * NP:(t + 1) * NP], u[c][:, t * P:(t + 1) * P], k.Wo2[:], start=True, stop=True)
                op.then_inc(k.ff_score, 1)

            def turned(it, c):
                pe.wait_ge(k.ff_hot, it * 2 + (base + c + 1))
                for t in range(TI):
                    op = nc.tensor.transpose(own[c][0:NP, t * P:(t + 1) * P], hot[c][:, t, :], k.ident[:])
                op.then_inc(k.ff_hotT, 1)

            def spread(it, c):
                g = it * 2 + (base + c)
                pe.wait_ge(k.ff_hot16, g + 1)
                for j in range(GR):
                    pe.wait_ge(k.ff_masked, g * 3 + (j + 1 + PRIMED["ff_masked"] - GR))
                    nc.tensor.matmul(masks[j][:], k.spread16[:, j, :], hotT[c], start=True, stop=True).then_inc(k.ff_spreads, 1)

            def down(it, c):
                g = it * 2 + (base + c)
                for j in range(GR):
                    rows = P if j == 0 else GW
                    pe.wait_ge(k.ff_masked, g * 3 + (j + 1 + PRIMED["ff_masked"]))
                    op = nc.tensor.matmul(own[c][:], k.W2[0:rows, j, :], hm[0:rows, j * CH:(j + 1) * CH], start=(j == 0), stop=(j == GR - 1))
                op.then_inc(k.ff_out, 1)

            def turn(it, first):
                for c in range(2):
                    before = (it - 1, 1) if c == 0 else (it, 0)
                    if not (first and c == 0):
                        turned(*before)
                    hidden(it, c)
                    if not (first and c == 0):
                        spread(*before)
                    scores(it, c)
                    if not (first and c == 0):
                        down(*before)

            turn(0, True)
            with pe.Fori(1, B) as it:
                turn(it, False)
            turned(B - 1, 1)
            spread(B - 1, 1)
            down(B - 1, 1)

        @block.scalar
        def _(act):
            def hidden(it, c):
                g = it * 2 + (base + c)
                for j in range(GR):
                    act.wait_ge(k.ff_h, g * 3 + (j + 1 + PRIMED["ff_h"]))
                    act.wait_ge(k.ff_masked, g * 3 + (j + 1))
                    nc.scalar.activation(hid[c][:, j * CH:(j + 1) * CH], k.bank[j][:], ACT.Identity, bias=k.vec(f"b1_{j}")).then_inc(k.ff_hid, 1)
                    if j == 0:
                        act.wait_ge(k.ff_up, g + 1)
                        nc.scalar.activation(u[c][0:DM, :], own[c][0:DM, :], ACT.Tanh, bias=k.vec("bo1", DM)).then_inc(k.ff_u, 1)

            def choice(it, c):
                act.wait_ge(k.ff_hotT, it * 2 + (base + c + 1))
                nc.scalar.activation(hotT[c][0:NP, :], own[c][0:NP, :], ACT.Copy).then_inc(k.ff_hot16, 1)

            def turn(it, first):
                for c in range(2):
                    if not (first and c == 0):
                        choice(*((it - 1, 1) if c == 0 else (it, 0)))
                    hidden(it, c)

            turn(0, True)
            with act.Fori(1, B) as it:
                turn(it, False)
            choice(B - 1, 1)


def stage_ffn(nc, k, a, X, Y):
    call = k.ff_calls
    k.ff_calls += 1
    k.ln(X, lambda it, c: padded(k.N, it, c), ahead=(lambda block: ffn_loads(k, a, block)) if call == 0 else None)
    feedforward(nc, k, a, call)
    k.ln(lambda it, c: plain(k.big[1], it, c), None, gain="gamma", bias="beta", residual=X)


def lru(nc, k, a):
    KK, KV, R = k.big[0], k.big[1], k.big[2]
    u1, u2 = k.big[3][:, 0:L + 1], k.big[3][:, L + 1:2 * L + 2]
    t1, t2 = k.big[4][:, 0:L], k.big[4][:, L:2 * L]
    W_rkv, W_o = k.lruw[:, 0:3 * P], k.lruw[:, 3 * P:4 * P]
    with nc.Block() as block:
        @block.tensor
        def _(pe):
            pe.wait_ge(k.lr_w_in, 32)
            with pe.Fori(0, B) as it:
                for c in range(2):
                    for j in range(3):
                        n = it * 6 + (3 * c + j)
                        pe.wait_ge(k.lr_read, n + 1)
                        nc.tensor.matmul(k.bank[3 * c + j][:], W_rkv[:, j * P:(j + 1) * P], k.Y[:, bass.ds(it * L + c * CH, CH)],
                                         start=True, stop=True).then_inc(k.lr_prod, 1)
            with pe.Fori(0, B) as it:
                pe.wait_ge(k.lr_x, it + 1)
                for c in range(2):
                    pe.wait_ge(k.lr_added, it * 2 + (c + 1))
                    nc.tensor.matmul(k.bank[6 + c][:], W_o, R[:, bass.ds(it * L + c * CH, CH)], start=True, stop=True).then_inc(k.lr_out, 1)

        @block.scalar
        def _(act):
            act.preload_act_table_set("natural_log_exp_and_others")
            act.wait_ge(k.lr_init, 1)
            nc.scalar.activation(k.lr_nu[:], k.vec("nu_log"), ACT.Exp).then_inc(k.lr_sc, 1)
            act.wait_ge(k.lr_sc, 1)
            nc.scalar.activation(k.lr_lam[:], k.lr_nu[:], ACT.Exp, scale=-1.0).then_inc(k.lr_sc, 1)
            nc.scalar.activation(k.lr_own[:], k.vec("nu_log"), ACT.Exp, bias=k.vec("gamma_log")).then_inc(k.lr_sc, 1)

            def exps(it):
                for c in range(2):
                    at = bass.ds(it * L + c * CH, CH)
                    n = it * 6 + 3 * c
                    wait_apart(act, k, k.lr_prod, n + 1)
                    nc.scalar.activation(R[:, at], k.bank[3 * c][:], ACT.Exp, bias=k.lr_nbr[:, 0:1], scale=-1.0).then_inc(k.lr_read, 1)
                    wait_apart(act, k, k.lr_prod, n + 2)
                    nc.scalar.activation(KK[:, at], k.bank[3 * c + 1][:], ACT.Exp, bias=k.vec("bkk")).then_inc(k.lr_read, 1)
                    wait_apart(act, k, k.lr_prod, n + 3)
                    nc.scalar.activation(KV[:, at], k.bank[3 * c + 2][:], ACT.Identity, bias=k.vec("bvv")).then_inc(k.lr_read, 1)

            def over(it):
                at = bass.ds(it * L, L)
                wait_apart(act, k, k.lr_den, it + 1)
                nc.scalar.activation(KK[:, at], KK[:, at], ACT.Ln).then_inc(k.lr_ln, 1)
                wait_apart(act, k, k.lr_ln, it + 1)
                nc.scalar.activation(KK[:, at], KK[:, at], ACT.Exp, scale=-1.0).then_inc(k.lr_rden, 1)

            exps(0)
            with act.Fori(1, B) as it:
                exps(it)
                over(it - 1)
            over(B - 1)

        @block.gpsimd
        def _(pool):
            def product(it):
                at = bass.ds(it * L, L)
                wait_apart(pool, k, k.lr_read, it * 6 + (6 + PRIMED["lr_read"]))
                nc.gpsimd.tensor_tensor(KV[:, at], KV[:, at], KK[:, at], ALU.mult).then_inc(k.lr_kv, 1)

            def quotient(it):
                at = bass.ds(it * L, L)
                wait_apart(pool, k, k.lr_rden, it + 1)
                nc.gpsimd.tensor_tensor(R[:, at], KV[:, at], KK[:, at], ALU.mult).then_inc(k.lr_x, 1)

            product(0)
            with pool.Fori(1, B) as it:
                product(it)
                quotient(it - 1)
            quotient(B - 1)

        @block.vector
        def _(dve):
            nc.vector.tensor_scalar(k.lr_nbr[:], k.vec("br"), -1.0, None, ALU.mult).then_inc(k.lr_init, 1)
            nc.vector.memset(u1[:, 0:1], 0.0)
            nc.vector.memset(u2[:, 0:1], 0.0)
            dve.wait_ge(k.lr_sc, 3)
            nc.vector.tensor_copy(k.lam, k.lr_lam[:, 0:1].to_broadcast([P, L])).then_inc(k.lr_init, 1)
            dve.wait_ge(k.lr_init, 2)

            def sums(it, first=False):
                at = bass.ds(it * L, L)
                s = it * 5
                dve.wait_ge(k.lr_read, it * 6 + (5 + PRIMED["lr_read"]))
                nc.vector.tensor_tensor_scan(u2[:, 1:L + 1], k.lam, KK[:, at], 0.0, ALU.mult, ALU.add).then_inc(k.lr_step, 1)
                if not first:
                    dve.wait_ge(k.lr_den, it)
                nc.vector.tensor_scalar(t2, KK[:, at], k.lr_own[:, 0:1], 1e-6, ALU.mult, ALU.add)
                dve.wait_ge(k.lr_kv, it + 1)
                nc.vector.tensor_tensor_scan(u1[:, 1:L + 1], k.lam, KV[:, at], 0.0, ALU.mult, ALU.add).then_inc(k.lr_step, 1)
                nc.vector.tensor_scalar(t1, KV[:, at], k.lr_own[:, 0:1], None, ALU.mult).then_inc(k.lr_step, 1)
                dve.wait_ge(k.lr_step, s + 3)
                nc.vector.scalar_tensor_tensor(t2, u2[:, 0:L], k.lr_lam[:, 0:1], t2, ALU.mult, ALU.add).then_inc(k.lr_step, 1)
                nc.vector.scalar_tensor_tensor(KV[:, at], u1[:, 0:L], k.lr_lam[:, 0:1], t1, ALU.mult, ALU.add).then_inc(k.lr_step, 1)
                dve.wait_ge(k.lr_step, s + 5)
                nc.vector.scalar_tensor_tensor(KK[:, at], R[:, at], 1.0, t2, ALU.add, ALU.mult).then_inc(k.lr_den, 1)

            def add(it):
                for c in range(2):
                    at = bass.ds(it * L + c * CH, CH)
                    dve.wait_ge(k.lr_out, it * 2 + (c + 1))
                    nc.vector.scalar_tensor_tensor(k.X[:, at], k.bank[6 + c][:], k.vec("lru_bo"), k.X[:, at], ALU.add, ALU.add).then_inc(k.lr_added, 1)

            sums(0, True)
            sums(1)
            with dve.Fori(2, B) as it:
                sums(it)
                add(it - 2)
            add(B - 2)
            add(B - 1)


def stage_lru(nc, k, a, X, Y):
    def ahead(block):
        @block.sync
        def _(sp):
            sp.dma_start(k.lruw[:, 0:3 * P], a["L1_attn_b_W_rkv"]).then_inc(k.lr_w_in, 16)
            sp.dma_start(k.lruw[:, 3 * P:4 * P], a["L1_attn_b_W_o"]).then_inc(k.lr_w_in, 16)

    k.ln(X, Y, ahead=ahead)
    lru(nc, k, a)


def tree_loads(k, a, block):
    rows = k.big[0][:, 0:8 * P].rearrange("p (j d) -> p j d", d=P)

    @block.sync
    def _(sp):
        sp.dma_start(rows[:, 0, :], a["L1_ffn_routers"][0:P, :]).then_inc(k.tw_in, 16)
        sp.dma_start(rows[0:P - 1, 1, :], a["L1_ffn_routers"][P:2 * P - 1, :]).then_inc(k.tw_in, 16)
        sp.dma_start(rows[:, 2:4, :], a["L1_ffn_leaf_values"].rearrange("(h m) d -> m h d", h=2)).then_inc(k.tw_in, 16)
        sp.dma_start(rows[:, 4, :], a["L1_ffn_Wout_w"]).then_inc(k.tw_in, 16)
        sp.dma_start(rows[:, 5, :], a["L1_ffn_Wq"]).then_inc(k.tw_in, 16)


def tree_weights(nc, k, a):
    rows = k.big[0][:, 0:8 * P].rearrange("p (j d) -> p j d", d=P)
    turned = k.big[1][:, 0:5 * P].rearrange("p (j d) -> p j d", d=P)
    with nc.Block() as block:
        @block.tensor
        def _(pe):
            pe.wait_ge(k.tw_in, 5 * 16)
            for j in range(5):
                n = P - 1 if j == 1 else P
                nc.tensor.transpose(k.bank[j // 4][:, (j % 4) * P:(j % 4) * P + n], rows[0:n, j, :], k.ident[0:n, 0:n]).then_inc(k.tw_turned, 1)
            pe.wait_ge(k.tw_copied, 5)
            nc.tensor.matmul(k.bank[2][:, 0:2 * P], rows[:, 5, :], turned[:, 0:2, :].rearrange("p j d -> p (j d)"), start=True, stop=True).then_inc(k.tw_prod, 1)
            for h in range(2):
                nc.tensor.matmul(k.bank[3 + h][:, 0:P], turned[:, 2 + h, :], turned[:, 4, :], start=True, stop=True).then_inc(k.tw_prod, 1)

        @block.vector
        def _(dve):
            nc.vector.memset(turned[:, 1, :], 0.0).then_inc(k.tw_zero, 1)
            dve.wait_ge(k.tw_zero, 1)
            dve.wait_ge(k.tw_turned, 5)
            for j in range(5):
                n = P - 1 if j == 1 else P
                nc.vector.tensor_copy(turned[:, j, 0:n], k.bank[j // 4][:, (j % 4) * P:(j % 4) * P + n]).then_inc(k.tw_copied, 1)
            dve.wait_ge(k.tw_prod, 3)
            nc.vector.tensor_copy(k.gates, k.bank[2][:, 0:2 * P])
            for h in range(2):
                nc.vector.tensor_copy(k.leaves[:, h, :], k.bank[3 + h][:, 0:P])


def tree(nc, k, a, call):
    TI, M, DEPTH = CH // P, 256, 8
    base = call * NCH
    wide = lambda v: v.rearrange("p (t m) -> p t m", m=M)
    gr = [wide(k.big[0][:, 2 * c * CH:2 * (c + 1) * CH]) for c in range(2)]
    gl = [wide(k.big[0][:, (4 + 2 * c) * CH:(6 + 2 * c) * CH]) for c in range(2)]
    lp = [[wide(k.big[1][:, (4 * c + 2 * s) * CH:(4 * c + 2 * s + 2) * CH]) for s in range(2)] for c in range(2)]
    th = k.big[2][:, 0:2 * CH]
    ys = [k.big[2][:, (2 + c) * CH:(3 + c) * CH] for c in range(2)]
    lpT = [k.big[2][:, (4 + 2 * c) * CH:(6 + 2 * c) * CH] for c in range(2)]

    def done(s, g):
        return g + (1 + PRIMED.get(s, 0))

    with nc.Block() as block:
        @block.tensor
        def _(pe):
            def front(it):
                for c in range(2):
                    g = it * 2 + (base + c)
                    pe.wait_ge(k.tr_th, g + 1)
                    pe.wait_ge(k.tr_ys, done("tr_ys", g))
                    for t in range(TI):
                        op = nc.tensor.matmul(k.bank[2 * c + t // 2][:, (t % 2) * M:(t % 2 + 1) * M], ys[c][:, t * P:(t + 1) * P], k.gates, start=True, stop=True)
                    op.then_inc(k.tr_z, 1)

            def back(it):
                for c in range(2):
                    g = it * 2 + (base + c)
                    pe.wait_ge(k.tr_lpT, g + 1)
                    pe.wait_ge(k.tr_lp, done("tr_lp", g))
                    for h in range(2):
                        for t in range(TI):
                            op = nc.tensor.transpose(k.bank[4 + h][:, t * P:(t + 1) * P], lp[c][1][:, t, h * P:(h + 1) * P], k.ident[:])
                    op.then_inc(k.tr_turned, 1)
                    pe.wait_ge(k.tr_x, g + 1)
                    pe.wait_ge(k.tr_lpT, done("tr_lpT", g))
                    for h in range(2):
                        op = nc.tensor.matmul(k.bank[6 + c][:], k.leaves[:, h, :], lpT[c][:, h * CH:(h + 1) * CH], start=(h == 0), stop=(h == 1))
                    op.then_inc(k.tr_out, 1)

            front(0)
            with pe.Fori(1, NCH // 2) as it:
                front(it)
                back(it - 1)
            back(NCH // 2 - 1)

        @block.scalar
        def _(act):
            def front(it):
                for c in range(2):
                    g = it * 2 + (base + c)
                    act.wait_ge(k.tr_z, g + 1)
                    nc.scalar.activation(ys[c], k.Y[:, bass.ds(it * L + c * CH, CH)], ACT.Copy).then_inc(k.tr_ys, 1)
                for c in range(2):
                    g = it * 2 + (base + c)
                    act.wait_ge(k.tr_z, done("tr_z", g))
                    act.wait_ge(k.tr_g, g + 1)
                    for h in range(2):
                        op = nc.scalar.activation(th[:, h * CH:(h + 1) * CH], k.bank[2 * c + h][:], ACT.Tanh, scale=0.5)
                    op.then_inc(k.tr_th, 1)

            def back(it):
                for c in range(2):
                    g = it * 2 + (base + c)
                    act.wait_ge(k.tr_turned, done("tr_turned", g))
                    act.wait_ge(k.tr_out, g + 1)
                    for h in range(2):
                        op = nc.scalar.activation(lpT[c][:, h * CH:(h + 1) * CH], k.bank[4 + h][:], ACT.Copy)
                    op.then_inc(k.tr_lpT, 1)

            front(0)
            with act.Fori(1, NCH // 2) as it:
                front(it)
                back(it - 1)
            back(NCH // 2 - 1)

        @block.vector
        def _(dve):
            def front(it):
                for c in range(2):
                    g = it * 2 + (base + c)
                    dve.wait_ge(k.tr_th, done("tr_th", g))
                    nc.vector.tensor_scalar(gr[c], wide(th), 0.5, 0.5, ALU.mult, ALU.add)
                    nc.vector.tensor_scalar(gl[c], wide(th), -0.5, 0.5, ALU.mult, ALU.add).then_inc(k.tr_g, 1)
                    dve.wait_ge(k.tr_g, done("tr_g", g))
                    dve.wait_ge(k.tr_turned, g + 1)
                    nc.vector.tensor_copy(lp[c][0][:, :, 0:1], gl[c][:, :, 0:1])
                    nc.vector.tensor_copy(lp[c][0][:, :, 1:2], gr[c][:, :, 0:1]).then_inc(k.tr_step, 1)
                    for level in range(1, DEPTH):
                        n = 2 ** level
                        dve.wait_ge(k.tr_step, g * (DEPTH - 1) + level)
                        src, dst = lp[c][(level - 1) % 2][:, :, 0:n], lp[c][level % 2][:, :, 0:2 * n]
                        pairs = dst.rearrange("p t (n s) -> p t n s", s=2)
                        nc.vector.tensor_tensor(pairs[:, :, :, 0], src, gl[c][:, :, n - 1:2 * n - 1], ALU.mult)
                        op = nc.vector.tensor_tensor(pairs[:, :, :, 1], src, gr[c][:, :, n - 1:2 * n - 1], ALU.mult)
                        op.then_inc(k.tr_lp if level == DEPTH - 1 else k.tr_step, 1)

            def back(it):
                for c in range(2):
                    g = it * 2 + (base + c)
                    at = bass.ds(it * L + c * CH, CH)
                    dve.wait_ge(k.tr_out, done("tr_out", g))
                    nc.vector.scalar_tensor_tensor(k.X[:, at], k.bank[6 + c][:], k.vec("wout_b"), k.X[:, at], ALU.add, ALU.add).then_inc(k.tr_x, 1)

            front(0)
            with dve.Fori(1, NCH // 2) as it:
                front(it)
                back(it - 1)
            back(NCH // 2 - 1)


def stage_tree(nc, k, a, X, Y):
    call = k.tr_calls
    k.tr_calls += 1
    k.ln(X, Y, ahead=(lambda block: tree_loads(k, a, block)) if call == 0 else None)
    if call == 0:
        tree_weights(nc, k, a)
    tree(nc, k, a, call)


def favor_loads(nc, k, a, block):
    H, M, DK, G = 16, 32, 8, 4

    @block.sync
    def _(sp):
        for j, w in enumerate((a["L0_attn_b_Wq"], a["L0_attn_b_Wk"], a["L0_attn_b_Wv"], a["L0_attn_b_Wo"])):
            sp.dma_start(k.fv_rows[:, j, :], w).then_inc(k.fw_in, 16)
        sp.dma_start(k.fv_proj_rows, a["L0_attn_b_proj"].rearrange("(g h) m d -> (h m) g d", g=G)).then_inc(k.fw_in, 16)

    @block.gpsimd
    def _(pool):
        nc.gpsimd.memset(k.fv_mask, 1.0).then_inc(k.fw_mask, 1)
        nc.gpsimd.memset(k.fv_own, 1.0 / M).then_inc(k.fw_mask, 1)
        pool.wait_ge(k.fw_mask, 2)
        nc.gpsimd.affine_select(out=k.fv_mask, in_=k.fv_mask, compare_op=ALU.is_ge, fill=0.0, base=0,
                                pattern=[[4 * M, G], [-M, H]], channel_multiplier=1).then_inc(k.fw_mask, 1)
        nc.gpsimd.affine_select(out=k.fv_own, in_=k.fv_own, compare_op=ALU.is_ge, fill=0.0, base=0,
                                pattern=[[-M, 4]], channel_multiplier=1).then_inc(k.fw_mask, 1)
        pool.wait_ge(k.fw_mask, 4)
        nc.gpsimd.affine_select(out=k.fv_mask, in_=k.fv_mask, compare_op=ALU.is_ge, fill=0.0, base=M - 1,
                                pattern=[[-4 * M, G], [M, H]], channel_multiplier=-1).then_inc(k.fw_mask, 1)
        nc.gpsimd.affine_select(out=k.fv_own, in_=k.fv_own, compare_op=ALU.is_ge, fill=0.0, base=M - 1,
                                pattern=[[M, 4]], channel_multiplier=-1).then_inc(k.fw_mask, 1)
        nc.gpsimd.memset(k.eps6[:], 1e-6).then_inc(k.fw_mask, 1)
        nc.gpsimd.memset(k.fv_eps, 1e-6)


def favor_weights(nc, k):
    H, M, DK, G = 16, 32, 8, 4
    rows, proj, mask = k.fv_rows, k.fv_proj_rows, k.fv_mask
    wide = k.arena[:, 6 * P:10 * P].rearrange("p (g n) -> p g n", g=G)
    diag = k.arena[:, 10 * P:14 * P]
    with nc.Block() as block:
        @block.tensor
        def _(pe):
            pe.wait_ge(k.fw_in, 5 * 16)
            for j in range(4):
                nc.tensor.transpose(k.bank[0][:, j * P:(j + 1) * P], rows[:, j, :], k.ident[:]).then_inc(k.fw_turned, 1)
            pe.wait_ge(k.fw_wide, 1)
            for g in range(G):
                nc.tensor.transpose(k.bank[1][:, g * P:(g + 1) * P], wide[:, g, :], k.ident[:]).then_inc(k.fw_turned, 1)
            pe.wait_ge(k.fw_copied, 2)
            for j in range(2):
                nc.tensor.matmul(k.bank[2 + j][:], rows[:, j, :], diag, start=True, stop=True).then_inc(k.fw_prod, 1)

        @block.vector
        def _(dve):
            dve.wait_ge(k.fw_in, 5 * 16)
            dve.wait_ge(k.fw_mask, 7)
            for g in range(G):
                op = nc.vector.tensor_tensor(wide[:, g, :].rearrange("p (h d) -> p h d", d=DK), proj[:, g:g + 1, :].to_broadcast([P, H, DK]),
                                             mask[:, g, :, None].to_broadcast([P, H, DK]), ALU.mult)
            op.then_inc(k.fw_wide, 1)
            dve.wait_ge(k.fw_turned, 4)
            nc.vector.tensor_copy(k.fv_wT, k.bank[0][:]).then_inc(k.fw_copied, 1)
            dve.wait_ge(k.fw_turned, 8)
            nc.vector.tensor_copy(diag, k.bank[1][:]).then_inc(k.fw_copied, 1)
            for j in range(2):
                dve.wait_ge(k.fw_prod, j + 1)
                nc.vector.tensor_scalar(k.fv_feat[:, j, :], k.bank[2 + j][:], DK ** -0.5, None, ALU.mult)


def favor(nc, k, a):
    H, M, DK, G = 16, 32, 8, 4
    TT = L // P
    take = [0]

    def part(n):
        take[0] += n
        return k.arena[:, take[0] - n:take[0]]

    ys = [part(CH) for _ in range(2)]
    sq = [part(P) for _ in range(2)]
    va = [part(144).rearrange("p (h n) -> p h n", n=9) for _ in range(4)]
    mx = [part(H) for _ in range(2)]
    nm = [part(H) for _ in range(2)]
    rd = [part(H) for _ in range(2)]
    kv = part(B * 144)
    ex = [part(CH) for _ in range(4)]
    exT = [part(CH) for _ in range(2)]
    o = [part(P) for _ in range(2)]
    oT = part(CH)
    wT = k.fv_wT

    def done(s, n):
        return n + (1 + PRIMED.get(s, 0))

    def there(at, i):
        return at is None or 0 <= at + i < B * TT

    def run(eng, turn, steps):
        turn(0, 0, TT)
        with eng.Fori(1, B) as u:
            turn(u, None, TT)
        turn(B, B * TT, steps)

    def copy_input(pool, b, c, n0):
        if n0 or not isinstance(b, int):
            wait_apart(pool, k, k.fv_proj, b * TT + (n0 + 4 * c + 3 - TT + 1 + PRIMED["fv_proj"]))
        nc.gpsimd.tensor_copy(ys[c], k.Y[:, bass.ds(b * L + c * CH, CH)]).then_inc(k.fv_ys, 1)

    def project(pe, n, i, b, y0, width, weight, read, feat):
        if i % 4 == 0:
            pe.wait_ge(k.fv_ys, b * 2 + (y0 + i // 4 + 1))
        y = ys[i // 4][:, (i % 4) * P:(i % 4 + 1) * P]
        pe.wait_ge(read, n + 1)
        nc.tensor.matmul(k.bank[i % 2][:, 0:width], y, weight, start=True, stop=True)
        pe.wait_ge(k.fv_arg, n + 1)
        nc.tensor.matmul(k.bank[2 + i % 2][:], y, feat, start=True, stop=True).then_inc(k.fv_proj, 1)

    def square(act, n, i):
        act.wait_ge(k.fv_proj, done("fv_proj", n))
        nc.scalar.activation(sq[i % 2], k.bank[i % 2][:, 0:P], ACT.Square, scale=(0.5 / DK) ** 0.5).then_inc(k.fv_sq, 1)

    def exp(act, n, i):
        act.wait_ge(k.fv_arg, done("fv_arg", n))
        nc.scalar.activation(ex[i % 4], ex[i % 4], ACT.Exp).then_inc(k.fv_exp, 1)

    def statistics(dve, n, i):
        s = i % 2
        heads = k.bank[2 + s][:].rearrange("p (h m) -> p h m", m=M)
        dve.wait_ge(k.fv_proj, done("fv_proj", n))
        nc.vector.tensor_reduce(mx[s], heads, AX.X, ALU.max).then_inc(k.fv_max, 1)
        dve.wait_ge(k.fv_sq, done("fv_sq", n))
        nc.vector.tensor_reduce(nm[s], sq[s].rearrange("p (h d) -> p h d", d=DK), AX.X, ALU.add).then_inc(k.fv_max, 1)
        dve.wait_ge(k.fv_max, n * 2 + 2)
        nc.vector.tensor_tensor(mx[s], mx[s], nm[s], ALU.add).then_inc(k.fv_off, 1)
        dve.wait_ge(k.fv_off, n + 1)
        dve.wait_ge(k.fv_used, n + 1)
        nc.vector.tensor_tensor(ex[i % 4].rearrange("p (h m) -> p h m", m=M), heads, mx[s][:, :, None].to_broadcast([P, H, M]),
                                ALU.subtract).then_inc(k.fv_arg, 1)

    with nc.Block() as block:
        @block.tensor
        def _(pe):
            def gather(n, i, b):
                if i % TT == 0:
                    pe.wait_ge(k.fv_kv, b + 1)
                pe.wait_ge(k.fv_va, done("fv_va", n))
                pe.wait_ge(k.fv_exp, n + 1)
                for g in range(G):
                    nc.tensor.matmul(k.bank[4][:, g * 36:(g + 1) * 36], ex[i % 4][:, g * P:(g + 1) * P],
                                     va[i % 4][:, 4 * g:4 * g + 4, :].rearrange("p h n -> p (h n)"),
                                     start=(i % TT == 0 and g == 0), stop=False, skip_group_check=True)
                nc.tensor.matmul(k.bank[4][:, 0:144], k.fv_eps, va[i % 4].rearrange("p h n -> p (h n)"),
                                 start=False, stop=(i % TT == TT - 1), skip_group_check=True).then_inc(k.fv_used, 1)

            def turn(u, at, steps):
                for i in range(steps):
                    if there(at, i):
                        project(pe, u * TT + i, i, u, 0, 2 * P, wT[:, P:3 * P], k.fv_va, k.fv_feat[:, 1, :])
                    if there(at, i - 2):
                        gather(u * TT + (i - 2), i - 2, u)

            run(pe, turn, 2)

        @block.scalar
        def _(act):
            act.preload_act_table_set("exp_and_others")

            def values(n, i):
                act.wait_ge(k.fv_used, n + 1)
                nc.scalar.activation(va[i % 4][:, :, 0:DK], k.bank[i % 2][:, P:2 * P].rearrange("p (h d) -> p h d", d=DK), ACT.Copy).then_inc(k.fv_va, 1)

            def turn(u, at, steps):
                for i in range(steps):
                    if there(at, i):
                        square(act, u * TT + i, i)
                    if there(at, i - 1):
                        exp(act, u * TT + (i - 1), i - 1)
                    if there(at, i):
                        values(u * TT + i, i)

            run(act, turn, 1)

        @block.gpsimd
        def _(pool):
            for s in range(4):
                nc.gpsimd.memset(va[s][:, :, DK:DK + 1], 1.0)

            def turn(u, at, steps):
                for i in range(steps):
                    if i % 4 == 0 and there(at, i):
                        copy_input(pool, u, i // 4, 0)

            run(pool, turn, 0)

        @block.vector
        def _(dve):
            def keep(b, column):
                dve.wait_ge(k.fv_used, b * TT + (TT + PRIMED["fv_used"]))
                nc.vector.tensor_tensor(kv[:, bass.ds(column, 144)].rearrange("p (g h n) -> p g h n", g=G, h=4),
                                        k.bank[4][:, 0:144].rearrange("p (g h n) -> p g h n", g=G, h=4),
                                        k.fv_own[:, None, :, None].to_broadcast([P, G, 4, 9]), ALU.mult).then_inc(k.fv_kv, 1)

            def turn(u, at, steps):
                for i in range(steps):
                    if there(at, i):
                        statistics(dve, u * TT + i, i)
                    if i == 1 and there(at, i - 2):
                        keep(u - 1, u * 144 - 144)

            run(dve, turn, 2)

    n0 = B * TT
    with nc.Block() as block:
        @block.tensor
        def _(pe):
            def turned(n, i):
                pe.wait_ge(k.fv_exp, n + (n0 + 1))
                pe.wait_ge(k.fv_exT, n + 1)
                for g in range(G):
                    op = nc.tensor.transpose(k.bank[4][:, g * P:(g + 1) * P], ex[i % 4][:, g * P:(g + 1) * P], k.ident[:])
                op.then_inc(k.fv_used, 1)

            def sums(n, i, column):
                pe.wait_ge(k.fv_exT, done("fv_exT", n))
                pe.wait_ge(k.fv_o, n + 1)
                for g in range(G):
                    op = nc.tensor.matmul(k.bank[5][:, g * 36:(g + 1) * 36], exT[i % 2][:, g * P:(g + 1) * P],
                                          kv[:, bass.ds(column + g * 36, 36)], start=True, stop=True)
                op.then_inc(k.fv_sums, 1)

            def back(n, i, g):
                pe.wait_ge(k.fv_o, done("fv_o", n))
                if i % 4 == 0:
                    pe.wait_ge(k.fv_oT, g + 1)
                nc.tensor.transpose(k.bank[6][:, (i % 4) * P:(i % 4 + 1) * P], o[i % 2], k.ident[:]).then_inc(k.fv_back, 1)

            def output(g):
                pe.wait_ge(k.fv_oT, done("fv_oT", g))
                pe.wait_ge(k.fv_x, g + 1)
                nc.tensor.matmul(k.bank[7][:], wT[:, 3 * P:4 * P], oT, start=True, stop=True).then_inc(k.fv_out, 1)

            def turn(u, at, steps):
                for i in range(steps):
                    if there(at, i):
                        project(pe, u * TT + (n0 + i), i, u, 2 * B, P, wT[:, 0:P], k.fv_sq, k.fv_feat[:, 0, :])
                    if there(at, i - 2):
                        turned(u * TT + (i - 2), i - 2)
                    if there(at, i - 3):
                        sums(u * TT + (i - 3), i - 3, u * 144 + (i - 3) // TT * 144)
                    if there(at, i - 4):
                        back(u * TT + (i - 4), i - 4, u * 2 + (i - 4) // 4)
                    if i % 4 == 0 and there(at, i - 8):
                        output(u * 2 + (i - 8) // 4)

            run(pe, turn, 5)

        @block.scalar
        def _(act):
            def turned(n, i):
                act.wait_ge(k.fv_used, done("fv_used", n + n0))
                act.wait_ge(k.fv_sums, n + 1)
                nc.scalar.activation(exT[i % 2], k.bank[4][:], ACT.Identity, bias=k.eps6[:, 0:1]).then_inc(k.fv_exT, 1)

            def heads(g):
                act.wait_ge(k.fv_back, g * 4 + 4)
                act.wait_ge(k.fv_out, g + 1)
                nc.scalar.activation(oT, k.bank[6][:], ACT.Copy).then_inc(k.fv_oT, 1)

            def turn(u, at, steps):
                for i in range(steps):
                    if there(at, i):
                        square(act, u * TT + (n0 + i), i)
                    if there(at, i - 1):
                        exp(act, u * TT + (n0 + i - 1), i - 1)
                    if there(at, i - 2):
                        turned(u * TT + (i - 2), i - 2)
                    if i % 4 == 3 and there(at, i - 7):
                        heads(u * 2 + (i - 7) // 4)

            run(act, turn, 4)

        @block.gpsimd
        def _(pool):
            with pool.Fori(0, B) as b:
                for c in range(2):
                    copy_input(pool, b, c, n0)

        @block.vector
        def _(dve):
            def quotient(n, i):
                s = i % 2
                sums = k.bank[5][:, 0:144].rearrange("p (h n) -> p h n", n=9)
                dve.wait_ge(k.fv_sums, done("fv_sums", n))
                nc.vector.tensor_scalar(rd[s], sums[:, :, DK], 1e-6, None, ALU.add).then_inc(k.fv_rd, 1)
                dve.wait_ge(k.fv_rd, n * 2 + 1)
                nc.vector.reciprocal(rd[s], rd[s]).then_inc(k.fv_rd, 1)
                dve.wait_ge(k.fv_rd, n * 2 + 2)
                nc.vector.tensor_tensor(o[s].rearrange("p (h d) -> p h d", d=DK), sums[:, :, 0:DK],
                                        rd[s][:, :, None].to_broadcast([P, H, DK]), ALU.mult).then_inc(k.fv_o, 1)

            def add(g, column):
                at = bass.ds(column, CH)
                dve.wait_ge(k.fv_out, done("fv_out", g))
                nc.vector.scalar_tensor_tensor(k.X[:, at], k.bank[7][:], k.vec("favor_bo"), k.X[:, at], ALU.add, ALU.add).then_inc(k.fv_x, 1)

            def turn(u, at, steps):
                for i in range(steps):
                    if there(at, i):
                        statistics(dve, u * TT + (n0 + i), i)
                    if there(at, i - 3):
                        quotient(u * TT + (i - 3), i - 3)
                    if i % 4 == 1 and there(at, i - 9):
                        add(u * 2 + (i - 9) // 4, u * L + (i - 9) // 4 * CH)

            run(dve, turn, 6)


def stage_favor(nc, k, a, X, Y):
    with ExitStack() as ctx:
        sems = begin_stage(nc, ctx, FAVOR_SEMS)
        (k.fw_in, k.fw_mask, k.fw_turned, k.fw_wide, k.fw_copied, k.fw_prod, k.fv_ys, k.fv_proj, k.fv_sq, k.fv_va,
         k.fv_max, k.fv_off, k.fv_arg, k.fv_exp, k.fv_used, k.fv_kv, k.fv_exT, k.fv_sums, k.fv_o,
         k.fv_rd, k.fv_back, k.fv_oT, k.fv_out, k.fv_x) = sems
        k.ln(X, Y, ahead=lambda block: favor_loads(nc, k, a, block))
        favor_weights(nc, k)
        favor(nc, k, a)
        end_stage(nc, sems)


def segment_loads(nc, k, a, block):
    DK, HALF = 8, P // 2

    @block.sync
    def _(sp):
        for j, w in enumerate((a["L1_attn_a_Wq"], a["L1_attn_a_Wk"], a["L1_attn_a_Wv"])):
            sp.dma_start(k.sg_w[:, j, :], w).then_inc(k.sw_in, 16)
        sp.wait_ge(k.sw_zero, 1)
        for seg in range(2):
            for half in range(2):
                sp.dma_start(k.sg_wo[seg * HALF:(seg + 1) * HALF, seg, half, :],
                             a["L1_attn_a_Wo"][half * HALF:(half + 1) * HALF, :]).then_inc(k.sw_in, 16)

    @block.gpsimd
    def _(pool):
        nc.gpsimd.memset(k.sg_wo, 0.0).then_inc(k.sw_zero, 1)
        nc.gpsimd.tensor_scalar(k.sg_bq, k.vec("bq"), DK ** -0.5, None, ALU.mult)
        nc.gpsimd.memset(k.sg_mask, 1.0).then_inc(k.sg_const, 1)
        pool.wait_ge(k.sg_const, 1)
        nc.gpsimd.affine_select(out=k.sg_mask, in_=k.sg_mask, compare_op=ALU.is_ge, fill=0.0, base=0,
                                pattern=[[-DK, 8], [-HALF, 2]], channel_multiplier=1).then_inc(k.sg_const, 1)
        pool.wait_ge(k.sg_const, 2)
        nc.gpsimd.affine_select(out=k.sg_mask, in_=k.sg_mask, compare_op=ALU.is_ge, fill=0.0, base=DK - 1,
                                pattern=[[DK, 8], [HALF, 2]], channel_multiplier=-1).then_inc(k.sg_const, 1)


def segments(nc, k, a):
    DK, SEG, PAD, UNITS = 8, 64, 2, 4
    NSEG = L // SEG
    STRIDE = NSEG + PAD
    TOTAL = B * STRIDE + PAD + 1
    TURNS = B * NSEG // UNITS
    TB = NSEG // UNITS
    HALF = P // 2
    take = [0]

    def part(n):
        take[0] += n
        return k.arena[:, take[0] - n:take[0]]

    qT = k.N[:, 0:NT]
    pr = [k.Y[:, i * 8 * P:(i + 1) * 8 * P] for i in range(4)]
    kv = part(2 * TOTAL * SEG).rearrange("p (a s n) -> p a s n", a=2, n=SEG)
    qm = [part(8 * P) for _ in range(4)]
    kvc = [part(2 * P).rearrange("p (a n) -> p a n", a=2) for _ in range(4)]
    vt = [part(2 * P).rearrange("p (s n) -> p s n", s=2) for _ in range(2)]
    pT = [part(8 * P) for _ in range(2)]
    mx = [part(40) for _ in range(2)]
    sm = [part(40) for _ in range(4)]
    quarter = part(1)
    o, oT = part(P), part(P)

    def split(v):
        v = v.rearrange("p (h n) -> p h n", h=8)
        return v[:, :, 0:SEG], v[:, :, SEG:2 * SEG].rearrange("p h (g n) -> p h g n", n=16)

    def spread(v):
        return v.rearrange("p (h g) -> p h g", h=8)[:, :, :, None].to_broadcast([P, 8, 4, 16])

    zeros = lambda v: v[:, 0:B * STRIDE, :].rearrange("p (b s) n -> p b (s n)", b=B)[:, :, 0:PAD * SEG]

    def done(s, n):
        return n + (1 + PRIMED.get(s, 0))

    with nc.Block() as block:
        @block.tensor
        def _(pe):
            pe.wait_ge(k.sw_in, 7 * 16)
            with pe.Fori(0, B) as b:
                for i in range(6):
                    pe.wait_ge(k.sg_took, b * 6 + (i + 1))
                    nc.tensor.matmul(k.bank[i][:], k.sg_w[:, i % 3, :], k.Y[:, bass.ds(b * L + i // 3 * CH, CH)],
                                     start=True, stop=True).then_inc(k.sg_proj, 1)

        @block.scalar
        def _(act):
            with act.Fori(0, B) as b:
                for i in range(6):
                    c, j = i // 3, i % 3
                    act.wait_ge(k.sg_proj, b * 6 + (i + 1))
                    if j == 0:
                        dst = qT[:, bass.ds(b * L + c * CH, CH)]
                    else:
                        dst = kv[:, j - 1, bass.ds(b * STRIDE + PAD + c * (CH // SEG), CH // SEG), :].rearrange("p s n -> p (s n)")
                    nc.scalar.activation(dst, k.bank[i][:], ACT.Identity, bias=(k.sg_bq, k.vec("bk"), k.vec("bv"))[j],
                                         scale=(DK ** -0.5, 1.0, 1.0)[j]).then_inc(k.sg_took, 1)

        @block.gpsimd
        def _(pool):
            for j in range(2):
                nc.gpsimd.memset(zeros(kv[:, j]), 0.0)
                nc.gpsimd.memset(kv[:, j, B * STRIDE:, :], 0.0)

        @block.vector
        def _(dve):
            nc.vector.memset(quarter[0:SEG], 1.0)
            nc.vector.memset(quarter[SEG:], 0.25)

    def there(at, i):
        return at is None or 0 <= at + i < TURNS * UNITS

    def run(eng, turn):
        turn(0, 0)
        turn(1, UNITS)
        with eng.Fori(2, TURNS) as u:
            turn(u, None)
        turn(TURNS, TURNS * UNITS)

    STEPS = UNITS + 3

    with nc.Block() as block:
        @block.tensor
        def _(pe):
            def scores(n, i):
                pe.wait_ge(k.sg_fill, n + 1)
                pe.wait_ge(k.sg_kv, n + 1)
                pe.wait_ge(k.sg_arg, n + 1)
                for p in range(8):
                    op = nc.tensor.matmul(k.bank[2 * (i % 2) + p // 4][:, (p % 4) * P:(p % 4 + 1) * P],
                                          qm[i % 4][:, p * P:(p + 1) * P], kvc[i % 4][:, 0, :], start=True, stop=True)
                op.then_inc(k.sg_score, 1)

            def values(n, T, i):
                pe.wait_ge(k.sg_kv, n + 1)
                for s in range(2):
                    op = nc.tensor.transpose(k.bank[6][:, (2 + s) * P:(3 + s) * P], kvc[(i - 1 + s) % 4][:, 1, :], k.ident[:])
                op.then_inc(k.sg_vT, 1)

            def turned(n, i):
                pe.wait_ge(k.sg_mul, n + 1)
                for q in range(2):
                    pe.wait_ge(k.sg_pT, n * 2 + (q + 1))
                    for p in range(4):
                        op = nc.tensor.transpose(k.bank[4 + q][:, p * P:(p + 1) * P], pr[i % 4][:, (4 * q + p) * P:(4 * q + p + 1) * P], k.ident[:])
                    op.then_inc(k.sg_turned, 1)

            def weighed(n, T, i, later):
                s = i % 2
                pe.wait_ge(k.sg_pT, n * 2 + (2 + PRIMED["sg_pT"]))
                if s == 0:
                    pe.wait_ge(k.sg_vt, T + (2 if later else 1))
                    pe.wait_ge(k.sg_o, T + 1)
                for p in range(8):
                    out = k.bank[6][:, s * P:(s + 1) * P].rearrange("p (h n) -> p h n", h=2)[:, :, p * DK:(p + 1) * DK]
                    v = vt[i // 2 % 2][:, s, :].rearrange("p (h n) -> p h n", h=2)[:, :, p * DK:(p + 1) * DK]
                    op = nc.tensor.matmul(out, pT[s][:, p * P:(p + 1) * P], v, start=True, stop=True)
                op.then_inc(k.sg_pv, 1)

            def heads(T):
                pe.wait_ge(k.sg_o, done("sg_o", T))
                pe.wait_ge(k.sg_x, T + PRIMED["sg_x"])
                nc.tensor.transpose(k.bank[7][:, 2 * P:3 * P], o, k.ident[:]).then_inc(k.sg_oturn, 1)

            def output(T):
                pe.wait_ge(k.sg_oT, T + 1)
                for s in range(2):
                    for h in range(2):
                        op = nc.tensor.matmul(k.bank[7][:, 3 * P + s * HALF:3 * P + (s + 1) * HALF], k.sg_wo[:, s, h, :],
                                              oT[:, h * HALF:(h + 1) * HALF], start=(h == 0), stop=(h == 1))
                op.then_inc(k.sg_out, 1)

            def turn(u, at):
                for i in range(UNITS if at != TURNS * UNITS else STEPS):
                    n, T = u * UNITS, u * 2
                    if there(at, i):
                        scores(n + i, i)
                    if there(at, i - 3):
                        turned(n + (i - 3), i - 3)
                    if i % 2 == 1 and there(at, i - 7):
                        output(T + (i // 2 - 3))
                    if there(at, i - 4):
                        weighed(n + (i - 4), T + (i - 4) // 2, i - 4, there(at, i - 1))
                    if i % 2 == 1 and there(at, i):
                        if at is not None and at + i > 1:
                            pe.wait_ge(k.sg_vt, T + i // 2)
                        values(n + i, T + i // 2, i)
                    if i % 2 == 0 and there(at, i - 6):
                        heads(T + (i // 2 - 3))

            run(pe, turn)

        @block.scalar
        def _(act):
            act.preload_act_table_set("exp_and_others")

            def values(T, i):
                act.wait_ge(k.sg_vT, T + (1 + PRIMED["sg_vT"]))
                nc.scalar.activation(vt[i // 2 % 2].rearrange("p s n -> p (s n)"), k.bank[6][:, 2 * P:4 * P], ACT.Identity, scale=quarter).then_inc(k.sg_vt, 1)

            def turned(n, i):
                for q in range(2):
                    act.wait_ge(k.sg_turned, n * 2 + (q + 1))
                    nc.scalar.activation(pT[i % 2][:, q * 4 * P:(q + 1) * 4 * P], k.bank[4 + q][:], ACT.Copy).then_inc(k.sg_pT, 1)

            def exp(n, i):
                act.wait_ge(k.sg_arg, done("sg_arg", n))
                nc.scalar.activation(pr[i % 4], pr[i % 4], ACT.Exp).then_inc(k.sg_exp, 1)

            def heads(T):
                act.wait_ge(k.sg_pv, T * 2 + 2)
                for h in range(2):
                    rows = slice(h * HALF, (h + 1) * HALF)
                    src = k.bank[6][rows, 0:2 * P].rearrange("p (s h n) -> p s h n", s=2, h=2)[:, :, h, :]
                    op = nc.scalar.activation(o[rows].rearrange("p (s n) -> p s n", s=2), src, ACT.Copy)
                op.then_inc(k.sg_o, 1)

            def heads_turned(T):
                act.wait_ge(k.sg_oturn, T + 1)
                nc.scalar.activation(oT, k.bank[7][:, 2 * P:3 * P], ACT.Copy).then_inc(k.sg_oT, 1)

            def gather(b, t, i):
                first = b * STRIDE + t * UNITS + i
                n = (b * TB + t) * UNITS + i
                wait_apart(act, k, k.sg_score, n + 1)
                wait_apart(act, k, k.sg_vT, (b * TB + t) * 2 + (i // 2 + 1))
                nc.scalar.activation(kvc[i][:, :, 0:SEG], kv[:, :, bass.ds(first + PAD, 1), :].rearrange("p a o n -> p a (o n)"), ACT.Copy)
                for j in range(2):
                    around = kv[:, j, bass.ds(first, 6), :].rearrange("p (side three) (n f) -> p side (three n) f", three=3, f=4)
                    op = nc.scalar.activation(kvc[i][:, j, SEG:].rearrange("p (side n) -> p side n", side=2), around[:, :, 0:2 * SEG // 4, 0], ACT.Copy)
                op.then_inc(k.sg_kv, 1)

            def turn(b, t, at):
                n, T = (b * TB + t) * UNITS, (b * TB + t) * 2
                for i in range(UNITS if at != TURNS * UNITS else STEPS + 2):
                    m = i - 2
                    if m % 2 == 0 and there(at, m - 2):
                        values(T + (m // 2 - 1), m - 2)
                    if m % 2 == 0 and there(at, m - 6):
                        heads(T + (m // 2 - 3))
                    if m % 2 == 1 and there(at, m - 7):
                        heads_turned(T + (m // 2 - 3))
                    if there(at, m - 3):
                        turned(n + (m - 3), m - 3)
                    if there(at, m):
                        exp(n + m, m)
                    if there(at, i):
                        gather(b, t, i)

            turn(0, 0, 0)
            turn(0, 1, UNITS)
            with act.Fori(2, TB) as t:
                turn(0, t, None)
            with act.Fori(1, B) as b:
                with act.Fori(0, TB) as t:
                    turn(b, t, None)
            turn(B, 0, TURNS * UNITS)

        @block.vector
        def _(dve):
            def maxima(n, i):
                s = i % 2
                dve.wait_ge(k.sg_score, done("sg_score", n))
                own, others = split(k.pair[s])
                nc.vector.tensor_reduce(mx[s][:, 0:8], own, AX.X, ALU.max)
                nc.vector.tensor_reduce(mx[s][:, 8:40], others, AX.X, ALU.max).then_inc(k.sg_max, 1)

            def shift(n, i):
                s = i % 2
                dve.wait_ge(k.sg_max, n + 1)
                own, others = split(k.pair[s])
                to_own, to_others = split(pr[i % 4])
                nc.vector.tensor_tensor(to_own, own, mx[s][:, 0:8, None].to_broadcast([P, 8, SEG]), ALU.subtract)
                nc.vector.tensor_tensor(to_others, others, spread(mx[s][:, 8:40]), ALU.subtract).then_inc(k.sg_arg, 1)

            def sums(n, i):
                own, others = split(pr[i % 4])
                dve.wait_ge(k.sg_exp, n + 1)
                nc.vector.tensor_reduce(sm[i % 4][:, 0:8], own, AX.X, ALU.add)
                nc.vector.tensor_reduce(sm[i % 4][:, 8:40], others, AX.X, ALU.add).then_inc(k.sg_sum, 1)

            def weight(n, i):
                dve.wait_ge(k.sg_sum, n + 1)
                nc.vector.reciprocal(sm[i % 4], sm[i % 4]).then_inc(k.sg_weight, 1)

            def add(T, column):
                at = bass.ds(column, P)
                dve.wait_ge(k.sg_out, T + 1)
                nc.vector.scalar_tensor_tensor(k.X[:, at], k.bank[7][:, 3 * P:4 * P], k.vec("bo"), k.X[:, at], ALU.add, ALU.add).then_inc(k.sg_x, 1)

            def turn(u, at):
                for i in range(UNITS if at != TURNS * UNITS else STEPS):
                    n, T = u * UNITS, u * 2
                    if i % 2 == 0 and there(at, i - 8):
                        add(T + (i // 2 - 4), u * (2 * P) + (i // 2 - 4) * P)
                    if there(at, i):
                        maxima(n + i, i)
                        shift(n + i, i)
                    if there(at, i - 1):
                        sums(n + (i - 1), i - 1)
                        weight(n + (i - 1), i - 1)

            run(dve, turn)

        @block.gpsimd
        def _(pool):
            def mask(n, i, column):
                wait_apart(pool, k, k.sg_score, n + 1)
                nc.gpsimd.tensor_tensor(qm[i].rearrange("p (h n) -> p h n", h=16), qT[:, None, bass.ds(column, SEG)].to_broadcast([P, 16, SEG]),
                                        k.sg_mask.rearrange("p a b -> p (a b)")[:, :, None].to_broadcast([P, 16, SEG]), ALU.mult).then_inc(k.sg_fill, 1)

            def weigh(n, i):
                own, others = split(pr[i % 4])
                pool.wait_ge(k.sg_weight, n + 1)
                nc.gpsimd.tensor_tensor(own, own, sm[i % 4][:, 0:8, None].to_broadcast([P, 8, SEG]), ALU.mult)
                nc.gpsimd.tensor_tensor(others, others, spread(sm[i % 4][:, 8:40]), ALU.mult).then_inc(k.sg_mul, 1)

            def turn(u, at):
                for i in range(UNITS if at != TURNS * UNITS else STEPS):
                    if there(at, i):
                        mask(u * UNITS + i, i, u * (UNITS * SEG) + i * SEG)
                    if there(at, i - 3):
                        weigh(u * UNITS + (i - 3), i - 3)

            run(pool, turn)


def stage_segments(nc, k, a, X, Y):
    with ExitStack() as ctx:
        sems = begin_stage(nc, ctx, SEGMENT_SEMS)
        (k.sw_in, k.sw_zero, k.sg_took, k.sg_proj, k.sg_fill, k.sg_kv, k.sg_arg, k.sg_score,
         k.sg_x, k.sg_vT, k.sg_mul, k.sg_pT, k.sg_turned, k.sg_vt, k.sg_o, k.sg_pv, k.sg_oturn, k.sg_oT, k.sg_out,
         k.sg_const, k.sg_weight, k.sg_exp, k.sg_max, k.sg_sum) = sems
        k.ln(X, Y, ahead=lambda block: segment_loads(nc, k, a, block))
        segments(nc, k, a)
        end_stage(nc, sems)


SEMS = ["passed", "ident_zero", "ident_one", "consts_set", "vrows_set", "vecs_in", "vecs_turned", "vecs_ready",
        "x_turned", "x_ready", "x_ready_a", "ln_centered", "ln_squared", "ln_var", "ln_logs", "ln_rstd",
        "ln_scaled", "ln_biased", "ln_out", "y_turned", "y_rows", "y_rows_a", "stored", "wA_in", "moe_w_in", 
        "ff_w_in", "ff_const", "ff_spread", "ff_spread16", "ff_hot0", "ff_mix1", "ff_mix2", "ff_mix", "ff_up",
        "ff_u", "ff_h", "ff_hid", "ff_score", "ff_step", "ff_hot", "ff_hotT", "ff_hot16", "ff_spreads", "ff_masked", "ff_out",
        "ff_z", "lr_w_in", "lr_prod", "lr_read", "lr_init", "lr_sc", "lr_den", "lr_ln", "lr_rden", "lr_step", "lr_x", "lr_kv", "lr_out", "lr_added", "tw_in",
        "tw_turned", "tw_zero", "tw_copied", "tw_prod", "tr_ys", "tr_z", "tr_th", "tr_g", "tr_step", "tr_lp", "tr_turned",
        "tr_lpT", "tr_out", "tr_x"]
MOE_SEMS = ["mix_diff", "mix_in", "kvr", "kvr_out", "wkv_w", "wkv_arg", "wkv_exp", "wkv_den", "wkv_ln", "wkv_rden", "wkv_init",
            "wkv_e2bv", "wkv_e2v", "wkv_pp", "wkv_max", "wkv_sub", "wkv_out", "wkv_prod", "wkv_step", "rt_prod", "rt_copied", "rt_turned", "rt_parts", "rt_wT", "rt_back",
            "rt_step", "rt_exps", "rt_const", "rt_sel", "ex_diff", "ex_mix", "ex_r", "ex_v", "ex_tanh", "ex_added", "ex_gate",
            "ex_tw", "ex_weighed", "ex_up", "ex_relu", "ex_sq", "ex_y"]
FAVOR_SEMS = ["fw_in", "fw_mask", "fw_turned", "fw_wide", "fw_copied", "fw_prod", "fv_ys", "fv_proj", "fv_sq", "fv_va", "fv_max",
              "fv_off", "fv_arg", "fv_exp", "fv_used", "fv_kv", "fv_exT", "fv_sums", "fv_o", "fv_rd",
              "fv_back", "fv_oT", "fv_out", "fv_x"]
SEGMENT_SEMS = ["sw_in", "sw_zero", "sg_took", "sg_proj", "sg_fill", "sg_kv", "sg_arg", "sg_score", "sg_x", "sg_vT",
                "sg_mul", "sg_pT", "sg_turned", "sg_vt", "sg_o", "sg_pv", "sg_oturn", "sg_oT", "sg_out", "sg_const", "sg_weight",
                "sg_exp", "sg_max", "sg_sum"]
PRIMED = {"ln_out": 4, "rt_copied": 4, "kvr": 6, "kvr_out": 6,
          "ex_r": 4, "ex_relu": 2, "ex_v": 2, "ex_gate": 2, "ex_added": 2, "ex_tanh": 1, "ex_weighed": 1, "ex_sq": 1,
          "ff_h": 6, "ff_out": 1, "ff_hid": 3, "ff_masked": 6, "ff_z": 2, "lr_read": 6, "lr_added": 2,
          "tr_th": 2, "tr_lpT": 1, "tr_x": 2, "tr_z": 2, "tr_g": 1, "tr_turned": 2, "tr_out": 2,
          "fv_proj": 2, "fv_sq": 2, "fv_arg": 2, "fv_used": 4, "fv_va": 2, "fv_kv": 1, "fv_exT": 1, "fv_o": 1, "fv_sums": 2,
          "fv_oT": 1, "fv_x": 1, "fv_out": 1,
          "sg_x": 3, "sg_arg": 2, "sg_pT": 2, "sg_o": 1, "sg_score": 4, "sg_vT": 2, "sg_took": 6}


def load(nc, k, a):
    row = lambda v: v.rearrange("(o n) -> o n", o=1)
    table = [
        ("ln1_g", row(a["L0_attn_a_ln1_g"])), ("ln1_b", row(a["L0_attn_a_ln1_b"])),
        ("ln2_g", row(a["L0_attn_a_ln2_g"])), ("ln2_b", row(a["L0_attn_a_ln2_b"])),
        ("mu_k", row(a["L0_attn_a_tm_mu_k"])), ("mu_v", row(a["L0_attn_a_tm_mu_v"])), ("mu_r", row(a["L0_attn_a_tm_mu_r"])),
        ("decay", row(a["L0_attn_a_time_decay"])), ("first", row(a["L0_attn_a_time_first"])),
        ("cm_k0", a["L0_attn_a_cm_mu_k"]), ("cm_r0", a["L0_attn_a_cm_mu_r"]),
        ("favor_bo", row(a["L0_attn_b_bo"])), ("mix0", a["L0_ffn_mix_kernel"]),
        ("gamma", row(a["L0_ffn_gamma"])), ("beta", row(a["L0_ffn_beta"])),
        ("bq", row(a["L1_attn_a_bq"])), ("bk", row(a["L1_attn_a_bk"])), ("bv", row(a["L1_attn_a_bv"])), ("bo", row(a["L1_attn_a_bo"])),
        ("br", a["L1_attn_b_b_rkv"].rearrange("(o n) -> o n", n=P)), ("lru_bo", row(a["L1_attn_b_b_o"])),
        ("nu_log", row(a["L1_attn_b_nu_log"])), ("gamma_log", row(a["L1_attn_b_gamma_log"])),
        ("wout_b", row(a["L1_ffn_Wout_b"])), ("b1_0", a["L0_ffn_b1"].rearrange("(o q) m -> o (q m)", q=3)),
        ("bo1", row(a["L0_ffn_bo1"]))]
    xv = k.X[:].rearrange("d (p t) -> d t p", t=NT // P)

    def vectors(eng, first):
        eng.wait_ge(k.vrows_set, 1)
        for name, src in table[first::2]:
            n, width = src.shape
            eng.dma_start(k.vrows[VI[name]:VI[name] + n, 0:width], src).then_inc(k.vecs_in, 16)

    with nc.Block() as block:
        @block.sync
        def _(sp):
            xin = a["L0_attn_a_x"].rearrange("b l d -> (b l) d").rearrange("(p t) d -> p t d", t=NT // P)
            for q in range(4):
                sp.dma_start(k.rows[:, 8 * q:8 * q + 8, :], xin[:, 8 * q:8 * q + 8, :]).then_inc(k.loaded[q], 16)
            vectors(sp, 1)

        @block.gpsimd
        def _(pool):
            nc.gpsimd.memset(k.ident[:], 0.0).then_inc(k.ident_zero, 1)
            pool.wait_ge(k.ident_zero, 1)
            nc.gpsimd.affine_select(out=k.ident[:], in_=k.ident[:], compare_op=ALU.not_equal, fill=1.0, base=0,
                                    pattern=[[-1, P]], channel_multiplier=1).then_inc(k.ident_one, 1)
            nc.gpsimd.memset(k.mean[:], 1.0 / P).then_inc(k.consts_set, 1)
            nc.gpsimd.memset(k.eps[:], EPS_LN).then_inc(k.consts_set, 1)
            nc.gpsimd.memset(k.W2[:, 0, :], 0.0)
            for b in range(B):
                nc.gpsimd.memset(k.N[:, b * PADL:b * PADL + 1], 0.0).then_inc(k.consts_set, 1)
                nc.gpsimd.memset(k.N[:, (b + 1) * PADL - 1:(b + 1) * PADL], 0.0).then_inc(k.consts_set, 1)

        @block.scalar
        def _(act):
            vectors(act, 0)

            for q in range(1, 8, 2):
                act.wait_ge(k.x_turned, q + 1)
                nc.scalar.activation(xv[:, 4 * q:4 * q + 4, :], k.bank[q % 4][:].rearrange("d (t p) -> d t p", t=4), ACT.Copy).then_inc(k.x_ready_a, 1)

        @block.tensor
        def _(pe):
            pe.wait_ge(k.ident_one, 1)
            for q in range(8):
                pe.wait_ge(k.loaded[q // 2], 16)
                if q >= 4:
                    pe.wait_ge((k.x_ready, k.x_ready_a)[q % 2], (q - 4) // 2 + 1)
                for t in range(4):
                    op = nc.tensor.transpose(k.bank[q % 4][:, t * P:(t + 1) * P], k.rows[:, 4 * q + t, :], k.ident[:])
                op.then_inc(k.x_turned, 1)
            pe.wait_ge(k.vecs_in, 16 * len(table))
            nc.tensor.transpose(k.bank[7][:, 0:len(VROWS)], k.vrows[:], k.ident[0:len(VROWS), 0:len(VROWS)]).then_inc(k.vecs_turned, 1)

        @block.vector
        def _(dve):
            for name, semaphore in zip(SEMS, k.sems):
                if name in PRIMED:
                    dve.sem_inc(semaphore, PRIMED[name])
            nc.vector.memset(k.vrows[:], 1.0).then_inc(k.vrows_set, 1)
            dve.wait_ge(k.ident_one, 1)
            dve.wait_ge(k.consts_set, 1)
            nc.vector.tensor_tensor(k.center[:], k.ident[:], k.mean[:], ALU.subtract).then_inc(k.consts_set, 1)
            for q in range(0, 8, 2):
                dve.wait_ge(k.x_turned, q + 1)
                nc.vector.tensor_copy(xv[:, 4 * q:4 * q + 4, :], k.bank[q % 4][:].rearrange("d (t p) -> d t p", t=4)).then_inc(k.x_ready, 1)
            dve.wait_ge(k.vecs_turned, 1)
            nc.vector.tensor_copy(k.vecs[:], k.bank[7][:, 0:len(VROWS)]).then_inc(k.vecs_ready, 1)


def store(nc, k, out):
    with nc.Block() as block:
        @block.tensor
        def _(pe):
            xv = k.X[:].rearrange("d (p t) -> d t p", t=NT // P)
            for q in range(8):
                if q >= 4:
                    pe.wait_ge((k.y_rows, k.y_rows_a)[q % 2], (q - 4) // 2 + 1)
                for t in range(4):
                    op = nc.tensor.transpose(k.bank[q % 4][:, t * P:(t + 1) * P], xv[:, 4 * q + t, :], k.ident[:])
                op.then_inc(k.y_turned, 1)

        @block.vector
        def _(dve):
            for q in range(0, 8, 2):
                dve.wait_ge(k.y_turned, q + 1)
                nc.vector.tensor_copy(k.rows[:, 4 * q:4 * q + 4, :],
                                      k.bank[q % 4][:].rearrange("p (t d) -> p t d", t=4)).then_inc(k.y_rows, 1)

        @block.scalar
        def _(act):
            for q in range(1, 8, 2):
                act.wait_ge(k.y_turned, q + 1)
                nc.scalar.activation(k.rows[:, 4 * q:4 * q + 4, :],
                                     k.bank[q % 4][:].rearrange("p (t d) -> p t d", t=4), ACT.Copy).then_inc(k.y_rows_a, 1)

        @block.sync
        def _(sp):
            yout = out.rearrange("b l d -> (b l) d").rearrange("(p t) d -> p t d", t=NT // P)
            for q in range(4):
                sp.wait_ge(k.y_rows, q + 1)
                sp.wait_ge(k.y_rows_a, q + 1)
                sp.dma_start(yout[:, 8 * q:8 * q + 8, :], k.rows[:, 8 * q:8 * q + 8, :]).then_inc(k.stored, 16)
            sp.wait_ge(k.stored, 4 * 16)


def build(nc, a, out):
    with ExitStack() as ctx:
        def sb(name, shape, dt=F32):
            return ctx.enter_context(nc.sbuf_tensor(name, shape, dt))

        k = Chip()
        k.sems = [ctx.enter_context(nc.semaphore(name)) for name in SEMS]
        (k.passed, k.ident_zero, k.ident_one, k.consts_set, k.vrows_set, k.vecs_in, k.vecs_turned,
         k.vecs_ready, k.x_turned, k.x_ready, k.x_ready_a, k.ln_centered, k.ln_squared, k.ln_var,
         k.ln_logs, k.ln_rstd, k.ln_scaled, k.ln_biased, k.ln_out, k.y_turned, k.y_rows, k.y_rows_a, k.stored, k.wA_in, k.moe_w_in,
         k.ff_w_in, k.ff_const, k.ff_spread, k.ff_spread16, k.ff_hot0, k.ff_mix1,
         k.ff_mix2, k.ff_mix, k.ff_up, k.ff_u, k.ff_h, k.ff_hid, k.ff_score, k.ff_step, k.ff_hot, k.ff_hotT,
         k.ff_hot16, k.ff_spreads, k.ff_masked, k.ff_out, k.ff_z, k.lr_w_in, k.lr_prod, k.lr_read, k.lr_init, k.lr_sc,
         k.lr_den, k.lr_ln, k.lr_rden, k.lr_step, k.lr_x, k.lr_kv, k.lr_out, k.lr_added, k.tw_in, k.tw_turned, k.tw_zero, k.tw_copied, k.tw_prod,
         k.tr_ys, k.tr_z, k.tr_th, k.tr_g, k.tr_step, k.tr_lp, k.tr_turned, k.tr_lpT, k.tr_out, k.tr_x) = k.sems
        k.loaded = [ctx.enter_context(nc.semaphore(f"loaded{q}")) for q in range(4)]
        psum = ctx.enter_context(nc.psum_tensor("psum", [P, 8 * CH], F32))
        k.bank = [psum[:, i * CH:(i + 1) * CH] for i in range(8)]
        k.pair = [psum[:, 2 * i * CH:2 * (i + 1) * CH] for i in range(4)]
        k.ident, k.mean, k.center, k.eps = sb("ident", [P, P]), sb("mean", [P, P]), sb("center", [P, P]), sb("eps", [P, 1])
        k.vrows, k.vecs = sb("vrows", [len(VROWS), P]), sb("vecs", [P, len(VROWS)])
        k.vec = lambda name, n=P: k.vecs[0:n, VI[name]:VI[name] + 1]
        k.X, k.Y, k.N = sb("X", [P, NT]), sb("Y", [P, NT]), sb("N", [P, B * PADL])
        k.ln_sq, k.ln_std = sb("ln_sq", [P, W, CH]), sb("ln_std", [P, W, CH])
        k.ln_scaled_0 = k.ln_biased_0 = 0
        k.arena = sb("arena", [P, 5 * NT])
        k.big = [k.arena[:, i * NT:(i + 1) * NT] for i in range(5)]
        k.rows = k.big[0].rearrange("p (t d) -> p t d", d=P)
        k.ln_calls = k.ff_calls = k.tr_calls = 0
        k.weights = sb("weights", [P, 5120])
        k.eWk = k.weights[:, 0:2048].rearrange("p (e f) -> p e f", e=E)
        k.eWv = k.weights[:, 2048:4096].rearrange("p (e h d) -> p e h d", e=E, h=2)
        k.eWr = k.weights[:, 4096:5120].rearrange("p (e g) -> p e g", e=E)
        k.wA, k.router = sb("wA", [P, 4, P]), sb("router", [P, E])
        k.diff, k.mixed = sb("diff", [P, 2, CH]), sb("mixed", [P, 2, 3, CH])
        k.wdec, k.wneg = sb("wdec", [P, 1]), sb("wneg", [P, 1])
        mixed = k.mixed[:].rearrange("p a j n -> p (a j n)")
        k.pp = [k.ln_sq[:].rearrange("p a n -> p (a n)")[:, 0:L + 1], mixed[:, L + 1:2 * L + 2]]
        k.aa = k.ln_std[:].rearrange("p a n -> p (a n)")[:, 0:L + 1]
        k.bb, k.lam = mixed[:, 0:L + 1], k.diff[:].rearrange("p a n -> p (a n)")
        k.logitT = k.big[3][0:E, :]
        k.twT = k.big[4][:, 0:NT // 2].bitcast(BF16)
        view = lambda j, n=256: k.big[0][:, j * 256:j * 256 + n].rearrange("p (t e) -> p t e", e=E)
        k.rt_logit, k.rt_exp, k.rt_w, k.rt_one, k.rt_cand, k.rt_two = (view(j) for j in range(6))
        k.rt_part = k.big[0][:, 6 * 256:9 * 256].rearrange("p (t e s) -> p t e s", e=E, s=3)
        k.rt_bf = k.big[0][:, 9 * 256:9 * 256 + 128].bitcast(BF16).rearrange("p (t e) -> p t e", e=E)
        k.rt_m, k.rt_c, k.rank = sb("rt_m", [P, NT // P]), sb("rt_c", [P, NT // P]), sb("rank", [P, E])
        k.sel = sb("sel", [P, E, P], BF16)
        ffw = sb("ffw", [P, 6 * P + DM])
        k.W1 = ffw[:, 0:3 * P].rearrange("p (g n) -> p g n", g=3)
        k.W2 = ffw[:, 3 * P:6 * P].rearrange("p (g n) -> p g n", g=3)
        k.Wo1 = ffw[:, 6 * P:6 * P + DM]
        k.Wo2, k.prank = sb("Wo2", [DM + 1, NP]), sb("prank", [P, NP])
        k.spread = k.big[4][:, 0:3 * P].rearrange("p (g n) -> p g n", g=3)
        k.spread16 = sb("spread16", [P, 3, P], BF16)
        k.lruw = k.weights[:, 0:4 * P]
        k.gates = k.weights[:, 4 * P:6 * P]
        k.leaves = k.weights[:, 6 * P:8 * P].rearrange("p (h d) -> p h d", h=2)
        k.lr_nu, k.lr_lam, k.lr_own, k.lr_nbr = (sb(n, [P, 1]) for n in ("lr_nu", "lr_lam", "lr_own", "lr_nbr"))
        k.fv_wT = k.weights[:, 0:4 * P]
        k.fv_feat = k.weights[:, 4 * P:12 * P].rearrange("p (j n) -> p j n", j=2)
        k.fv_eps = k.weights[:, 13 * P:14 * P]
        k.fv_rows = k.arena[:, 0:4 * P].rearrange("p (j d) -> p j d", d=P)
        k.fv_proj_rows = k.arena[:, 4 * P:4 * P + 32].rearrange("p (g d) -> p g d", g=4)
        k.fv_mask = k.arena[:, 5 * P:5 * P + 64].rearrange("p (g h) -> p g h", g=4)
        k.fv_own, k.eps6 = k.weights[:, 12 * P:12 * P + 4], sb("eps6", [P, 1])
        k.sg_w = k.weights[:, 0:4 * P].rearrange("p (j n) -> p j n", j=4)
        k.sg_wo = k.weights[:, 4 * P:8 * P].rearrange("p (s h n) -> p s h n", s=2, h=2)
        k.sg_bq = k.weights[:, 8 * P:8 * P + 1]
        k.sg_mask = k.weights[:, 9 * P:9 * P + 16].rearrange("p (s h) -> p s h", s=8)

        def ln(src, dst, **kw):
            layernorm(nc, k, k.ln_calls, src, dst, **kw)
            k.ln_calls += 1

        k.ln = ln
        X, Y = (lambda it, c: plain(k.X, it, c)), (lambda it, c: plain(k.Y, it, c))
        load(nc, k, a)
        for st in STAGES:
            STAGE[st](nc, k, a, X, Y)
        store(nc, k, out)


STAGE = {"A": stage_rwkv, "B": stage_ffn, "C": stage_favor, "D": stage_ffn, "E": stage_segments, "F": stage_tree, "G": stage_lru, "H": stage_tree}
_OUTS = [((4, 1024, 128), 'float32')]


def kernel(**inputs):
    import numpy as _np
    import concourse.bacc as _bacc
    from concourse import mybir as _mybir
    from concourse.bass_utils import run_bass_kernel_spmd as _run

    nc = _bacc.Bacc("TRN2", target_bir_lowering=False, num_devices=1)
    arrays, args = {}, {}
    for name in inputs:
        a = _np.ascontiguousarray(inputs[name])
        arrays[f"in_{name}_dram"] = a
        args[name] = nc.dram_tensor(f"in_{name}_dram", a.shape, _mybir.dt.from_np(a.dtype), kind="ExternalInput").ap()
    outs = []
    for i, (shape, dtype) in enumerate(_OUTS):
        dt = _mybir.dt.from_np(_np.dtype(dtype))
        outs.append(nc.dram_tensor(f"out_{i}_dram", shape, dt, kind="ExternalOutput").ap())
    build(nc, args, outs[0])
    r = _run(nc, [arrays], core_ids=[0])
    return r.results[0]["out_0_dram"]
```
